# Optimizing a Trainium2 kernel written in Bass

```python
import numpy as np
import jax
import jax.numpy as jnp

def _softmax(x, axis=-1):
    return jax.nn.softmax(x, axis=axis)

def _gelu(x):
    return jax.nn.gelu(x, approximate=True)

def _silu(x):
    return jax.nn.silu(x)

def _sigmoid(x):
    return jax.nn.sigmoid(x)

def _layernorm(x, axis=-1, eps=1e-05):
    m = jnp.mean(x, axis=axis, keepdims=True)
    v = jnp.var(x, axis=axis, keepdims=True)
    return (x - m) / jnp.sqrt(v + eps)

def _scatter_add(tgt, idx, src, axis=0):
    return tgt.at[idx].add(src)

def _segment_sum(src, seg, n):
    return jax.ops.segment_sum(src, seg, n)
kernel_name = 'mk_adaln_ffn_d2_seqx_r4_cbe976'

def setup_inputs(seed: int=0):
    np.random.seed(seed)
    _w = jnp.asarray

    def _rec_inputs():
        import jax
        import jax.numpy as jnp
        _rk = jax.random.key(seed)
        x = -0.0003929 + 0.9999 * jax.random.normal(jax.random.fold_in(_rk, 1), (8, 256, 512), jnp.float32)
        _lenS = 256 - jax.random.randint(jax.random.fold_in(_rk, 7), (8,), 0, max(1, 256 // 4) + 1, jnp.int32)
        _lenS2 = 256 - jax.random.randint(jax.random.fold_in(_rk, 8), (8,), 0, max(1, 256 // 4) + 1, jnp.int32)
        cond_2048 = 0.00782532 + 1.00527 * jax.random.normal(jax.random.fold_in(_rk, 11), (8, 512), jnp.float32)
        return (x, cond_2048)
    x, cond_2048 = _rec_inputs()

    def _L0_cond_setup():
        import jax, jax.numpy as jnp
        import numpy as np
        HEADS = 16
        EPS = 1e-06

        def _rms_norm(x, g):
            xf = x.astype(jnp.float32)
            y = xf * jax.lax.rsqrt(jnp.mean(xf * xf, axis=-1, keepdims=True) + EPS)
            return y.astype(x.dtype) * g
        key = jax.random.key(seed)
        ks = jax.random.split(key, 6)
        b, n, dim, emb_dim = (4, 512, 512, 512)
        d_head = dim // HEADS
        return {'x': jax.random.normal(ks[0], (b, n, dim), jnp.float32), 'emb': jax.random.normal(ks[1], (b, 1, emb_dim), jnp.float32), 'W_emb': jax.random.normal(ks[2], (emb_dim, 2 * dim), jnp.float32) * emb_dim ** (-0.5), 'b_emb': jnp.zeros((2 * dim,), jnp.float32), 'g_norm': jnp.ones((dim,), jnp.float32), 'W_qkv': jax.random.normal(ks[3], (dim, 3 * dim), jnp.float32) * dim ** (-0.5), 'g_q': jnp.ones((d_head,), jnp.float32), 'g_k': jnp.ones((d_head,), jnp.float32), 'W_out': jax.random.normal(ks[4], (dim, dim), jnp.float32) * dim ** (-0.5)}
    _L0_cond_all = _L0_cond_setup()
    _L0_cond_in = {k: v for k, v in _L0_cond_all.items() if k in ('W_emb', 'b_emb', 'g_norm', 'W_qkv', 'g_q', 'g_k', 'W_out')}
    del _L0_cond_all

    def _L0_ffn_setup():
        import jax, jax.numpy as jnp
        import numpy as np
        LHS_BITS = 8
        RHS_BITS = 8

        def fake_quant(x, bits, axes):
            qmax = 2.0 ** (bits - 1) - 1.0
            amax = jnp.max(jnp.abs(x), axis=axes, keepdims=True)
            scale = jnp.where(amax > 0, amax / qmax, jnp.ones_like(amax))
            q = jnp.clip(jnp.round(x / scale), -qmax, qmax) * scale
            return x + jax.lax.stop_gradient(q - x)
        key = jax.random.key(seed)
        k1, k2, k3 = jax.random.split(key, 3)
        B, S, D, F = (4, 512, 512, 512)
        x = jax.random.normal(k1, (B, S, D), dtype=jnp.float32)
        kernel = jax.random.normal(k2, (D, F), dtype=jnp.float32) * (1.0 / np.sqrt(D))
        bias = jax.random.normal(k3, (F,), dtype=jnp.float32) * 0.02
        return {'x': x, 'kernel': kernel, 'bias': bias}
    _L0_ffn_all = _L0_ffn_setup()
    _L0_ffn_in = {k: v for k, v in _L0_ffn_all.items() if k in ('kernel', 'bias')}
    del _L0_ffn_all

    def _L1_cond_setup():
        import jax, jax.numpy as jnp
        import numpy as np
        B, T, D = (16, 128, 512)
        key = jax.random.key(seed)
        k0, k1, k2, k3 = jax.random.split(key, 4)
        scale = 1.0 / np.sqrt(D)
        return {'initial_state': jax.random.normal(k0, (B, D), jnp.float32), 'inputs': jax.random.normal(k1, (B, T, D), jnp.float32), 'W_ih': jax.random.normal(k2, (D, 3 * D), jnp.float32) * scale, 'W_hh': jax.random.normal(k3, (D, 3 * D), jnp.float32) * scale, 'b_ih': jnp.zeros((3 * D,), jnp.float32), 'b_hh': jnp.zeros((3 * D,), jnp.float32)}
    _L1_cond_all = _L1_cond_setup()
    _L1_cond_in = {k: v for k, v in _L1_cond_all.items() if k in ('W_ih', 'W_hh', 'b_ih', 'b_hh')}
    del _L1_cond_all

    def _L1_ffn_setup():
        import jax, jax.numpy as jnp
        import numpy as np
        from jax import lax
        E = 64
        H = 512
        I = 176
        G = 8
        TOPK_GROUP = 4
        K = 8
        B, S = (2, 512)
        N = B * S
        CAP = 2 * N * K // E
        SCALE = 2.5

        def _route(x, router_weight, e_bias):
            logits = x.astype(jnp.float32) @ router_weight.astype(jnp.float32).T
            scores = jax.nn.sigmoid(logits)
            sc = scores + e_bias
            n = x.shape[0]
            group_scores = lax.top_k(sc.reshape(n, G, E // G), 2)[0].sum(-1)
            grp_idx = lax.top_k(group_scores, TOPK_GROUP)[1]
            group_mask = jnp.zeros((n, G), jnp.float32).at[jnp.arange(n)[:, None], grp_idx].set(1.0)
            score_mask = jnp.repeat(group_mask, E // G, axis=1)
            masked = jnp.where(score_mask > 0, sc, 0.0)
            topk_idx = lax.top_k(masked, K)[1]
            topk_w = jnp.take_along_axis(scores, topk_idx, axis=1)
            topk_w = topk_w / (topk_w.sum(-1, keepdims=True) + 1e-20)
            return (topk_idx, topk_w * SCALE)

        def _moe_experts(x, topk_idx, topk_w, w_gate, w_up, w_down):
            n = x.shape[0]
            flat_e = topk_idx.reshape(-1)
            rows = jnp.repeat(jnp.arange(n), K)
            oh = jax.nn.one_hot(flat_e, E, dtype=jnp.int32)
            pos = jnp.cumsum(oh, axis=0) - oh
            pos = jnp.take_along_axis(pos, flat_e[:, None], axis=1)[:, 0]
            valid = (pos < CAP).astype(x.dtype)
            p = jnp.minimum(pos, CAP - 1)
            buf = jnp.zeros((E, CAP, H), x.dtype).at[flat_e, p].add(x[rows] * valid[:, None])
            g = jnp.einsum('ech,ehi->eci', buf, w_gate)
            u = jnp.einsum('ech,ehi->eci', buf, w_up)
            y = jnp.einsum('eci,eih->ech', jax.nn.silu(g) * u, w_down)
            y_tok = y[flat_e, p] * (topk_w.reshape(-1) * valid)[:, None]
            return jnp.zeros((n, H), x.dtype).at[rows].add(y_tok)

        def _shared_mlp(x, sh_gate, sh_up, sh_down):
            return jax.nn.silu(x @ sh_gate) * (x @ sh_up) @ sh_down
        key = jax.random.key(seed)
        ks = jax.random.split(key, 9)
        f32 = jnp.float32
        return {'hidden_states': jax.random.normal(ks[0], (B, S, H), f32), 'router_weight': jax.random.normal(ks[1], (E, H), f32) * (2.0 / H) ** 0.5, 'e_bias': jnp.zeros((E,), f32), 'w_gate': jax.random.normal(ks[2], (E, H, I), f32) * (1.0 / H) ** 0.5, 'w_up': jax.random.normal(ks[3], (E, H, I), f32) * (1.0 / H) ** 0.5, 'w_down': jax.random.normal(ks[4], (E, I, H), f32) * (1.0 / I) ** 0.5, 'sh_gate': jax.random.normal(ks[5], (H, I), f32) * (1.0 / H) ** 0.5, 'sh_up': jax.random.normal(ks[6], (H, I), f32) * (1.0 / H) ** 0.5, 'sh_down': jax.random.normal(ks[7], (I, H), f32) * (1.0 / I) ** 0.5}
    _L1_ffn_all = _L1_ffn_setup()
    _L1_ffn_in = {k: v for k, v in _L1_ffn_all.items() if k in ('router_weight', 'e_bias', 'w_gate', 'w_up', 'w_down', 'sh_gate', 'sh_up', 'sh_down')}
    del _L1_ffn_all
    return {'x': x, 'cond_2048': cond_2048, 'L0_cond_W_emb': _L0_cond_in['W_emb'], 'L0_cond_b_emb': _L0_cond_in['b_emb'], 'L0_cond_g_norm': _L0_cond_in['g_norm'], 'L0_cond_W_qkv': _L0_cond_in['W_qkv'], 'L0_cond_g_q': _L0_cond_in['g_q'], 'L0_cond_g_k': _L0_cond_in['g_k'], 'L0_cond_W_out': _L0_cond_in['W_out'], 'L0_ffn_kernel': _L0_ffn_in['kernel'], 'L0_ffn_bias': _L0_ffn_in['bias'], 'L1_cond_W_ih': _L1_cond_in['W_ih'], 'L1_cond_W_hh': _L1_cond_in['W_hh'], 'L1_cond_b_ih': _L1_cond_in['b_ih'], 'L1_cond_b_hh': _L1_cond_in['b_hh'], 'L1_ffn_router_weight': _L1_ffn_in['router_weight'], 'L1_ffn_e_bias': _L1_ffn_in['e_bias'], 'L1_ffn_w_gate': _L1_ffn_in['w_gate'], 'L1_ffn_w_up': _L1_ffn_in['w_up'], 'L1_ffn_w_down': _L1_ffn_in['w_down'], 'L1_ffn_sh_gate': _L1_ffn_in['sh_gate'], 'L1_ffn_sh_up': _L1_ffn_in['sh_up'], 'L1_ffn_sh_down': _L1_ffn_in['sh_down']}

def reference(x, cond_2048, L0_cond_W_emb, L0_cond_b_emb, L0_cond_g_norm, L0_cond_W_qkv, L0_cond_g_q, L0_cond_g_k, L0_cond_W_out, L0_ffn_kernel, L0_ffn_bias, L1_cond_W_ih, L1_cond_W_hh, L1_cond_b_ih, L1_cond_b_hh, L1_ffn_router_weight, L1_ffn_e_bias, L1_ffn_w_gate, L1_ffn_w_up, L1_ffn_w_down, L1_ffn_sh_gate, L1_ffn_sh_up, L1_ffn_sh_down):
    import jax
    import jax.numpy as jnp

    def _L0_cond_ref(x, emb, W_emb, b_emb, g_norm, W_qkv, g_q, g_k, W_out):
        import jax, jax.numpy as jnp
        import numpy as np
        HEADS = 16
        EPS = 1e-06

        def _rms_norm(x, g):
            xf = x.astype(jnp.float32)
            y = xf * jax.lax.rsqrt(jnp.mean(xf * xf, axis=-1, keepdims=True) + EPS)
            return y.astype(x.dtype) * g
        b, n, dim = x.shape
        h = HEADS
        d = dim // h
        scale_shift = emb @ W_emb + b_emb
        scale, shift = jnp.split(scale_shift, 2, axis=-1)
        xn = _rms_norm(x, g_norm) * (1.0 + scale) + shift
        qkv = xn @ W_qkv
        qkv = qkv.reshape(b, n, 3, h, d)
        q, k, v = jnp.moveaxis(qkv, 2, 0)
        q = jnp.swapaxes(q, 1, 2)
        k = jnp.swapaxes(k, 1, 2)
        v = jnp.swapaxes(v, 1, 2)
        q = _rms_norm(q, g_q)
        k = _rms_norm(k, g_k)
        logits = jnp.einsum('bhqd,bhkd->bhqk', q, k) * d ** (-0.5)
        attn = jax.nn.softmax(logits, axis=-1)
        o = jnp.einsum('bhqk,bhkd->bhqd', attn, v)
        o = jnp.swapaxes(o, 1, 2).reshape(b, n, dim)
        return o + o @ W_out

    def _L0_ffn_ref(x, kernel, bias):
        import jax, jax.numpy as jnp
        import numpy as np
        LHS_BITS = 8
        RHS_BITS = 8

        def fake_quant(x, bits, axes):
            qmax = 2.0 ** (bits - 1) - 1.0
            amax = jnp.max(jnp.abs(x), axis=axes, keepdims=True)
            scale = jnp.where(amax > 0, amax / qmax, jnp.ones_like(amax))
            q = jnp.clip(jnp.round(x / scale), -qmax, qmax) * scale
            return x + jax.lax.stop_gradient(q - x)
        bq = fake_quant(bias, RHS_BITS, -1)
        xq = fake_quant(x, LHS_BITS, -1)
        kq = fake_quant(kernel, RHS_BITS, 0)
        y = jnp.einsum('bsd,df->bsf', xq, kq)
        y = y + bq[None, None, :]
        y = jax.nn.relu(y)
        return fake_quant(y, LHS_BITS, -1)

    def _L1_cond_ref(initial_state, inputs, W_ih, W_hh, b_ih, b_hh):
        import jax, jax.numpy as jnp
        import numpy as np
        B, T, D = (16, 128, 512)
        "ScanOverTime(GRU cell): sequential per-timestep module call with\n            dict-state passing; merge_dict_trees stacks the per-step\n            'state_predicted' tensors along axis=1 -> [B, T, D]."

        def cell(h, x):
            gi = x @ W_ih + b_ih
            gh = h @ W_hh + b_hh
            i_r, i_z, i_n = jnp.split(gi, 3, axis=-1)
            h_r, h_z, h_n = jnp.split(gh, 3, axis=-1)
            r = jax.nn.sigmoid(i_r + h_r)
            z = jax.nn.sigmoid(i_z + h_z)
            n = jnp.tanh(i_n + r * h_n)
            h_new = (1.0 - z) * n + z * h
            return (h_new, h_new)
        xs = jnp.swapaxes(inputs, 0, 1)
        _, hs = jax.lax.scan(cell, initial_state, xs)
        return jnp.swapaxes(hs, 0, 1)

    def _L1_ffn_ref(hidden_states, router_weight, e_bias, w_gate, w_up, w_down, sh_gate, sh_up, sh_down):
        import jax, jax.numpy as jnp
        import numpy as np
        from jax import lax
        E = 64
        H = 512
        I = 176
        G = 8
        TOPK_GROUP = 4
        K = 8
        B, S = (2, 512)
        N = B * S
        CAP = 2 * N * K // E
        SCALE = 2.5

        def _route(x, router_weight, e_bias):
            logits = x.astype(jnp.float32) @ router_weight.astype(jnp.float32).T
            scores = jax.nn.sigmoid(logits)
            sc = scores + e_bias
            n = x.shape[0]
            group_scores = lax.top_k(sc.reshape(n, G, E // G), 2)[0].sum(-1)
            grp_idx = lax.top_k(group_scores, TOPK_GROUP)[1]
            group_mask = jnp.zeros((n, G), jnp.float32).at[jnp.arange(n)[:, None], grp_idx].set(1.0)
            score_mask = jnp.repeat(group_mask, E // G, axis=1)
            masked = jnp.where(score_mask > 0, sc, 0.0)
            topk_idx = lax.top_k(masked, K)[1]
            topk_w = jnp.take_along_axis(scores, topk_idx, axis=1)
            topk_w = topk_w / (topk_w.sum(-1, keepdims=True) + 1e-20)
            return (topk_idx, topk_w * SCALE)

        def _moe_experts(x, topk_idx, topk_w, w_gate, w_up, w_down):
            n = x.shape[0]
            flat_e = topk_idx.reshape(-1)
            rows = jnp.repeat(jnp.arange(n), K)
            oh = jax.nn.one_hot(flat_e, E, dtype=jnp.int32)
            pos = jnp.cumsum(oh, axis=0) - oh
            pos = jnp.take_along_axis(pos, flat_e[:, None], axis=1)[:, 0]
            valid = (pos < CAP).astype(x.dtype)
            p = jnp.minimum(pos, CAP - 1)
            buf = jnp.zeros((E, CAP, H), x.dtype).at[flat_e, p].add(x[rows] * valid[:, None])
            g = jnp.einsum('ech,ehi->eci', buf, w_gate)
            u = jnp.einsum('ech,ehi->eci', buf, w_up)
            y = jnp.einsum('eci,eih->ech', jax.nn.silu(g) * u, w_down)
            y_tok = y[flat_e, p] * (topk_w.reshape(-1) * valid)[:, None]
            return jnp.zeros((n, H), x.dtype).at[rows].add(y_tok)

        def _shared_mlp(x, sh_gate, sh_up, sh_down):
            return jax.nn.silu(x @ sh_gate) * (x @ sh_up) @ sh_down
        orig_shape = hidden_states.shape
        x = hidden_states.reshape(-1, H)
        topk_idx, topk_w = _route(x, router_weight, e_bias)
        moe_out = _moe_experts(x, topk_idx, topk_w.astype(x.dtype), w_gate, w_up, w_down)
        out = moe_out + _shared_mlp(x, sh_gate, sh_up, sh_down)
        return out.reshape(orig_shape)
    x = x + _L0_ffn_ref(_L0_cond_ref(x, cond_2048[:, None, :], L0_cond_W_emb, L0_cond_b_emb, L0_cond_g_norm, L0_cond_W_qkv, L0_cond_g_q, L0_cond_g_k, L0_cond_W_out), L0_ffn_kernel, L0_ffn_bias)
    x = x + _L1_ffn_ref(_L1_cond_ref(cond_2048, x, L1_cond_W_ih, L1_cond_W_hh, L1_cond_b_ih, L1_cond_b_hh), L1_ffn_router_weight, L1_ffn_e_bias, L1_ffn_w_gate, L1_ffn_w_up, L1_ffn_w_down, L1_ffn_sh_gate, L1_ffn_sh_up, L1_ffn_sh_down)
    return x

_drawn_inputs = setup_inputs


def setup_inputs(seed=0):
    import zlib

    import numpy as np

    out = dict(_drawn_inputs(seed))
    spreads = {'L0_cond_b_emb': (0.0, 0.1),
     'L0_cond_g_norm': (1.0, 0.2),
     'L0_cond_g_q': (1.0, 0.576),
     'L0_cond_g_k': (1.0, 0.2),
     'L1_cond_b_ih': (0.0, 0.1),
     'L1_cond_b_hh': (0.0, 0.1),
     'L1_ffn_e_bias': (0.0, 0.1)}
    factors = {'L0_ffn_bias': 3.216}
    for name, (base, spread) in spreads.items():
        noise = np.random.default_rng([zlib.crc32(name.encode()), seed]).standard_normal(out[name].shape)
        drawn = base * np.exp(spread * noise) if base else spread * noise
        out[name] = jnp.asarray(drawn.astype(out[name].dtype))
    for name, factor in factors.items():
        out[name] = (out[name] * factor).astype(out[name].dtype)
    return out
```

```python
from contextlib import ExitStack

import concourse.bass as bass
from concourse import mybir

P = 128
F32 = mybir.dt.float32
BF16 = mybir.dt.bfloat16
I32 = mybir.dt.int32
U32 = mybir.dt.uint32
ALU = mybir.AluOpType
ACT = mybir.ActivationFunctionType
AX = mybir.AxisListType

B, T, D = 8, 256, 512
N = B * T
KC = D // P
NT = N // P
TB = T // P
HEADS = 16
DH = D // HEADS
HPC = P // DH
NG = 3
TC = 8
GB = KC * B
E, I = 64, 176
IH = I // 2
NGRP, GSZ, TOPG, TOPK = 8, 8, 4, 8
CAP = 256
SLOTS = E * CAP
NU = SLOTS // P
ROUTE_SCALE = 2.5
QMAX = 127.0
MAGIC = 12582912.0
RMS_EPS = 1e-6
TAKEN = -1e30
KEY0 = 32768.0


class Chain:

    def __init__(self, eng, sem, base=0):
        self.eng, self.sem, self.base, self.n = eng, sem, base, 0

    def __call__(self, ins):
        self.n += 1
        ins.then_inc(self.sem, 1)
        self.eng.wait_ge(self.sem, self.base + self.n)


PRIME = 1
PRIME_DMA = 16


class Kernel:
    def __init__(self, nc, io, out):
        self.nc, self.io, self.out = nc, io, out
        self.hs_rows = nc.dram_tensor("hs_rows", [N + CAP, D], F32, kind="Internal").ap()
        self.acc_rows = nc.dram_tensor("acc_rows", [N + CAP, D], F32, kind="Internal").ap()
        self.table = nc.dram_tensor("slot_table", [SLOTS + TOPK * P, 2], I32, kind="Internal").ap()

    def build(self):
        with ExitStack() as ctx:
            nc = self.nc
            self.x = ctx.enter_context(nc.sbuf_tensor("x", [P, NT, D], F32))
            self.ident = ctx.enter_context(nc.sbuf_tensor("ident", [P, P], F32))
            self.ones = ctx.enter_context(nc.sbuf_tensor("ones", [P, P], F32))
            self.bank = [ctx.enter_context(nc.psum_tensor(f"bank{i}", [P, 512], F32)) for i in range(8)]
            self.xT = ctx.enter_context(nc.sbuf_tensor("xT", [P, KC, N], F32))
            with ExitStack() as c0:
                self.layer0(c0)
            with ExitStack() as c1:
                self.gru(c1)
            with ExitStack() as c2:
                self.router(c2)
            with ExitStack() as c3:
                self.experts(c3)

    def layer0(self, ctx):
        nc, io, x, ident, ones, bank, xT = self.nc, self.io, self.x, self.ident, self.ones, self.bank, self.xT

        def sb(name, shape, dt=F32):
            return ctx.enter_context(nc.sbuf_tensor(name, shape, dt))

        def sem(name):
            return ctx.enter_context(nc.semaphore("a_" + name))

        identb = sb("identb", [P, P], BF16)
        headmean = sb("headmean", [P, P])
        gcol = sb("gcol", [P, 2])
        wqkv = sb("wqkv", [P, KC, 3 * D])
        wout = sb("wout", [P, KC, D])
        biasrow = sb("biasrow", [P, D])
        modG = sb("modG", [P, KC, B])
        modS = sb("modS", [P, KC, B])
        kq = sb("kq", [P, KC, D], BF16)
        krow = sb("krow", [P, D])
        rin = sb("rin", [P, NT])
        epsc = sb("epsc", [P, 1])

        setup = ExitStack()

        def tmp_sb(name, shape, dt=F32):
            return setup.enter_context(nc.sbuf_tensor(name, shape, dt))

        wemb = tmp_sb("wemb", [P, KC, 2 * D])
        condT = tmp_sb("condT", [P, KC, B])
        bembc = tmp_sb("bembc", [P, 2 * KC])
        gnc = tmp_sb("gnc", [P, KC])
        kern = tmp_sb("kern", [P, KC, D])
        kernT = tmp_sb("kernT", [P, KC, D])
        krinv = tmp_sb("krinv", [P, D])
        kcol = tmp_sb("kcol", [P, KC])
        kz = tmp_sb("kz", [P, KC])
        diag = tmp_sb("diag", [P, P])
        tmp = tmp_sb("tmp", [P, D])
        bqs = tmp_sb("bqs", [P, 3])
        ssq = tmp_sb("ssq", [P, NT])
        rms = tmp_sb("rms", [P, NT])
        sqd = tmp_sb("sqd", [P, D])
        sqa = tmp_sb("sqa", [P, D])

        ld_x, ld_w, ld_k = [sem(f"ld_x{i}") for i in range(NT // 4)], sem("ld_w"), sem("ld_k")
        c_id, c_ready = sem("c_id"), sem("c_ready")
        emb_done, mod_chain, ss_act, ss_done, rms_done = (
            sem("emb_done"), sem("mod_chain"), sem("ss_act"), sem("ss_done"), sem("rms_done"))
        krow_done, diag_ready = sem("krow_done"), sem("diag_ready")
        with nc.Block() as block:
            @block.sync
            def _(sp):
                sp.dma_start(condT[:], io["condT"].rearrange("(k p) b -> p k b", p=P)).then_inc(ld_w, 16)
                sp.dma_start(wemb[:], io["W_emb"].rearrange("(k p) n -> p k n", p=P)).then_inc(ld_w, 16)
                for t in range(0, NT, 4):
                    sp.dma_start(x[:, t:t + 4, :], io["x"][t * P:(t + 4) * P, :].rearrange("(t p) d -> p t d", p=P)
                                 ).then_inc(ld_x[t // 4], 16)
                sp.dma_start(wqkv[:], io["W_qkv"].rearrange("(k p) n -> p k n", p=P)).then_inc(ld_k, 16)

            @block.scalar
            def _(act):
                act.dma_start(bembc[:], io["b_emb"]).then_inc(ld_w, 16)
                act.dma_start(gnc[:], io["g_norm"]).then_inc(ld_w, 16)
                for r in range(HPC):
                    act.dma_start(gcol[DH * r:DH * r + DH, 0:1], io["g_q"]).then_inc(ld_w, 16)
                    act.dma_start(gcol[DH * r:DH * r + DH, 1:2], io["g_k"]).then_inc(ld_w, 16)
                act.dma_start(kern[:], io["kernel"].rearrange("(k p) n -> p k n", p=P)).then_inc(ld_k, 16)
                act.dma_start(kernT[:], io["kernelT"].rearrange("(k p) n -> p k n", p=P)).then_inc(ld_k, 16)
                act.dma_start(wout[:], io["W_out"].rearrange("(k p) n -> p k n", p=P)).then_inc(ld_k, 16)
                act.dma_start(biasrow[:], io["ffn_bias"].partition_broadcast(P)).then_inc(ld_k, 16)
                for t in range(1, NT, 2):
                    act.wait_ge(ld_x[t // 4], 16)
                    if t > 1:
                        act.wait_ge(ss_act, t // 2)
                    nc.scalar.activation(sqa[:], x[:, t, :], ACT.Square, accum_out=ssq[:, t:t + 1]
                                         ).then_inc(ss_act, 1)
                act.wait_ge(ss_act, NT // 2)
                act.wait_ge(ss_done, NT // 2)
                act.wait_ge(c_ready, 1)
                nc.scalar.activation(rms[:], ssq[:], ACT.Sqrt, bias=epsc[:], scale=1.0 / D).then_inc(rms_done, 1)

            @block.gpsimd
            def _(pool):
                nc.gpsimd.memset(ident[:], 0.0).then_inc(c_id, 1)
                nc.gpsimd.memset(identb[:], 0.0).then_inc(c_id, 1)
                pool.wait_ge(c_id, 2)
                for m in (ident, identb):
                    nc.gpsimd.affine_select(out=m[:], in_=m[:], compare_op=ALU.not_equal, fill=1.0, base=0,
                                            pattern=[[-1, P]], channel_multiplier=1)
                nc.gpsimd.memset(ones[:], 1.0)
                nc.gpsimd.memset(epsc[:], RMS_EPS).then_inc(c_ready, 1)

            @block.vector
            def _(dve):
                step = Chain(dve, mod_chain)
                step(nc.vector.memset(headmean[:], 0.0))
                for r in range(HPC):
                    nc.vector.memset(headmean[DH * r:DH * r + DH, DH * r:DH * r + DH], 1.0 / DH)
                dve.wait_ge(ld_w, 16 * (4 + 2 * HPC))
                dve.wait_ge(emb_done, 1)
                emb = bank[0][:, 0:2 * KC * B].rearrange("p (m b) -> p m b", b=B)
                for k in range(KC):
                    nc.vector.tensor_scalar(modG[:, k, :], emb[:, k, :], bembc[:, k:k + 1], 1.0, ALU.add, ALU.add)
                    last = nc.vector.tensor_scalar(modS[:, k, :], emb[:, KC + k, :], bembc[:, KC + k:KC + k + 1],
                                                   None, ALU.add)
                step(last)
                for k in range(KC):
                    nc.vector.tensor_scalar(modG[:, k, :], modG[:, k, :], gnc[:, k:k + 1], None, ALU.mult)
                nc.vector.tensor_scalar(gcol[:, 0:1], gcol[:, 0:1], float(DH) ** -0.5, None, ALU.mult)
                for t in range(0, NT, 2):
                    dve.wait_ge(ld_x[t // 4], 16)
                    if t:
                        dve.wait_ge(ss_done, t // 2)
                    nc.vector.tensor_tensor_reduce(sqd[:], x[:, t, :], x[:, t, :], 1.0, 0.0, ALU.mult, ALU.add,
                                                   ssq[:, t:t + 1]).then_inc(ss_done, 1)
                dve.wait_ge(ld_k, 16 * 5)
                step(nc.vector.tensor_reduce(kcol[:], kernT[:], AX.X, ALU.max, apply_absolute_value=True))
                step(nc.vector.tensor_scalar(kz[:], kcol[:], 0.0, None, ALU.is_equal))
                step(nc.vector.scalar_tensor_tensor(out=kcol[:], in0=kcol[:], scalar=1.0 / QMAX, in1=kz[:],
                                                    op0=ALU.mult, op1=ALU.add))
                dve.wait_ge(c_ready, 1)
                for k in range(KC):
                    if k:
                        dve.wait_ge(krow_done, k)
                    nc.vector.tensor_scalar(diag[:], ident[:], kcol[:, k:k + 1], None, ALU.mult).then_inc(diag_ready, 1)
                dve.wait_ge(krow_done, KC)
                step(nc.vector.tensor_copy(krow[:], bank[1][:]))
                step(nc.vector.reciprocal(krinv[:], krow[:]))
                for k in range(KC):
                    step(nc.vector.tensor_tensor(kern[:, k, :], kern[:, k, :], krinv[:], ALU.mult))
                    step(nc.vector.tensor_scalar(kern[:, k, :], kern[:, k, :], MAGIC, None, ALU.add))
                    nc.vector.tensor_scalar(kq[:, k, :], kern[:, k, :], MAGIC, None, ALU.subtract)
                am, z, inv = bqs[:, 0:1], bqs[:, 1:2], bqs[:, 2:3]
                step(nc.vector.tensor_reduce(am, biasrow[:], AX.X, ALU.max, apply_absolute_value=True))
                step(nc.vector.tensor_scalar(z, am, 0.0, None, ALU.is_equal))
                step(nc.vector.scalar_tensor_tensor(out=am, in0=am, scalar=1.0 / QMAX, in1=z,
                                                    op0=ALU.mult, op1=ALU.add))
                step(nc.vector.reciprocal(inv, am))
                step(nc.vector.tensor_scalar(biasrow[:], biasrow[:], inv, None, ALU.mult))
                step(nc.vector.tensor_scalar(biasrow[:], biasrow[:], MAGIC, None, ALU.add))
                step(nc.vector.tensor_scalar(biasrow[:], biasrow[:], MAGIC, am, ALU.subtract, ALU.mult))
                for k in range(KC):
                    nc.vector.tensor_tensor(wout[:, k, k * P:(k + 1) * P], wout[:, k, k * P:(k + 1) * P], ident[:],
                                            ALU.add)
                dve.wait_ge(rms_done, 1)
                nc.vector.reciprocal(rin[:], rms[:])

            @block.tensor
            def _(pe):
                pe.wait_ge(ld_w, 16 * (4 + 2 * HPC))
                for m in range(2 * KC):
                    for k in range(KC):
                        last = nc.tensor.matmul(bank[0][:, m * B:(m + 1) * B], wemb[:, k, m * P:(m + 1) * P],
                                                condT[:, k, :], start=(k == 0), stop=(k == KC - 1))
                last.then_inc(emb_done, 1)
                pe.wait_ge(c_ready, 1)
                for k in range(KC):
                    pe.wait_ge(diag_ready, k + 1)
                    nc.tensor.matmul(bank[1][:, k * P:(k + 1) * P], ones[:], diag[:], start=True, stop=True
                                     ).then_inc(krow_done, 1)

        setup.close()

        xr = sb("xr", [P, TB, D])
        xnT = sb("xnT", [P, KC, T])
        sq = sb("sq", [P, 2, T])
        rs = sb("rs", [P, 2, T])
        ri = sb("ri", [P, 2, T])
        qk = sb("qk", [P, 2 * KC, T])
        v = sb("v", [P, TB, D])
        nmax = sb("nmax", [P, KC, HPC * TB])
        esum = sb("esum", [P, KC, HPC * TB])
        erec = sb("erec", [P, KC, HPC * TB])
        prob = sb("prob", [P, 2, HPC, TB, T])
        probT = sb("probT", [P, HPC, TB, T])
        oT = sb("oT", [P, KC, T])
        yq = sb("yq", [P, TB, D])
        ys = sb("ys", [P, TB, 8])
        qn = sb("qn", [P, TB, D], BF16)
        qT = sb("qT", [P, TB, KC, P], BF16)
        zt = sb("zt", [P, TB, D])
        x1s = sb("x1s", [P, TB, D])

        G, S, PVB = bank[0:2], bank[2:6], bank[6]
        XB = [bank[7][:, :].bitcast(BF16), bank[6][:, :].bitcast(BF16)]
        xr_ready, xT_done, xn_ready = sem("xr_ready"), sem("xT_done"), sem("xn_ready")
        qk_done, sq_ready, ms_done, rs_ready, ri_ready, qk_ready = (
            sem("qk_done"), sem("sq_ready"), sem("ms_done"), sem("rs_ready"), sem("ri_ready"), sem("qk_ready"))
        v_done, v_ready = sem("v_done"), sem("v_ready")
        sc_done, max_ready, exp_ready, rec_ready, prob_ready = (
            sem("sc_done"), sem("max_ready"), sem("exp_ready"), sem("rec_ready"), sem("prob_ready"))
        pT_done, pT_ready, pv_done, oT_ready = sem("pT_done"), sem("pT_ready"), sem("pv_done"), sem("oT_ready")
        y_done, yc, q_ready, qT_done, qT_ready, acc_done, x1_ready, x1T_done, x1T_ready, x1_kept = (
            sem("y_done"), sem("yc"), sem("q_ready"), sem("qT_done"), sem("qT_ready"), sem("acc_done"),
            sem("x1_ready"), sem("x1T_done"), sem("x1T_ready"), sem("x1_kept"))
        M2 = 2 * KC
        NP_ = KC * HPC
        YSTEPS = 30
        with nc.Block() as block:
            @block.tensor
            def _(pe):
                with pe.Fori(0, B) as b:
                    pe.wait_ge(x1T_ready, PRIME + b * TB)
                    for h in range(TB):
                        pe.wait_ge(xr_ready, b * TB + h + 1)
                        for k in range(KC):
                            last = nc.tensor.transpose(G[h][:, k * P:(k + 1) * P], xr[:, h, k * P:(k + 1) * P], ident[:])
                        last.then_inc(xT_done, 1)
                    pe.wait_ge(xn_ready, b * TB + TB)

                    def head_ms(m):
                        pe.wait_ge(sq_ready, b * M2 + m + 1)
                        if m >= 2:
                            pe.wait_ge(rs_ready, b * M2 + m - 1)
                        nc.tensor.matmul(S[m % 2][:, 0:T], headmean[:], sq[:, m % 2, :], start=True, stop=True
                                         ).then_inc(ms_done, 1)

                    for m in range(M2):
                        if m >= 2:
                            pe.wait_ge(qk_ready, b * M2 + m - 1)
                        for k in range(KC):
                            last = nc.tensor.matmul(G[m % 2][:, 0:T], wqkv[:, k, m * P:(m + 1) * P], xnT[:, k, :],
                                                    start=(k == 0), stop=(k == KC - 1))
                        last.then_inc(qk_done, 1)
                        if m:
                            head_ms(m - 1)
                    for h in range(TB):
                        for k in range(KC):
                            last = nc.tensor.matmul(S[2 + h][:], xnT[:, k, h * P:(h + 1) * P], wqkv[:, k, 2 * D:3 * D],
                                                    start=(k == 0), stop=(k == KC - 1))
                        last.then_inc(v_done, 1)
                        if h == 0:
                            head_ms(M2 - 1)

                    def scores(m):
                        if m == 0:
                            pe.wait_ge(qk_ready, b * M2 + M2)
                            pe.wait_ge(v_ready, b * TB + TB)
                        for q in range(TB):
                            for r in range(HPC):
                                if q == 0 and m:
                                    pe.wait_ge(exp_ready, b * NP_ * TB + (m - 1) * HPC * TB + r * TB + TB)
                                rows = slice(DH * r, DH * r + DH)
                                last = nc.tensor.matmul(S[r][:, q * T:(q + 1) * T], qk[rows, m, q * P:(q + 1) * P],
                                                        qk[rows, KC + m, :], start=True, stop=True)
                                if q == TB - 1:
                                    last.then_inc(sc_done, 1)

                    scores(0)
                    for m in range(KC):
                        if m + 1 < KC:
                            scores(m + 1)
                        for r in range(HPC):
                            n = m * HPC + r
                            pe.wait_ge(prob_ready, b * NP_ + n + 1)
                            if n >= 2:
                                pe.wait_ge(pT_ready, b * NP_ + n - 1)
                            for kt in range(TB):
                                for q in range(TB):
                                    c = kt * T + q * P
                                    last = nc.tensor.transpose(G[r % 2][:, c:c + P],
                                                               prob[:, m % 2, r, q, kt * P:(kt + 1) * P], ident[:])
                            last.then_inc(pT_done, 1)
                        pe.wait_ge(pT_ready, b * NP_ + (m + 1) * HPC)
                        if m:
                            pe.wait_ge(oT_ready, b * KC + m)
                        for kt in range(TB):
                            for r in range(HPC):
                                hd = (m * HPC + r) * DH
                                last = nc.tensor.matmul(PVB[DH * r:DH * r + DH, (m % 2) * T:(m % 2 + 1) * T],
                                                        v[:, kt, hd:hd + DH], probT[:, r, kt, :],
                                                        start=(kt == 0), stop=(kt == TB - 1))
                        last.then_inc(pv_done, 1)
                    pe.wait_ge(oT_ready, b * KC + KC)
                    for h in range(TB):
                        for k in range(KC):
                            last = nc.tensor.matmul(S[h][:], oT[:, k, h * P:(h + 1) * P], wout[:, k, :],
                                                    start=(k == 0), stop=(k == KC - 1))
                        last.then_inc(y_done, 1)
                    for h in range(TB):
                        pe.wait_ge(q_ready, b * TB + h + 1)
                        for k in range(KC):
                            last = nc.tensor.transpose(XB[h][:, k * P:(k + 1) * P],
                                                       qn[:, h, k * P:(k + 1) * P], identb[:])
                        last.then_inc(qT_done, 1)
                    for h in range(TB):
                        pe.wait_ge(qT_ready, b * TB + h + 1)
                        for k in range(KC):
                            last = nc.tensor.matmul(S[2 + h][:], qT[:, h, k, :], kq[:, k, :],
                                                    start=(k == 0), stop=(k == KC - 1))
                        last.then_inc(acc_done, 1)
                    for h in range(TB):
                        pe.wait_ge(x1_ready, b * TB + h + 1)
                        for k in range(KC):
                            last = nc.tensor.transpose(G[h][:, k * P:(k + 1) * P], x1s[:, h, k * P:(k + 1) * P], ident[:])
                        last.then_inc(x1T_done, 1)

            @block.scalar
            def _(act):
                act.sem_inc(x1T_ready, PRIME)
                with act.Fori(0, B) as b:
                    def root(m):
                        act.wait_ge(ms_done, b * M2 + m + 1)
                        if m >= 2:
                            act.wait_ge(ri_ready, b * M2 + m - 1)
                        nc.scalar.activation(rs[:, m % 2, :], S[m % 2][:, 0:T], ACT.Sqrt, bias=epsc[:]
                                             ).then_inc(rs_ready, 1)

                    for m in range(M2):
                        act.wait_ge(qk_done, b * M2 + m + 1)
                        nc.scalar.activation(sq[:, m % 2, :], G[m % 2][:, 0:T], ACT.Square).then_inc(sq_ready, 1)
                        if m:
                            root(m - 1)
                    root(M2 - 1)
                    for h in range(TB):
                        act.wait_ge(v_done, b * TB + h + 1)
                        nc.scalar.copy(v[:, h, :], S[2 + h][:]).then_inc(v_ready, 1)

                    def exps(m):
                        if m >= 2:
                            act.wait_ge(pT_done, b * NP_ + (m - 1) * HPC)
                        for r in range(HPC):
                            act.wait_ge(max_ready, b * NP_ + m * HPC + r + 1)
                            for q in range(TB):
                                c = r * TB + q
                                nc.scalar.activation(prob[:, m % 2, r, q, :], S[r][:, q * T:(q + 1) * T], ACT.Exp,
                                                     bias=nmax[:, m, c:c + 1], accum_out=esum[:, m, c:c + 1]
                                                     ).then_inc(exp_ready, 1)

                    def turn(m):
                        if m:
                            act.wait_ge(pv_done, b * KC + m)
                        for r in range(HPC):
                            act.wait_ge(pT_done, b * NP_ + m * HPC + r + 1)
                            nc.scalar.copy(probT[:, r, :, :], G[r % 2][:].rearrange("p (k q) -> p k q", k=TB)
                                           ).then_inc(pT_ready, 1)

                    exps(0)
                    for m in range(KC):
                        if m + 1 < KC:
                            exps(m + 1)
                        turn(m)
                    for h in range(TB):
                        act.wait_ge(qT_done, b * TB + h + 1)
                        nc.scalar.copy(qT[:, h, :, :], XB[h][:, 0:D].rearrange("p (k q) -> p k q", k=KC)
                                       ).then_inc(qT_ready, 1)
                    for h in range(TB):
                        act.wait_ge(x1T_done, b * TB + h + 1)
                        nc.scalar.copy(xT[:, :, bass.ds(b * T + h * P, P)],
                                       G[h][:].rearrange("p (k q) -> p k q", k=KC)).then_inc(x1T_ready, 1)

            @block.vector
            def _(dve):
                with dve.Fori(0, B) as b:
                    for h in range(TB):
                        nc.vector.tensor_scalar(xr[:, h, :], x[:, b * TB + h, :],
                                                rin[:, bass.ds(b * TB + h, 1)], None, ALU.mult).then_inc(xr_ready, 1)
                    for h in range(TB):
                        dve.wait_ge(xT_done, b * TB + h + 1)
                        for k in range(KC):
                            last = nc.vector.tensor_scalar(xnT[:, k, h * P:(h + 1) * P], G[h][:, k * P:(k + 1) * P],
                                                           modG[:, k, bass.ds(b, 1)], modS[:, k, bass.ds(b, 1)],
                                                           ALU.mult, ALU.add)
                        last.then_inc(xn_ready, 1)
                    for m in range(M2):
                        dve.wait_ge(rs_ready, b * M2 + m + 1)
                        nc.vector.reciprocal(ri[:, m % 2, :], rs[:, m % 2, :]).then_inc(ri_ready, 1)
                        dve.wait_ge(ri_ready, b * M2 + m + 1)
                        g = gcol[:, 0:1] if m < KC else gcol[:, 1:2]
                        nc.vector.scalar_tensor_tensor(out=qk[:, m, :], in0=G[m % 2][:, 0:T], scalar=g,
                                                       in1=ri[:, m % 2, :], op0=ALU.mult, op1=ALU.mult
                                                       ).then_inc(qk_ready, 1)

                    def maxes(m):
                        for r in range(HPC):
                            dve.wait_ge(sc_done, b * NP_ + m * HPC + r + 1)
                            nc.vector.tensor_reduce(nmax[:, m, r * TB:(r + 1) * TB],
                                                    S[r][:].rearrange("p (q k) -> p q k", q=TB), AX.X, ALU.max,
                                                    negate=True).then_inc(max_ready, 1)

                    def normalise(m):
                        dve.wait_ge(exp_ready, (b * NP_ + (m + 1) * HPC) * TB)
                        nc.vector.reciprocal(erec[:, m, :], esum[:, m, :]).then_inc(rec_ready, 1)
                        dve.wait_ge(rec_ready, b * KC + m + 1)
                        for r in range(HPC):
                            for q in range(TB):
                                c = r * TB + q
                                last = nc.vector.tensor_scalar(prob[:, m % 2, r, q, :], prob[:, m % 2, r, q, :],
                                                               erec[:, m, c:c + 1], None, ALU.mult)
                            last.then_inc(prob_ready, 1)

                    def keep_o(m):
                        dve.wait_ge(pv_done, b * KC + m + 1)
                        nc.vector.tensor_copy(oT[:, m, :], PVB[:, (m % 2) * T:(m % 2 + 1) * T]).then_inc(oT_ready, 1)

                    maxes(0)
                    for m in range(KC):
                        if m + 1 < KC:
                            maxes(m + 1)
                        normalise(m)
                        if m:
                            keep_o(m - 1)
                    keep_o(KC - 1)

                    step = Chain(dve, yc, b * YSTEPS)

                    def scale(h, c):
                        am, z, inv = ys[:, h, c:c + 1], ys[:, h, c + 1:c + 2], ys[:, h, c + 2:c + 3]
                        step(nc.vector.tensor_scalar(z, am, 0.0, None, ALU.is_equal))
                        step(nc.vector.scalar_tensor_tensor(out=am, in0=am, scalar=1.0 / QMAX, in1=z,
                                                            op0=ALU.mult, op1=ALU.add))
                        step(nc.vector.reciprocal(inv, am))
                        return am, inv

                    for h in range(TB):
                        dve.wait_ge(y_done, b * TB + h + 1)
                        step(nc.vector.tensor_reduce(ys[:, h, 0:1], S[h][:], AX.X, ALU.max, apply_absolute_value=True))
                        _, inv = scale(h, 0)
                        step(nc.vector.tensor_scalar(yq[:, h, :], S[h][:], inv, None, ALU.mult))
                        step(nc.vector.tensor_scalar(yq[:, h, :], yq[:, h, :], MAGIC, None, ALU.add))
                        nc.vector.tensor_scalar(qn[:, h, :], yq[:, h, :], MAGIC, None, ALU.subtract).then_inc(q_ready, 1)
                    for h in range(TB):
                        dve.wait_ge(acc_done, b * TB + h + 1)
                        step(nc.vector.scalar_tensor_tensor(out=zt[:, h, :], in0=S[2 + h][:], scalar=ys[:, h, 0:1],
                                                            in1=krow[:], op0=ALU.mult, op1=ALU.mult))
                        step(nc.vector.tensor_tensor(zt[:, h, :], zt[:, h, :], biasrow[:], ALU.add))
                        step(nc.vector.tensor_reduce(ys[:, h, 4:5], zt[:, h, :], AX.X, ALU.max))
                        step(nc.vector.tensor_scalar(ys[:, h, 4:5], ys[:, h, 4:5], 0.0, None, ALU.max))
                        s2, inv2 = scale(h, 4)
                        if h == 0:
                            dve.wait_ge(x1_kept, PRIME + b * TB)
                        step(nc.vector.tensor_scalar(zt[:, h, :], zt[:, h, :], 0.0, inv2, ALU.max, ALU.mult))
                        step(nc.vector.tensor_scalar(zt[:, h, :], zt[:, h, :], MAGIC, MAGIC, ALU.add, ALU.subtract))
                        nc.vector.scalar_tensor_tensor(out=x1s[:, h, :], in0=zt[:, h, :], scalar=s2,
                                                       in1=x[:, b * TB + h, :], op0=ALU.mult, op1=ALU.add
                                                       ).then_inc(x1_ready, 1)
                    assert step.n <= YSTEPS, step.n
                    self.ysteps = step.n

            @block.gpsimd
            def _(pool):
                pool.sem_inc(x1_kept, PRIME)
                with pool.Fori(0, B) as b:
                    for h in range(TB):
                        pool.wait_ge(x1_ready, b * TB + h + 1)
                        nc.gpsimd.tensor_copy(x[:, b * TB + h, :], x1s[:, h, :]).then_inc(x1_kept, 1)
        assert self.ysteps == YSTEPS, self.ysteps

    def gru(self, ctx):
        nc, io, ident, bank, xT = self.nc, self.io, self.ident, self.bank, self.xT

        def sb(name, shape, dt=F32):
            return ctx.enter_context(nc.sbuf_tensor(name, shape, dt))

        def sem(name):
            return ctx.enter_context(nc.semaphore("g_" + name))

        gi = sb("gi", [P, 2, TC, NG * GB])
        wih = sb("wih", [P, KC, NG * D])
        whh = sb("whh", [P, KC, NG * D])
        bic = sb("bic", [P, NG * KC])
        bhc = sb("bhc", [P, NG * KC])
        bhn = sb("bhn", [P, KC, B])
        hT = sb("hT", [P, KC, 32])
        fold = sb("fold", [P, GB])
        gh = sb("gh", [P, NG, P])
        rg = sb("rg", [P, GB])
        zg = sb("zg", [P, GB])
        ng = sb("ng", [P, GB])
        t1 = sb("t1", [P, GB])
        t2 = sb("t2", [P, GB])
        dh = sb("dh", [P, GB])
        zd = sb("zd", [P, GB])

        ld = sem("ld")
        bias_ready, gi_done, gi_kept = sem("bias_ready"), sem("gi_done"), sem("gi_kept")
        h_ready, rn_done, z_done, rn_kept, z_kept = (
            sem("h_ready"), sem("rn_done"), sem("z_done"), sem("rn_kept"), sem("z_kept"))
        r_folded, n_folded, z_folded = sem("r_folded"), sem("n_folded"), sem("z_folded")
        r_ready, n_ready, z_ready, t1_ready, t2_ready, dh_ready, zd_ready, h_kept = (
            sem("r_ready"), sem("n_ready"), sem("z_ready"), sem("t1_ready"), sem("t2_ready"), sem("dh_ready"),
            sem("zd_ready"), sem("h_kept"))
        R, Z, NN = 0, 1, 2
        RN, ZB, FR, FN = bank[0], bank[1], bank[2], bank[3]
        FZ = bank[4:6]
        GI = bank[6:8]
        hv = hT[:, :, 0:B]
        NCH = T // TC
        MG = NG * KC
        UPS = 2

        def cols(t):
            return t[:].rearrange("p (j b) -> p j b", b=B)

        with nc.Block() as block:
            @block.sync
            def _(sp):
                sp.dma_start(bic[:], io["b_ih"]).then_inc(ld, 16)
                sp.dma_start(bhc[:], io["b_hh"]).then_inc(ld, 16)
                sp.dma_start(hT[:, :, 0:B], io["condT"].rearrange("(k p) b -> p k b", p=P)).then_inc(ld, 16)
                sp.dma_start(wih[:], io["W_ih"].rearrange("(k p) n -> p k n", p=P)).then_inc(ld, 16)
                sp.dma_start(whh[:], io["W_hh"].rearrange("(k p) n -> p k n", p=P)).then_inc(ld, 16)

            @block.tensor
            def _(pe):
                pe.wait_ge(ld, 80)
                pe.wait_ge(bias_ready, 2)
                steps_of = xT[:].rearrange("p k (b t) -> p k b t", t=T)
                w = whh[:].rearrange("p k (g n) -> p k g n", g=NG)

                def input_part(c, p, m):
                    g, j = m // KC, m % KC
                    if j == 0:
                        if not isinstance(c, int):
                            pe.wait_ge(gi_kept, c * NG + g - 1)
                        elif c * NG + g >= 2:
                            pe.wait_ge(gi_kept, c * NG + g - 1)
                    for k in range(KC):
                        last = nc.tensor.matmul(GI[(p + g) % 2][:, j * TC * B:(j + 1) * TC * B],
                                                wih[:, k, m * P:(m + 1) * P],
                                                steps_of[:, k, :, bass.ds(c * TC, TC)],
                                                start=(k == 0), stop=(k == KC - 1))
                    if j == KC - 1:
                        last.then_inc(gi_done, 1)

                def seed(p, s):
                    nc.tensor.matmul(FR[:, 0:GB], ident[:], gi[:, p, s, 0:GB], start=True, stop=False)
                    nc.tensor.matmul(FN[:, 0:GB], ident[:], bhn[:].rearrange("p j b -> p (j b)"),
                                     start=True, stop=False)
                    nc.tensor.matmul(FZ[s % 2][:, 0:GB], ident[:], gi[:, p, s, GB:2 * GB], start=True, stop=False)

                def chunk(c, p, final):
                    for s in range(TC):
                        t = c * TC + s
                        fill = [] if final else [m for m in range(s * UPS, (s + 1) * UPS) if m < MG]
                        pe.wait_ge(h_ready, t + 1)
                        for k in range(KC):
                            for j in range(KC):
                                last = nc.tensor.matmul(RN[32 * j:32 * j + 32, 0:2 * P], hT[:, k, :],
                                                        w[:, k, 0::2, j * P:(j + 1) * P],
                                                        start=(k == 0), stop=(k == KC - 1))
                        last.then_inc(rn_done, 1)
                        for k in range(KC):
                            if k == 2:
                                pe.wait_ge(rn_kept, t + 1)
                                nc.tensor.matmul(FR[:, 0:GB], gh[:, 0, :], fold[:], start=False, stop=True
                                                 ).then_inc(r_folded, 1)
                                nc.tensor.matmul(FN[:, 0:GB], gh[:, 1, :], fold[:], start=False, stop=True
                                                 ).then_inc(n_folded, 1)
                            for j in range(KC):
                                last = nc.tensor.matmul(ZB[32 * j:32 * j + 32, 0:P], hT[:, k, :],
                                                        w[:, k, Z, j * P:(j + 1) * P],
                                                        start=(k == 0), stop=(k == KC - 1))
                        last.then_inc(z_done, 1)
                        for m in fill[:1]:
                            input_part(c + 1, 1 - p, m)
                        pe.wait_ge(z_kept, t + 1)
                        nc.tensor.matmul(FZ[s % 2][:, 0:GB], gh[:, 2, :], fold[:], start=False, stop=True
                                         ).then_inc(z_folded, 1)
                        for m in fill[1:]:
                            input_part(c + 1, 1 - p, m)
                        if s + 1 < TC or not final:
                            pe.wait_ge(t1_ready, t + 1)
                            if s + 1 < TC:
                                seed(p, s + 1)
                            else:
                                pe.wait_ge(gi_kept, (c + 2) * NG)
                                seed(1 - p, 0)

                for m in range(MG):
                    input_part(0, 0, m)
                pe.wait_ge(gi_kept, NG)
                seed(0, 0)
                with pe.Fori(0, NCH // 2 - 1) as cc:
                    chunk(cc * 2, 0, False)
                    chunk(cc * 2 + 1, 1, False)
                chunk(NCH - 2, 0, False)
                chunk(NCH - 1, 1, True)

            @block.scalar
            def _(act):
                with act.Fori(0, NCH) as c:
                    for s in range(TC):
                        t = c * TC + s
                        act.wait_ge(rn_done, t + 1)
                        nc.scalar.copy(gh[:, 0:2, :], RN[:, 0:2 * P].rearrange("p (g c) -> p g c", g=2)
                                       ).then_inc(rn_kept, 1)
                        act.wait_ge(r_folded, t + 1)
                        nc.scalar.activation(rg[:], FR[:, 0:GB], ACT.Tanh, scale=0.5).then_inc(r_ready, 1)
                        act.wait_ge(z_done, t + 1)
                        nc.scalar.copy(gh[:, 2, :], ZB[:, 0:P]).then_inc(z_kept, 1)
                        act.wait_ge(t2_ready, t + 1)
                        nc.scalar.activation(ng[:], t2[:], ACT.Tanh).then_inc(n_ready, 1)
                        act.wait_ge(z_folded, t + 1)
                        nc.scalar.activation(zg[:], FZ[s % 2][:, 0:GB], ACT.Tanh, scale=0.5).then_inc(z_ready, 1)

            @block.vector
            def _(dve):
                dve.wait_ge(ld, 80)
                nc.vector.memset(hT[:, :, B:32], 0.0).then_inc(h_ready, 1)
                nc.vector.tensor_copy(bhn[:], bhc[:, 2 * KC:3 * KC].unsqueeze(2).broadcast_to([P, KC, B]))
                nc.vector.tensor_tensor(bic[:, 0:2 * KC], bic[:, 0:2 * KC], bhc[:, 0:2 * KC], ALU.add
                                        ).then_inc(bias_ready, 1)
                for j in range(KC):
                    last = nc.vector.tensor_copy(fold[:, j * B:(j + 1) * B], ident[:, 32 * j:32 * j + B])
                last.then_inc(bias_ready, 1)
                dve.wait_ge(bias_ready, 2)

                def keep_input(n, p, g):
                    dve.wait_ge(gi_done, n + 1)
                    nc.vector.tensor_tensor(
                        gi[:, p, :, g * GB:(g + 1) * GB].rearrange("p t (j b) -> p j b t", b=B),
                        GI[(p + g) % 2][:].rearrange("p (j b t) -> p j b t", b=B, t=TC)[:, 0:KC],
                        bic[:, g * KC:(g + 1) * KC].unsqueeze(2).unsqueeze(3).broadcast_to([P, KC, B, TC]),
                        ALU.add).then_inc(gi_kept, 1)

                def chunk(c, p, final):
                    dve.wait_ge(gi_kept, (c + 1) * NG)
                    for s in range(TC):
                        t = c * TC + s
                        if not final and s in (2, 4, 6):
                            keep_input((c + 1) * NG + s // 2 - 1, 1 - p, s // 2 - 1)
                        dve.wait_ge(r_ready, t + 1)
                        dve.wait_ge(n_folded, t + 1)
                        nc.vector.scalar_tensor_tensor(out=t1[:], in0=rg[:], scalar=1.0, in1=FN[:, 0:GB],
                                                       op0=ALU.add, op1=ALU.mult).then_inc(t1_ready, 1)
                        dve.wait_ge(t1_ready, t + 1)
                        nc.vector.scalar_tensor_tensor(out=t2[:], in0=t1[:], scalar=0.5,
                                                       in1=gi[:, p, s, 2 * GB:3 * GB],
                                                       op0=ALU.mult, op1=ALU.add).then_inc(t2_ready, 1)
                        dve.wait_ge(n_ready, t + 1)
                        nc.vector.tensor_tensor(cols(dh), hv, cols(ng), ALU.subtract).then_inc(dh_ready, 1)
                        dve.wait_ge(dh_ready, t + 1)
                        dve.wait_ge(z_ready, t + 1)
                        nc.vector.scalar_tensor_tensor(out=zd[:], in0=zg[:], scalar=1.0, in1=dh[:],
                                                       op0=ALU.add, op1=ALU.mult).then_inc(zd_ready, 1)
                        dve.wait_ge(h_kept, PRIME + t)
                        dve.wait_ge(zd_ready, t + 1)
                        nc.vector.scalar_tensor_tensor(out=hv, in0=cols(zd), scalar=0.5, in1=cols(ng),
                                                       op0=ALU.mult, op1=ALU.add).then_inc(h_ready, 1)

                for g in range(NG):
                    keep_input(g, 0, g)
                with dve.Fori(0, NCH // 2 - 1) as cc:
                    chunk(cc * 2, 0, False)
                    chunk(cc * 2 + 1, 1, False)
                chunk(NCH - 2, 0, False)
                chunk(NCH - 1, 1, True)

            @block.gpsimd
            def _(pool):
                hseq = xT[:].rearrange("p k (b t) -> p k b t", t=T)
                pool.sem_inc(h_kept, PRIME)
                with pool.Fori(0, T) as t:
                    pool.wait_ge(h_ready, t + 2)
                    nc.gpsimd.tensor_copy(hseq[:, :, :, t], hv).then_inc(h_kept, 1)

    def router(self, ctx):
        nc, io, x, ident, ones, bank, hT = self.nc, self.io, self.x, self.ident, self.ones, self.bank, self.xT

        def sb(name, shape, dt=F32):
            return ctx.enter_context(nc.sbuf_tensor(name, shape, dt))

        def sem(name):
            return ctx.enter_context(nc.semaphore("r_" + name))

        wr = sb("wr", [P, KC, E])
        shgu = sb("shgu", [P, 2, KC, I])
        shd = sb("shd", [IH, 2, D])
        ebias = sb("ebias", [P, E])
        before = sb("before", [P, P], BF16)
        onesb = sb("onesb", [P, P], BF16)
        slot0 = sb("slot0", [P, E])
        tokid = sb("tokid", [P, NT], I32)
        spare = sb("spare", [P, TOPK])
        zero = sb("zero", [P, 2, D])
        blank = sb("blank", [E, CAP, 2], I32)
        hs = sb("hs", [P, KC, P])
        rows = sb("rows", [P, D])
        sig = sb("sig", [P, I])
        gs = sb("gs", [P, I])
        act_h = sb("act_h", [P, I])
        hTs = sb("hTs", [IH, 2, P])
        sco = sb("sco", [P, E])
        sc = sb("sc", [P, E])
        top2 = sb("top2", [P, NGRP, 8])
        gsc = sb("gsc", [P, NGRP + 4])
        gtop = sb("gtop", [P, 8])
        grep = sb("grep", [P, 16])
        gpick = sb("gpick", [P, 8])
        gmask = sb("gmask", [P, NGRP])
        mk = sb("mk", [P, E])
        top8 = sb("top8", [P, 8])
        taken = sb("taken", [P, E])
        sel = sb("sel", [P, E], BF16)
        count = sb("count", [P, E], BF16)
        wsum = sb("wsum", [P, 2])
        w = sb("w", [P, E])
        fits = sb("fits", [P, E])
        slot = sb("slot", [P, E])
        key = sb("key", [P, E])
        key8 = sb("key8", [P, 8])
        junk = sb("junk", [P, E])
        w8 = sb("w8", [P, 8])
        drop8 = sb("drop8", [P, 8])
        dest = sb("dest", [P, 8])
        desti = sb("desti", [P, 8], I32)
        entry = sb("entry", [P, 8, 2], I32)

        ld, c_ready, k_ready = sem("ld"), sem("c_ready"), sem("k_ready")
        blank_ready, blank_out = sem("blank_ready"), sem("blank_out")
        staged, gu_done, sig_ready, act_ready, hT_done, hT_ready, dn_done, sum_ready = (
            sem("staged"), sem("gu_done"), sem("sig_ready"), sem("act_ready"), sem("hT_done"), sem("hT_ready"),
            sem("dn_done"), sem("sum_ready"))
        lg_done, sco_ready, sel_ready, pos_done, chain, row_done, row_ready, row_out = (
            sem("lg_done"), sem("sco_ready"), sem("sel_ready"), sem("pos_done"), sem("chain"), sem("row_done"),
            sem("row_ready"), sem("row_out"))
        entry_ready, scattered, dchain = sem("entry_ready"), sem("scattered"), sem("dchain")
        acc_out, pool_turn, dve_turn = sem("acc_out"), sem("pool_turn"), sem("dve_turn")
        LG, GU, RW, HT, DN, PS = bank[0], bank[1], bank[2], bank[3], bank[4], bank[5]
        CSTEPS = 33
        with nc.Block() as block:
            @block.sync
            def _(sp):
                sp.dma_start(wr[:], io["routerT"].rearrange("(k p) e -> p k e", p=P)).then_inc(ld, 16)
                for a, n in enumerate(("sh_gate", "sh_up")):
                    sp.dma_start(shgu[:, a], io[n].rearrange("(k p) i -> p k i", p=P)).then_inc(ld, 16)
                sp.dma_start(shd[:], io["sh_down"].rearrange("(p c) d -> p c d", c=2)).then_inc(ld, 16)
                sp.dma_start(ebias[:], io["e_bias"].partition_broadcast(P)).then_inc(ld, 16)
                sp.wait_ge(blank_ready, 1)
                sp.dma_start(self.hs_rows[N:N + CAP, :].rearrange("(c p) d -> p c d", p=P),
                             zero[:]).then_inc(blank_out, 16)
                sp.sem_inc(row_out, PRIME_DMA)
                with sp.Fori(0, NT) as i:
                    sp.wait_ge(row_ready, i + 1)
                    sp.dma_start(self.hs_rows[bass.ds(i * P, P), :], rows[:]).then_inc(row_out, 16)
                sp.wait_ge(sum_ready, NT)
                sp.dma_start(self.acc_rows[0:N, :].rearrange("(t p) d -> p t d", p=P), x[:]).then_inc(acc_out, 16)
                sp.wait_ge(acc_out, 16)
                sp.wait_ge(row_out, PRIME_DMA + 16 * NT)
                sp.wait_ge(blank_out, 16)

            @block.gpsimd
            def _(pool):
                nc.gpsimd.memset(zero[:], 0.0)
                nc.gpsimd.memset(onesb[:], 1.0).then_inc(c_ready, 1)
                nc.gpsimd.memset(before[:], 1.0).then_inc(c_ready, 1)
                nc.gpsimd.iota(tokid[:], pattern=[[P, NT]], base=0, channel_multiplier=1).then_inc(c_ready, 1)
                nc.gpsimd.iota(slot0[:], pattern=[[-CAP, E]], base=int(KEY0), channel_multiplier=0,
                               allow_small_or_imprecise_dtypes=True).then_inc(c_ready, 1)
                nc.gpsimd.iota(spare[:], pattern=[[P, TOPK]], base=SLOTS, channel_multiplier=1,
                               allow_small_or_imprecise_dtypes=True).then_inc(c_ready, 1)
                nc.gpsimd.memset(blank[:], 0).then_inc(c_ready, 1)
                pool.wait_ge(c_ready, 6)
                nc.gpsimd.iota(blank[:, :, 0], pattern=[[1, CAP]], base=N, channel_multiplier=0).then_inc(blank_ready, 1)
                nc.gpsimd.affine_select(out=before[:], in_=before[:], compare_op=ALU.is_gt, fill=0.0, base=0,
                                        pattern=[[1, P]], channel_multiplier=-1).then_inc(c_ready, 1)
                pool.wait_ge(blank_ready, 1)
                nc.gpsimd.dma_start(self.table[0:SLOTS, :].rearrange("(e s) w -> e s w", e=E), blank[:]
                                    ).then_inc(scattered, 16)
                pool.wait_ge(scattered, PRIME_DMA)
                with pool.Fori(0, NT) as i:
                    pool.wait_ge(gu_done, PRIME + i)
                    nc.gpsimd.tensor_copy(hs[:], hT[:, :, bass.ds(i * P, P)]).then_inc(staged, 1)
                    pool.wait_ge(entry_ready, i + 1)
                    pool.sem_inc(pool_turn, 1)
                    for c in range(TOPK):
                        nc.gpsimd.indirect_dma_start(
                            self.table, bass.IndirectOffsetOnAxis(desti[:, c:c + 1].bitcast(U32), 0),
                            entry[:, c, :], None).then_inc(scattered, 16)
                pool.wait_ge(scattered, PRIME_DMA + 16 * TOPK * NT)

            @block.tensor
            def _(pe):
                pe.wait_ge(ld, 80)
                pe.wait_ge(c_ready, 7)
                pe.sem_inc(gu_done, PRIME)
                with pe.Fori(0, NT) as i:
                    pe.wait_ge(staged, i + 1)
                    for k in range(KC):
                        last = nc.tensor.matmul(LG[:, 0:E], hs[:, k, :], wr[:, k, :], start=(k == 0), stop=(k == KC - 1))
                    last.then_inc(lg_done, 1)
                    for k in range(KC):
                        last = nc.tensor.transpose(RW[:, k * P:(k + 1) * P], hs[:, k, :], ident[:])
                    last.then_inc(row_done, 1)
                    for k in range(KC):
                        last = nc.tensor.matmul(GU[:, 0:2 * I], hs[:, k, :], shgu[:, :, k, :],
                                                start=(k == 0), stop=(k == KC - 1))
                    last.then_inc(gu_done, 1)
                    pe.wait_ge(act_ready, i + 1)
                    for c in range(2):
                        last = nc.tensor.transpose(HT[0:IH, c * P:(c + 1) * P], act_h[:, c::2], ident[:])
                    last.then_inc(hT_done, 1)
                    pe.wait_ge(hT_ready, i + 1)
                    for c in range(2):
                        last = nc.tensor.matmul(DN[:], hTs[:, c, :], shd[:, c, :], start=(c == 0), stop=(c == 1))
                    last.then_inc(dn_done, 1)
                    pe.wait_ge(sel_ready, i + 1)
                    nc.tensor.matmul(PS[:, 0:E], before[:], sel[:], start=True, stop=False)
                    nc.tensor.matmul(PS[:, 0:E], onesb[:], count[:], start=False, stop=True).then_inc(pos_done, 1)

            @block.scalar
            def _(act):
                with act.Fori(0, NT) as i:
                    act.wait_ge(lg_done, i + 1)
                    nc.scalar.activation(sco[:], LG[:, 0:E], ACT.Sigmoid).then_inc(sco_ready, 1)
                    act.wait_ge(row_done, i + 1)
                    act.wait_ge(row_out, PRIME_DMA + i * 16)
                    nc.scalar.copy(rows[:], RW[:]).then_inc(row_ready, 1)
                    act.wait_ge(gu_done, PRIME + i + 1)
                    nc.scalar.activation(sig[:], GU[:, 0:I], ACT.Sigmoid).then_inc(sig_ready, 1)
                    act.wait_ge(hT_done, i + 1)
                    nc.scalar.copy(hTs[:], HT[0:IH, 0:2 * P].rearrange("p (c q) -> p c q", c=2)).then_inc(hT_ready, 1)

            @block.vector
            def _(dve):
                first = Chain(dve, dchain)
                first(nc.vector.memset(count[:], 0.0))
                first(nc.vector.memset(gsc[:, NGRP:NGRP + 4], TAKEN))
                first(nc.vector.memset(gpick[:, TOPG:8], TAKEN))
                dve.wait_ge(ld, 80)
                dve.wait_ge(c_ready, 7)
                with dve.Fori(0, NT) as i:
                    step = Chain(dve, chain, i * CSTEPS)
                    dve.wait_ge(sco_ready, i + 1)
                    step(nc.vector.tensor_tensor(sc[:], sco[:], ebias[:], ALU.add))
                    dve.sem_inc(dve_turn, 1)
                    for g in range(NGRP):
                        last = nc.vector.max(top2[:, g, :], sc[:, g * GSZ:(g + 1) * GSZ])
                    step(last)
                    step(nc.vector.tensor_tensor(gsc[:, 0:NGRP], top2[:, :, 0], top2[:, :, 1], ALU.add))
                    dve.sem_inc(dve_turn, 1)
                    step(nc.vector.max(gtop[:], gsc[:, 0:NGRP]))
                    step(nc.vector.tensor_copy(gpick[:, 0:TOPG], gtop[:, 0:TOPG]))
                    dve.sem_inc(dve_turn, 1)
                    step(nc.vector.match_replace(grep[:, 0:NGRP + 4], gpick[:], gsc[:], -2.0 * TAKEN))
                    step(nc.vector.tensor_scalar(gmask[:], grep[:, 0:NGRP], -2.0 * TAKEN, None, ALU.is_equal))
                    step(nc.vector.tensor_tensor(mk[:].rearrange("p (g s) -> p g s", s=GSZ),
                                                 sc[:].rearrange("p (g s) -> p g s", s=GSZ),
                                                 gmask[:].unsqueeze(2).broadcast_to([P, NGRP, GSZ]), ALU.mult))
                    dve.sem_inc(dve_turn, 1)
                    step(nc.vector.max(top8[:], mk[:]))
                    dve.sem_inc(dve_turn, 1)
                    step(nc.vector.match_replace(taken[:], top8[:], mk[:], TAKEN))
                    nc.vector.tensor_scalar(sel[:], taken[:], TAKEN, None, ALU.is_equal).then_inc(sel_ready, 1)
                    step(nc.vector.scalar_tensor_tensor(out=w[:], in0=taken[:], scalar=TAKEN, in1=sco[:],
                                                        op0=ALU.is_equal, op1=ALU.mult, accum_out=wsum[:, 0:1]))
                    step(nc.vector.tensor_scalar(wsum[:, 0:1], wsum[:, 0:1], 1e-20, None, ALU.add))
                    step(nc.vector.reciprocal(wsum[:, 1:2], wsum[:, 0:1]))
                    step(nc.vector.tensor_scalar(w[:], w[:], wsum[:, 1:2], ROUTE_SCALE, ALU.mult, ALU.mult))
                    dve.wait_ge(sig_ready, i + 1)
                    step(nc.vector.tensor_tensor(gs[:], GU[:, 0:I], sig[:], ALU.mult))
                    nc.vector.tensor_tensor(act_h[:], GU[:, I:2 * I], gs[:], ALU.mult).then_inc(act_ready, 1)
                    dve.wait_ge(pos_done, i + 1)
                    step(nc.vector.tensor_scalar(fits[:], PS[:, 0:E], float(CAP), None, ALU.is_lt))
                    step(nc.vector.tensor_scalar(slot[:], PS[:, 0:E], float(CAP - 1), None, ALU.min))
                    step(nc.vector.tensor_tensor(w[:], w[:], fits[:], ALU.mult))
                    step(nc.vector.tensor_tensor(slot[:], slot0[:], slot[:], ALU.subtract))
                    step(nc.vector.tensor_tensor(key[:], slot[:], sel[:], ALU.mult))
                    step(nc.vector.tensor_tensor(count[:], count[:], sel[:], ALU.add))
                    dve.sem_inc(dve_turn, 1)
                    step(nc.vector.max(key8[:], key[:]))
                    dve.wait_ge(scattered, PRIME_DMA + i * 16 * TOPK)
                    for c in range(TOPK):
                        step(nc.vector.scalar_tensor_tensor(out=junk[:], in0=key[:], scalar=key8[:, c:c + 1], in1=w[:],
                                                            op0=ALU.is_equal, op1=ALU.mult, accum_out=w8[:, c:c + 1]))
                    step(nc.vector.scalar_tensor_tensor(out=drop8[:], in0=w8[:], scalar=0.0, in1=spare[:],
                                                        op0=ALU.is_equal, op1=ALU.mult))
                    step(nc.vector.tensor_scalar(dest[:], key8[:], -1.0, KEY0, ALU.mult, ALU.add))
                    step(nc.vector.tensor_tensor(dest[:], dest[:], drop8[:], ALU.max))
                    nc.vector.tensor_copy(desti[:], dest[:])
                    nc.vector.tensor_copy(entry[:, :, 1].bitcast(F32), w8[:])
                    nc.vector.tensor_copy(entry[:, :, 0], tokid[:, bass.ds(i, 1)].broadcast_to([P, TOPK])
                                          ).then_inc(entry_ready, 1)
                    dve.wait_ge(dn_done, i + 1)
                    nc.vector.tensor_tensor(x[:, i, :], x[:, i, :], DN[:], ALU.add).then_inc(sum_ready, 1)
                    self.csteps = step.n
        assert self.csteps == CSTEPS, self.csteps

    def experts(self, ctx):
        nc, io, ident, bank = self.nc, self.io, self.ident, self.bank

        def sb(name, shape, dt=F32):
            return ctx.enter_context(nc.sbuf_tensor(name, shape, dt))

        def sem(name):
            return ctx.enter_context(nc.semaphore("e_" + name))

        wgu = [sb(f"wgu{s}", [P, 2, KC, I]) for s in range(2)]
        wdn = [sb(f"wdn{s}", [IH, 2, D]) for s in range(2)]
        tab = sb("tab", [P, P, 2], I32)
        tabf = sb("tabf", [P, 2, P])
        slot_tok = sb("slot_tok", [P, NU], I32)
        slot_w = sb("slot_w", [P, NU])
        idx = [sb(f"idx{h}", [P, 1], I32) for h in range(2)]
        idy = [sb(f"idy{h}", [P, 1], I32) for h in range(2)]
        xg = [sb(f"xg{h}", [P, D]) for h in range(2)]
        xgT = sb("xgT", [P, 2, KC, P])
        sig = sb("sig_e", [P, 2, I])
        gs = sb("gs_e", [P, 2, I])
        ah = sb("ah", [P, 2, I])
        ahT = sb("ahT", [IH, 2, 2, P])
        y = [sb(f"y{h}", [P, D]) for h in range(2)]

        tab_ld, tab_f, tab_T, tab_ready = sem("tab_ld"), sem("tab_f"), sem("tab_T"), sem("tab_ready")
        w_ld = [sem("w_ld0"), sem("w_ld1")]
        idx_ready, gathered, idy_ready, added = (sem("idx_ready"), [sem("gathered0"), sem("gathered1")],
                                                 sem("idy_ready"), [sem("added0"), sem("added1")])
        xT_done, xT_ready, gu_done, sig_ready, gs_ready, ah_ready, ahT_done, ahT_ready, y_done, y_ready = (
            sem("xT_done"), sem("xT_ready"), sem("gu_done"), sem("sig_ready"), sem("gs_ready"), sem("ah_ready"),
            sem("ahT_done"), sem("ahT_ready"), sem("y_done"), sem("y_ready"))
        out_done, pool_turn, cleared = sem("out_done"), sem("pool_turn"), sem("cleared")
        XT, GU, HT, DN = bank[0:2], bank[2:4], bank[4:6], bank[6:8]

        def load(eng, e, s):
            for a, n in enumerate(("w_gate", "w_up")):
                eng.dma_start(wgu[s][:, a], io[n][e].rearrange("(p k) i -> p k i", k=KC)).then_inc(w_ld[s], 16)
            eng.dma_start(wdn[s][:], io["w_down"][e].rearrange("(p c) d -> p c d", c=2)).then_inc(w_ld[s], 16)

        with nc.Block() as block:
            @block.sync
            def _(sp):
                sp.dma_start(tab[:], self.table[0:SLOTS, :].rearrange("(c p) w -> c p w", p=P)).then_inc(tab_ld, 16)
                load(sp, 0, 0)
                load(sp, 1, 1)
                with sp.Fori(0, E // 2 - 1) as ee:
                    for s in range(2):
                        sp.wait_ge(y_done, (ee * 2 + s) * 2 + 2)
                        for a, n in enumerate(("w_gate", "w_up")):
                            sp.dma_start(wgu[s][:, a], io[n][bass.ds(ee * 2 + 2 + s, 1)].rearrange("e (p k) i -> p (e k) i", k=KC)
                                         ).then_inc(w_ld[s], 16)
                        sp.dma_start(wdn[s][:], io["w_down"][bass.ds(ee * 2 + 2 + s, 1)].rearrange("e (p c) d -> p (e c) d", c=2)
                                     ).then_inc(w_ld[s], 16)
                for h in range(2):
                    sp.wait_ge(added[h], PRIME_DMA + 16 * E)
                sp.dma_start(self.out, self.acc_rows[0:N, :]).then_inc(out_done, 16)
                sp.wait_ge(out_done, 16)

            @block.gpsimd
            def _(pool):
                pool.wait_ge(tab_ready, 1)

                def gather(u, h):
                    nc.gpsimd.tensor_copy(idx[h][:], slot_tok[:, bass.ds(u, 1)]).then_inc(idx_ready, 1)
                    pool.wait_ge(idx_ready, u + 1)
                    pool.sem_inc(pool_turn, 1)
                    nc.gpsimd.indirect_dma_start(xg[h][:], None, self.hs_rows,
                                                 bass.IndirectOffsetOnAxis(idx[h][:].bitcast(U32), 0)
                                                 ).then_inc(gathered[h], 16)

                def add_rows(u, e, h):
                    pool.wait_ge(added[h], PRIME_DMA + e * 16)
                    nc.gpsimd.tensor_copy(idy[h][:], slot_tok[:, bass.ds(u, 1)]).then_inc(idy_ready, 1)
                    pool.wait_ge(idy_ready, u + 1)
                    pool.wait_ge(y_ready, u + 1)
                    if h == 0:
                        pool.wait_ge(added[1], PRIME_DMA + e * 16)
                    pool.sem_inc(pool_turn, 1)
                    nc.gpsimd.indirect_dma_start(self.acc_rows, bass.IndirectOffsetOnAxis(idy[h][:].bitcast(U32), 0),
                                                 y[h][:], None, compute_op=ALU.add).then_inc(added[h], 16)

                for h in range(2):
                    nc.gpsimd.memset(y[h][:], 0.0).then_inc(cleared, 1)
                    pool.wait_ge(cleared, h + 1)
                    nc.gpsimd.dma_start(self.acc_rows[N + h * P:N + (h + 1) * P, :], y[h][:]).then_inc(added[h], 16)
                    gather(h, h)
                for h in range(2):
                    pool.wait_ge(xT_done, h + 1)
                    gather(2 + h, h)
                with pool.Fori(0, E - 2) as e:
                    for h in range(2):
                        pool.wait_ge(xT_done, e * 2 + 2 + h + 1)
                        gather(e * 2 + 4 + h, h)
                        add_rows(e * 2 + h, e, h)
                for e in (E - 2, E - 1):
                    for h in range(2):
                        add_rows(e * 2 + h, e, h)

            @block.tensor
            def _(pe):
                pe.wait_ge(tab_f, 1)
                for a in range(2):
                    last = nc.tensor.transpose(bank[0][:, a * P:(a + 1) * P], tabf[:, a, :], ident[:])
                last.then_inc(tab_T, 1)
                pe.wait_ge(tab_ready, 1)

                def turn_x(e, h):
                    pe.wait_ge(gathered[h], e * 16 + 16)
                    for k in range(KC):
                        last = nc.tensor.transpose(XT[h][:, k * P:(k + 1) * P], xg[h][:, k::KC], ident[:])
                    last.then_inc(xT_done, 1)

                def expert(e, s, wl, last_one):
                    pe.wait_ge(w_ld[s], wl)
                    for h in range(2):
                        pe.wait_ge(xT_ready, e * 2 + h + 1)
                        for k in range(KC):
                            last = nc.tensor.matmul(GU[h][:, 0:2 * I], xgT[:, h, k, :], wgu[s][:, :, k, :],
                                                    start=(k == 0), stop=(k == KC - 1))
                        last.then_inc(gu_done, 1)
                    def turn_inner(h):
                        pe.wait_ge(ah_ready, e * 2 + h + 1)
                        for c in range(2):
                            last = nc.tensor.transpose(HT[h][0:IH, c * P:(c + 1) * P], ah[:, h, c::2], ident[:])
                        last.then_inc(ahT_done, 1)

                    def down(h):
                        pe.wait_ge(ahT_ready, e * 2 + h + 1)
                        for c in range(2):
                            last = nc.tensor.matmul(DN[h][:], ahT[:, h, c, :], wdn[s][:, c, :],
                                                    start=(c == 0), stop=(c == 1))
                        last.then_inc(y_done, 1)

                    turn_inner(0)
                    if not last_one:
                        turn_x(e + 1, 0)
                    turn_inner(1)
                    down(0)
                    if not last_one:
                        turn_x(e + 1, 1)
                    down(1)

                for h in range(2):
                    turn_x(0, h)
                with pe.Fori(0, E // 2 - 1) as ee:
                    for s in range(2):
                        expert(ee * 2 + s, s, ee * 48 + 48, False)
                expert(E - 2, 0, 24 * E, False)
                expert(E - 1, 1, 24 * E, True)

            @block.scalar
            def _(act):
                def keep_x(e, h):
                    act.wait_ge(xT_done, e * 2 + h + 1)
                    nc.scalar.copy(xgT[:, h, :, :], XT[h][:].rearrange("p (k q) -> p k q", k=KC)).then_inc(xT_ready, 1)

                def expert(e, last_one):
                    for h in range(2):
                        act.wait_ge(gu_done, e * 2 + h + 1)
                        nc.scalar.activation(sig[:, h, :], GU[h][:, 0:I], ACT.Sigmoid).then_inc(sig_ready, 1)
                    def keep_inner(h):
                        act.wait_ge(ahT_done, e * 2 + h + 1)
                        nc.scalar.copy(ahT[:, h, :, :], HT[h][0:IH, 0:2 * P].rearrange("p (c q) -> p c q", c=2)
                                       ).then_inc(ahT_ready, 1)

                    keep_inner(0)
                    keep_inner(1)
                    if not last_one:
                        keep_x(e + 1, 0)
                        keep_x(e + 1, 1)

                for h in range(2):
                    keep_x(0, h)
                with act.Fori(0, E - 1) as e:
                    expert(e, False)
                expert(E - 1, True)

            @block.vector
            def _(dve):
                dve.wait_ge(tab_ld, 16)
                nc.vector.tensor_copy(tabf[:, 0, :], tab[:, :, 0])
                nc.vector.tensor_copy(tabf[:, 1, :], tab[:, :, 1].bitcast(F32)).then_inc(tab_f, 1)
                dve.wait_ge(tab_T, 1)
                nc.vector.tensor_copy(slot_tok[:], bank[0][:, 0:P])
                nc.vector.tensor_copy(slot_w[:], bank[0][:, P:2 * P]).then_inc(tab_ready, 1)
                dve.wait_ge(tab_ready, 1)

                with dve.Fori(0, E) as e:
                    for h in range(2):
                        u = e * 2 + h
                        dve.wait_ge(sig_ready, u + 1)
                        nc.vector.tensor_tensor(gs[:, h, :], GU[h][:, 0:I], sig[:, h, :], ALU.mult).then_inc(gs_ready, 1)
                        dve.wait_ge(gs_ready, u + 1)
                        nc.vector.tensor_tensor(ah[:, h, :], GU[h][:, I:2 * I], gs[:, h, :], ALU.mult
                                                ).then_inc(ah_ready, 1)
                    for h in range(2):
                        u = e * 2 + h
                        dve.wait_ge(y_done, u + 1)
                        dve.wait_ge(added[h], PRIME_DMA + e * 16)
                        nc.vector.tensor_scalar(y[h][:], DN[h][:], slot_w[:, bass.ds(u, 1)], None, ALU.mult
                                                ).then_inc(y_ready, 1)


_DIRECT = {"W_emb": "L0_cond_W_emb", "W_qkv": "L0_cond_W_qkv", "W_out": "L0_cond_W_out", "kernel": "L0_ffn_kernel",
           "ffn_bias": "L0_ffn_bias", "W_ih": "L1_cond_W_ih", "W_hh": "L1_cond_W_hh", "e_bias": "L1_ffn_e_bias",
           "w_gate": "L1_ffn_w_gate", "w_up": "L1_ffn_w_up", "w_down": "L1_ffn_w_down",
           "sh_gate": "L1_ffn_sh_gate", "sh_up": "L1_ffn_sh_up", "sh_down": "L1_ffn_sh_down"}


def lay_out(inputs):
    import numpy as np

    def chunks(v):
        return np.ascontiguousarray(np.asarray(v).reshape(-1, P).T)

    a = {k: np.ascontiguousarray(inputs[n]) for k, n in _DIRECT.items()}
    a["x"] = np.ascontiguousarray(inputs["x"]).reshape(N, D)
    a["condT"] = np.ascontiguousarray(np.asarray(inputs["cond_2048"]).T)
    a["b_emb"] = chunks(inputs["L0_cond_b_emb"])
    a["g_norm"] = chunks(inputs["L0_cond_g_norm"])
    a["g_q"] = np.ascontiguousarray(inputs["L0_cond_g_q"]).reshape(DH, 1)
    a["g_k"] = np.ascontiguousarray(inputs["L0_cond_g_k"]).reshape(DH, 1)
    a["kernelT"] = np.ascontiguousarray(np.asarray(inputs["L0_ffn_kernel"]).T)
    a["b_ih"] = chunks(inputs["L1_cond_b_ih"])
    a["b_hh"] = chunks(inputs["L1_cond_b_hh"])
    a["routerT"] = np.ascontiguousarray(np.asarray(inputs["L1_ffn_router_weight"]).T)
    return a


def program(nc, shapes):
    io = {n: nc.dram_tensor("in_" + n, s, dt, kind="ExternalInput").ap() for n, (s, dt) in shapes.items()}
    out = nc.dram_tensor("out_rows", [N, D], F32, kind="ExternalOutput").ap()
    Kernel(nc, io, out).build()


def kernel(**inputs):
    import numpy as np
    import concourse.bacc as bacc
    from concourse.bass_utils import run_bass_kernel_spmd

    arrays = lay_out(inputs)
    nc = bacc.Bacc("TRN2", target_bir_lowering=False, num_devices=1)
    program(nc, {n: (a.shape, mybir.dt.from_np(a.dtype)) for n, a in arrays.items()})
    r = run_bass_kernel_spmd(nc, [{"in_" + n: a for n, a in arrays.items()}], core_ids=[0])
    return np.asarray(r.results[0]["out_rows"]).reshape(B, T, D)
```

```python
from contextlib import ExitStack

import concourse.bass as bass
from concourse import mybir

P = 128
F32 = mybir.dt.float32
BF16 = mybir.dt.bfloat16
I32 = mybir.dt.int32
U32 = mybir.dt.uint32
ALU = mybir.AluOpType
ACT = mybir.ActivationFunctionType
AX = mybir.AxisListType

B, T, D = 8, 256, 512
N = B * T
KC = D // P
NT = N // P
TB = T // P
HEADS = 16
DH = D // HEADS
HPC = P // DH
NG = 3
TC = 16
GB = KC * B
E, I = 64, 176
IH = I // 2
NGRP, GSZ, TOPG, TOPK = 8, 8, 4, 8
CAP = 256
SLOTS = E * CAP
NU = SLOTS // P
ROUTE_SCALE = 2.5
QMAX = 127.0
MAGIC = 12582912.0
RMS_EPS = 1e-6
TAKEN = -1e30
KEY0 = 32768.0


class Chain:

    def __init__(self, eng, sem, base=0):
        self.eng, self.sem, self.base, self.n = eng, sem, base, 0

    def __call__(self, ins):
        self.n += 1
        ins.then_inc(self.sem, 1)
        self.eng.wait_ge(self.sem, self.base + self.n)


PRIME = 1
PRIME_DMA = 16


class Kernel:
    def __init__(self, nc, io, out):
        self.nc, self.io, self.out = nc, io, out
        self.hs_rows = nc.dram_tensor("hs_rows", [N + CAP, D + E], F32, kind="Internal").ap()
        self.acc_rows = nc.dram_tensor("acc_rows", [N + CAP, D], F32, kind="Internal").ap()
        self.table = nc.dram_tensor("slot_table", [SLOTS + TOPK * P, 1], I32, kind="Internal").ap()

    def build(self):
        with ExitStack() as ctx:
            nc = self.nc
            self.x = ctx.enter_context(nc.sbuf_tensor("x", [P, NT, D], F32))
            self.ident = ctx.enter_context(nc.sbuf_tensor("ident", [P, P], F32))
            self.ones = ctx.enter_context(nc.sbuf_tensor("ones", [P, P], F32))
            self.bank = [ctx.enter_context(nc.psum_tensor(f"bank{i}", [P, 512], F32)) for i in range(8)]
            self.xT = ctx.enter_context(nc.sbuf_tensor("xT", [P, KC, N], F32))
            with ExitStack() as c01:
                self.w_in = c01.enter_context(nc.sbuf_tensor("w_in", [P, KC, 3 * D], F32))
                self.whh = c01.enter_context(nc.sbuf_tensor("whh", [P, KC, NG * D], F32))
                with ExitStack() as c0:
                    self.layer0(c0)
                with ExitStack() as c1:
                    self.gru(c1)
            with ExitStack() as c2:
                self.router(c2)
            with ExitStack() as c3:
                self.experts(c3)

    def layer0(self, ctx):
        nc, io, x, ident, ones, bank, xT = self.nc, self.io, self.x, self.ident, self.ones, self.bank, self.xT

        def sb(name, shape, dt=F32):
            return ctx.enter_context(nc.sbuf_tensor(name, shape, dt))

        def sem(name):
            return ctx.enter_context(nc.semaphore("a_" + name))

        identb = sb("identb", [P, P], BF16)
        onesb = sb("ones_bf16", [P, P], BF16)
        gcol = sb("gcol", [P, 2])
        wqkv = self.w_in
        wout = sb("wout", [P, KC, D])
        biasrow = sb("biasrow", [P, D])
        modG = sb("modG", [P, KC, B])
        modS = sb("modS", [P, KC, B])
        kq = sb("kq", [P, KC, D], BF16)
        krow = sb("krow", [P, D])
        rin = sb("rin", [P, NT])
        epsc = sb("epsc", [P, 1])

        setup = ExitStack()

        def tmp_sb(name, shape, dt=F32):
            return setup.enter_context(nc.sbuf_tensor(name, shape, dt))

        wemb = tmp_sb("wemb", [P, KC, 2 * D])
        condT = tmp_sb("condT", [P, KC, B])
        bembc = tmp_sb("bembc", [P, 2 * KC])
        gnc = tmp_sb("gnc", [P, KC])
        kern = tmp_sb("kern", [P, KC, D])
        kernT = tmp_sb("kernT", [P, KC, D])
        krinv = tmp_sb("krinv", [P, D])
        kcol = tmp_sb("kcol", [P, KC])
        kz = tmp_sb("kz", [P, KC])
        diag = tmp_sb("diag", [P, P])
        tmp = tmp_sb("tmp", [P, D])
        bqs = tmp_sb("bqs", [P, 3])
        ssq = tmp_sb("ssq", [P, NT])
        rms = tmp_sb("rms", [P, NT])
        sqd = tmp_sb("sqd", [P, D])
        sqa = tmp_sb("sqa", [P, D])

        ld_x, ld_w, ld_k = [sem(f"ld_x{i}") for i in range(NT // 4)], sem("ld_w"), sem("ld_k")
        c_id, c_ready = sem("c_id"), sem("c_ready")
        emb_done, mod_chain, ss_act, ss_done, rms_done = (
            sem("emb_done"), sem("mod_chain"), sem("ss_act"), sem("ss_done"), sem("rms_done"))
        krow_done, diag_ready = sem("krow_done"), sem("diag_ready")
        with nc.Block() as block:
            @block.sync
            def _(sp):
                sp.dma_start(condT[:], io["condT"].rearrange("(k p) b -> p k b", p=P)).then_inc(ld_w, 16)
                sp.dma_start(wemb[:], io["W_emb"].rearrange("(k p) n -> p k n", p=P)).then_inc(ld_w, 16)
                for t in range(0, NT, 4):
                    sp.dma_start(x[:, t:t + 4, :], io["x"][t * P:(t + 4) * P, :].rearrange("(t p) d -> p t d", p=P)
                                 ).then_inc(ld_x[t // 4], 16)
                sp.dma_start(wqkv[:], io["W_qkv"].rearrange("(k p) n -> p k n", p=P)).then_inc(ld_k, 16)

            @block.scalar
            def _(act):
                act.dma_start(bembc[:], io["b_emb"]).then_inc(ld_w, 16)
                act.dma_start(gnc[:], io["g_norm"]).then_inc(ld_w, 16)
                for r in range(HPC):
                    act.dma_start(gcol[DH * r:DH * r + DH, 0:1], io["g_q"]).then_inc(ld_w, 16)
                    act.dma_start(gcol[DH * r:DH * r + DH, 1:2], io["g_k"]).then_inc(ld_w, 16)
                act.dma_start(kern[:], io["kernel"].rearrange("(k p) n -> p k n", p=P)).then_inc(ld_k, 16)
                act.dma_start(kernT[:], io["kernelT"].rearrange("(k p) n -> p k n", p=P)).then_inc(ld_k, 16)
                act.dma_start(wout[:], io["W_out"].rearrange("(k p) n -> p k n", p=P)).then_inc(ld_k, 16)
                act.dma_start(biasrow[:], io["ffn_bias"].partition_broadcast(P)).then_inc(ld_k, 16)
                for t in range(1, NT, 2):
                    act.wait_ge(ld_x[t // 4], 16)
                    if t > 1:
                        act.wait_ge(ss_act, t // 2)
                    nc.scalar.activation(sqa[:], x[:, t, :], ACT.Square, accum_out=ssq[:, t:t + 1]
                                         ).then_inc(ss_act, 1)
                act.wait_ge(ss_act, NT // 2)
                act.wait_ge(ss_done, NT // 2)
                act.wait_ge(c_ready, 1)
                nc.scalar.activation(rms[:], ssq[:], ACT.Sqrt, bias=epsc[:], scale=1.0 / D).then_inc(rms_done, 1)

            @block.gpsimd
            def _(pool):
                nc.gpsimd.memset(ident[:], 0.0).then_inc(c_id, 1)
                nc.gpsimd.memset(identb[:], 0.0).then_inc(c_id, 1)
                pool.wait_ge(c_id, 2)
                for m in (ident, identb):
                    nc.gpsimd.affine_select(out=m[:], in_=m[:], compare_op=ALU.not_equal, fill=1.0, base=0,
                                            pattern=[[-1, P]], channel_multiplier=1)
                nc.gpsimd.memset(ones[:], 1.0)
                nc.gpsimd.memset(onesb[:], 1.0)
                nc.gpsimd.memset(epsc[:], RMS_EPS).then_inc(c_ready, 1)

            @block.vector
            def _(dve):
                step = Chain(dve, mod_chain)
                dve.wait_ge(ld_w, 16 * (4 + 2 * HPC))
                dve.wait_ge(emb_done, 1)
                emb = bank[0][:, 0:2 * KC * B].rearrange("p (m b) -> p m b", b=B)
                for k in range(KC):
                    nc.vector.tensor_scalar(modG[:, k, :], emb[:, k, :], bembc[:, k:k + 1], 1.0, ALU.add, ALU.add)
                    last = nc.vector.tensor_scalar(modS[:, k, :], emb[:, KC + k, :], bembc[:, KC + k:KC + k + 1],
                                                   None, ALU.add)
                step(last)
                for k in range(KC):
                    nc.vector.tensor_scalar(modG[:, k, :], modG[:, k, :], gnc[:, k:k + 1], None, ALU.mult)
                nc.vector.tensor_scalar(gcol[:, 0:1], gcol[:, 0:1], float(DH) ** -0.5, None, ALU.mult)
                for t in range(0, NT, 2):
                    dve.wait_ge(ld_x[t // 4], 16)
                    if t:
                        dve.wait_ge(ss_done, t // 2)
                    nc.vector.tensor_tensor_reduce(sqd[:], x[:, t, :], x[:, t, :], 1.0, 0.0, ALU.mult, ALU.add,
                                                   ssq[:, t:t + 1]).then_inc(ss_done, 1)
                dve.wait_ge(ld_k, 16 * 5)
                step(nc.vector.tensor_reduce(kcol[:], kernT[:], AX.X, ALU.max, apply_absolute_value=True))
                step(nc.vector.tensor_scalar(kz[:], kcol[:], 0.0, None, ALU.is_equal))
                step(nc.vector.scalar_tensor_tensor(out=kcol[:], in0=kcol[:], scalar=1.0 / QMAX, in1=kz[:],
                                                    op0=ALU.mult, op1=ALU.add))
                dve.wait_ge(c_ready, 1)
                for k in range(KC):
                    if k:
                        dve.wait_ge(krow_done, k)
                    nc.vector.tensor_scalar(diag[:], ident[:], kcol[:, k:k + 1], None, ALU.mult).then_inc(diag_ready, 1)
                dve.wait_ge(krow_done, KC)
                step(nc.vector.tensor_copy(krow[:], bank[1][:]))
                step(nc.vector.reciprocal(krinv[:], krow[:]))
                for k in range(KC):
                    step(nc.vector.tensor_tensor(kern[:, k, :], kern[:, k, :], krinv[:], ALU.mult))
                    step(nc.vector.tensor_scalar(kern[:, k, :], kern[:, k, :], MAGIC, None, ALU.add))
                    nc.vector.tensor_scalar(kq[:, k, :], kern[:, k, :], MAGIC, None, ALU.subtract)
                am, z, inv = bqs[:, 0:1], bqs[:, 1:2], bqs[:, 2:3]
                step(nc.vector.tensor_reduce(am, biasrow[:], AX.X, ALU.max, apply_absolute_value=True))
                step(nc.vector.tensor_scalar(z, am, 0.0, None, ALU.is_equal))
                step(nc.vector.scalar_tensor_tensor(out=am, in0=am, scalar=1.0 / QMAX, in1=z,
                                                    op0=ALU.mult, op1=ALU.add))
                step(nc.vector.reciprocal(inv, am))
                step(nc.vector.tensor_scalar(biasrow[:], biasrow[:], inv, None, ALU.mult))
                step(nc.vector.tensor_scalar(biasrow[:], biasrow[:], MAGIC, None, ALU.add))
                step(nc.vector.tensor_scalar(biasrow[:], biasrow[:], MAGIC, am, ALU.subtract, ALU.mult))
                for k in range(KC):
                    nc.vector.tensor_tensor(wout[:, k, k * P:(k + 1) * P], wout[:, k, k * P:(k + 1) * P], ident[:],
                                            ALU.add)
                dve.wait_ge(rms_done, 1)
                nc.vector.reciprocal(rin[:], rms[:])

            @block.tensor
            def _(pe):
                pe.wait_ge(ld_w, 16 * (4 + 2 * HPC))
                for m in range(2 * KC):
                    for k in range(KC):
                        last = nc.tensor.matmul(bank[0][:, m * B:(m + 1) * B], wemb[:, k, m * P:(m + 1) * P],
                                                condT[:, k, :], start=(k == 0), stop=(k == KC - 1))
                last.then_inc(emb_done, 1)
                pe.wait_ge(c_ready, 1)
                for k in range(KC):
                    pe.wait_ge(diag_ready, k + 1)
                    nc.tensor.matmul(bank[1][:, k * P:(k + 1) * P], ones[:], diag[:], start=True, stop=True
                                     ).then_inc(krow_done, 1)

        setup.close()

        xr = sb("xr", [P, TB, D])
        xnT = sb("xnT", [P, KC, T])
        sq = sb("sq", [P, 2 * D])
        ss = sb("ss", [P, TB, 2 * HEADS])
        rt = sb("rt", [P, TB, 2 * HEADS])
        ri = sb("ri", [P, TB, 2 * HEADS])
        qkn = sb("qkn", [P, TB, 2 * D])
        qT = sb("qT", [P, KC, T])
        kT = sb("kT", [P, KC, T])
        v = sb("v", [P, TB, D])
        nmax = sb("nmax", [P, KC, TB, HPC])
        nmb = sb("nmb", [P, TB, KC, P], BF16)
        nmT = sb("nmT", [P, KC, T], BF16)
        pT = sb("pT", [P, 2 * HPC, TB, T])
        orc = sb("orc", [P, 2, T])
        oT = sb("oT", [P, KC, T])
        yq = sb("yq", [P, TB, D])
        ys = sb("ys", [P, TB, 8])
        qn = sb("qn", [P, TB, D], BF16)
        qnT = sb("qnT", [P, TB, KC, P], BF16)
        zt = sb("zt", [P, TB, D])
        x1s = sb("x1s", [P, TB, D])

        G, S, A = bank[0:2], bank[2:6], bank[6:8]
        GB16 = [g[:].bitcast(BF16) for g in G]
        NMB = A[0][:].bitcast(BF16)
        xr_ready, xT_done, xn_act, xn_dve = sem("xr_ready"), sem("xT_done"), sem("xn_act"), sem("xn_dve")
        qk_done, sq_ready, ss_ready, rt_ready, ri_ready, qkn_ready = (
            sem("qk_done"), sem("sq_ready"), sem("ss_ready"), sem("rt_ready"), sem("ri_ready"), sem("qkn_ready"))
        v_done, v_ready = sem("v_done"), sem("v_ready")
        qT_done, qT_ready, kT_done, kT_ready = sem("qT_done"), sem("qT_ready"), sem("kT_done"), sem("kT_ready")
        s_done, max_ready, hi_ready, nm_ready, nmT_done, nmT_ready = (
            sem("s_done"), sem("max_ready"), sem("hi_ready"), sem("nm_ready"), sem("nmT_done"), sem("nmT_ready"))
        st_done, exp_ready, pv_done, orc_ready, oT_ready = (
            sem("st_done"), sem("exp_ready"), sem("pv_done"), sem("orc_ready"), sem("oT_ready"))
        y_done, yc, q_ready, qnT_done, qnT_ready, acc_done, x1_ready, x1T_done, x1T_ready, x1_kept = (
            sem("y_done"), sem("yc"), sem("q_ready"), sem("qnT_done"), sem("qnT_ready"), sem("acc_done"),
            sem("x1_ready"), sem("x1T_done"), sem("x1T_ready"), sem("x1_kept"))
        pool_turn = sem("pool_turn")
        w_next = sem("w_next")
        YSTEPS = 28

        with nc.Block() as block:
            @block.sync
            def _(sp):
                sp.dma_start(self.whh[:], io["W_hh"].rearrange("(k p) n -> p k n", p=P)).then_inc(w_next, 16)
                sp.wait_ge(v_done, B * TB)
                sp.dma_start(self.w_in[:], io["W_ih"].rearrange("(k p) n -> p k n", p=P)).then_inc(w_next, 16)
                sp.wait_ge(w_next, 32)

            @block.tensor
            def _(pe):
                def project(f, h, k):
                    if h == 0 and k == 0:
                        pe.wait_ge(oT_ready, f * KC + KC)
                    last = nc.tensor.matmul(G[h][:], oT[:, k, h * P:(h + 1) * P], wout[:, k, :],
                                            start=(k == 0), stop=(k == KC - 1))
                    if k == KC - 1:
                        last.then_inc(y_done, 1)

                def turn_quantised(f, h):
                    pe.wait_ge(q_ready, f * TB + h + 1)
                    for k in range(KC):
                        last = nc.tensor.transpose(GB16[h][:, k * P:(k + 1) * P], qn[:, h, k * P:(k + 1) * P], identb[:])
                    last.then_inc(qnT_done, 1)

                def feed(f, h):
                    pe.wait_ge(qnT_ready, f * TB + h + 1)
                    for k in range(KC):
                        last = nc.tensor.matmul(G[h][:], qnT[:, h, k, :], kq[:, k, :],
                                                start=(k == 0), stop=(k == KC - 1))
                    last.then_inc(acc_done, 1)

                def turn_x1(f, h):
                    pe.wait_ge(x1_ready, f * TB + h + 1)
                    for k in range(KC):
                        last = nc.tensor.transpose(G[h][:, k * P:(k + 1) * P], x1s[:, h, k * P:(k + 1) * P], ident[:])
                    last.then_inc(x1T_done, 1)

                def scores(b, m, f):
                    if m % 2 == 0:
                        pe.wait_ge(qT_ready, b * 2 + m // 2 + 1)
                        pe.wait_ge(kT_ready, b * 2 + m // 2 + 1)
                    for h in range(TB):
                        for r in range(HPC):
                            if m and h == 0:
                                pe.wait_ge(max_ready, b * HEADS + (m - 1) * HPC + r + 1)
                            rows = slice(DH * r, DH * r + DH)
                            last = nc.tensor.matmul(S[r][:, h * T:(h + 1) * T], qT[rows, m, h * P:(h + 1) * P],
                                                    kT[rows, m, :], start=True, stop=True)
                            if h == TB - 1:
                                last.then_inc(s_done, 1)
                        if f is not None:
                            project(f, m // 2, (m % 2) * 2 + h)

                def turn_max(b, m):
                    pe.wait_ge(nm_ready, b * KC + m + 1)
                    if m:
                        pe.wait_ge(nmT_ready, b * KC + m)
                    for h in range(TB):
                        last = nc.tensor.transpose(NMB[:, (m % 2) * T + h * P:(m % 2) * T + (h + 1) * P],
                                                   nmb[:, h, m, :], identb[:])
                    last.then_inc(nmT_done, 1)

                def scores_t(b, n):
                    m, r = n // HPC, n % HPC
                    if r == 0:
                        pe.wait_ge(nmT_ready, b * KC + m + 1)
                    if m == 0:
                        pe.wait_ge(max_ready, b * HEADS + (KC - 1) * HPC + r + 1)
                    else:
                        pe.wait_ge(exp_ready, b * HEADS + n - HPC + 1)
                    rows = slice(DH * r, DH * r + DH)
                    for kt in range(TB):
                        nc.tensor.matmul(S[r][:, kt * T:(kt + 1) * T], kT[rows, m, kt * P:(kt + 1) * P],
                                         qT[rows, m, :], start=True, stop=False)
                        last = nc.tensor.matmul(S[r][:, kt * T:(kt + 1) * T], onesb[rows, :], nmT[rows, m, :],
                                                start=False, stop=True)
                    last.then_inc(st_done, 1)

                def values(b, m):
                    pe.wait_ge(exp_ready, b * HEADS + (m + 1) * HPC)
                    if m == 1:
                        pe.wait_ge(nmT_ready, b * KC + KC)
                    if m >= 2:
                        pe.wait_ge(oT_ready, b * KC + m - 1)
                    for which in range(2):
                        for kt in range(TB):
                            for r in range(HPC):
                                n = m * HPC + r
                                last = nc.tensor.matmul(A[(m + 1) % 2][DH * r:DH * r + DH, which * T:(which + 1) * T],
                                                        ones[:, 0:DH] if which else v[:, kt, n * DH:(n + 1) * DH],
                                                        pT[:, n % (2 * HPC), kt, :],
                                                        start=(kt == 0), stop=(kt == TB - 1))
                    last.then_inc(pv_done, 1)

                def turn(b, f):
                    if f is not None:
                        pe.wait_ge(x1T_ready, PRIME + f * TB)
                    pe.wait_ge(xr_ready, b * TB + TB)
                    for g in range(2):
                        for k in (2 * g, 2 * g + 1):
                            for h in range(TB):
                                last = nc.tensor.transpose(G[g][:, (k % 2) * T + h * P:(k % 2) * T + (h + 1) * P],
                                                           xr[:, h, k * P:(k + 1) * P], ident[:])
                        last.then_inc(xT_done, 1)
                    pe.wait_ge(xn_act, b + 1)
                    pe.wait_ge(xn_dve, b + 1)
                    for h in range(TB):
                        for s in range(2):
                            for k in range(KC):
                                last = nc.tensor.matmul(S[2 * h + s][:], xnT[:, k, h * P:(h + 1) * P],
                                                        wqkv[:, k, s * D:(s + 1) * D],
                                                        start=(k == 0), stop=(k == KC - 1))
                        last.then_inc(qk_done, 1)
                    if f is not None:
                        pe.wait_ge(oT_ready, f * KC + KC)
                    for h in range(TB):
                        for k in range(KC):
                            last = nc.tensor.matmul(A[h][:], xnT[:, k, h * P:(h + 1) * P], wqkv[:, k, 2 * D:3 * D],
                                                    start=(k == 0), stop=(k == KC - 1))
                        last.then_inc(v_done, 1)
                    pe.wait_ge(qkn_ready, b * TB + TB)
                    for g in range(2):
                        for s, (dst, done) in enumerate(((G[g], qT_done), (A[g], kT_done))):
                            if s:
                                pe.wait_ge(v_ready, b * TB + g + 1)
                            for m in (2 * g, 2 * g + 1):
                                for h in range(TB):
                                    c = (m % 2) * T + h * P
                                    last = nc.tensor.transpose(dst[:, c:c + P],
                                                               qkn[:, h, s * D + m * P:s * D + (m + 1) * P], ident[:])
                            last.then_inc(done, 1)
                    for m in range(KC):
                        scores(b, m, f)
                        if m:
                            turn_max(b, m - 1)
                    for n in range(HEADS + 2):
                        if n < HEADS:
                            scores_t(b, n)
                        if n == 2:
                            turn_max(b, 3)
                        if n % HPC == 1 and n > HPC:
                            values(b, n // HPC - 1)
                        if f is not None:
                            if n in (2, 4):
                                turn_quantised(f, n // 2 - 1)
                            if n in (5, 7):
                                feed(f, (n - 5) // 2)
                            if n in (HEADS - 3, HEADS + 1):
                                turn_x1(f, 0 if n < HEADS else 1)

                turn(0, None)
                with pe.Fori(1, B) as b:
                    turn(b, b - 1)
                for h in range(TB):
                    if h == 0:
                        pe.wait_ge(x1T_ready, PRIME + (B - 1) * TB)
                    for k in range(KC):
                        project(B - 1, h, k)
                for stage in (turn_quantised, feed, turn_x1):
                    for h in range(TB):
                        stage(B - 1, h)

            @block.scalar
            def _(act):
                act.sem_inc(x1T_ready, PRIME)

                def keep_quantised(f, h):
                    act.wait_ge(qnT_done, f * TB + h + 1)
                    nc.scalar.copy(qnT[:, h, :, :], GB16[h][:, 0:D].rearrange("p (k q) -> p k q", k=KC)
                                   ).then_inc(qnT_ready, 1)

                def keep_x1(f, h):
                    act.wait_ge(x1T_done, f * TB + h + 1)
                    nc.scalar.copy(xT[:, :, bass.ds(f * T + h * P, P)],
                                   G[h][:].rearrange("p (k q) -> p k q", k=KC)).then_inc(x1T_ready, 1)

                def keep_max(b, m):
                    act.wait_ge(nmT_done, b * KC + m + 1)
                    nc.scalar.copy(nmT[:, m, :], NMB[:, (m % 2) * T:(m % 2 + 1) * T]).then_inc(nmT_ready, 1)

                def turn(b, f):
                    act.wait_ge(xT_done, b * 2 + 1)
                    for k in range(2):
                        last = nc.scalar.activation(xnT[:, k, :], G[0][:, k * T:(k + 1) * T], ACT.Identity,
                                                    bias=modS[:, k, bass.ds(b, 1)], scale=modG[:, k, bass.ds(b, 1)])
                    last.then_inc(xn_act, 1)
                    for h in range(TB):
                        act.wait_ge(qk_done, b * TB + h + 1)
                        for s in range(2):
                            last = nc.scalar.activation(sq[:, s * D:(s + 1) * D], S[2 * h + s][:], ACT.Square)
                        last.then_inc(sq_ready, 1)
                        act.wait_ge(ss_ready, b * TB + h + 1)
                        nc.scalar.activation(rt[:, h, :], ss[:, h, :], ACT.Sqrt, bias=epsc[:], scale=1.0 / DH
                                             ).then_inc(rt_ready, 1)
                    for h in range(TB):
                        act.wait_ge(v_done, b * TB + h + 1)
                        nc.scalar.copy(v[:, h, :], A[h][:]).then_inc(v_ready, 1)
                    for g in range(2):
                        act.wait_ge(qT_done, b * 2 + g + 1)
                        nc.scalar.activation(qT[:, 2 * g:2 * g + 2, :], G[g][:].rearrange("p (k q) -> p k q", k=2),
                                             ACT.Identity, scale=gcol[:, 0:1]).then_inc(qT_ready, 1)
                    for m in range(KC - 1):
                        keep_max(b, m)
                    for n in range(HEADS):
                        act.wait_ge(st_done, b * HEADS + n + 1)
                        if n >= 2 * HPC and n % HPC == 0:
                            act.wait_ge(pv_done, b * KC + n // HPC - 1)
                        nc.scalar.activation(pT[:, n % (2 * HPC), :, :], S[n % HPC][:].rearrange("p (k q) -> p k q", k=TB),
                                             ACT.Exp).then_inc(exp_ready, 1)
                        if n == 2:
                            keep_max(b, KC - 1)
                        if f is not None and n in (3, 5):
                            keep_quantised(f, (n - 3) // 2)
                        if f is not None and n == HEADS - 1:
                            keep_x1(f, 0)
                    if f is not None:
                        keep_x1(f, 1)

                turn(0, None)
                with act.Fori(1, B) as b:
                    turn(b, b - 1)
                for stage in (keep_quantised, keep_x1):
                    for h in range(TB):
                        stage(B - 1, h)

            @block.vector
            def _(dve):
                def scale(step, h, c):
                    am, z, inv = ys[:, h, c:c + 1], ys[:, h, c + 1:c + 2], ys[:, h, c + 2:c + 3]
                    step(nc.vector.tensor_scalar(z, am, 0.0, None, ALU.is_equal))
                    step(nc.vector.scalar_tensor_tensor(out=am, in0=am, scalar=1.0 / QMAX, in1=z,
                                                        op0=ALU.mult, op1=ALU.add))
                    step(nc.vector.reciprocal(inv, am))
                    return am, inv

                def quantise(f, h, step):
                    dve.wait_ge(y_done, f * TB + h + 1)
                    step(nc.vector.tensor_reduce(ys[:, h, 0:1], G[h][:], AX.X, ALU.max, apply_absolute_value=True))
                    _, inv = scale(step, h, 0)
                    step(nc.vector.tensor_scalar(yq[:, h, :], G[h][:], inv, MAGIC, ALU.mult, ALU.add))
                    nc.vector.tensor_scalar(qn[:, h, :], yq[:, h, :], MAGIC, None, ALU.subtract).then_inc(q_ready, 1)

                def feed_forward(f, h, step):
                    dve.wait_ge(acc_done, f * TB + h + 1)
                    step(nc.vector.scalar_tensor_tensor(out=zt[:, h, :], in0=G[h][:], scalar=ys[:, h, 0:1],
                                                        in1=krow[:], op0=ALU.mult, op1=ALU.mult))
                    step(nc.vector.tensor_tensor(zt[:, h, :], zt[:, h, :], biasrow[:], ALU.add))
                    step(nc.vector.tensor_reduce(ys[:, h, 4:5], zt[:, h, :], AX.X, ALU.max))
                    step(nc.vector.tensor_scalar(ys[:, h, 4:5], ys[:, h, 4:5], 0.0, None, ALU.max))
                    s2, inv2 = scale(step, h, 4)
                    if h == 0:
                        dve.wait_ge(x1_kept, PRIME + f * TB)
                    step(nc.vector.tensor_scalar(zt[:, h, :], zt[:, h, :], 0.0, inv2, ALU.max, ALU.mult))
                    step(nc.vector.tensor_scalar(zt[:, h, :], zt[:, h, :], MAGIC, MAGIC, ALU.add, ALU.subtract))
                    nc.vector.scalar_tensor_tensor(out=x1s[:, h, :], in0=zt[:, h, :], scalar=s2,
                                                   in1=x[:, f * TB + h, :], op0=ALU.mult, op1=ALU.add
                                                   ).then_inc(x1_ready, 1)

                def keep_o(b, m):
                    dve.wait_ge(pv_done, b * KC + m + 1)
                    nc.vector.reciprocal(orc[:, m % 2, :], A[(m + 1) % 2][:, T:2 * T]).then_inc(orc_ready, 1)
                    dve.wait_ge(orc_ready, b * KC + m + 1)
                    nc.vector.tensor_tensor(oT[:, m, :], A[(m + 1) % 2][:, 0:T], orc[:, m % 2, :],
                                            ALU.mult).then_inc(oT_ready, 1)

                def turn(b, f):
                    step = f is not None and Chain(dve, yc, f * YSTEPS)
                    dve.wait_ge(xT_done, b * 2 + 2)
                    for k in (2, 3):
                        last = nc.vector.tensor_scalar(xnT[:, k, :], G[1][:, (k - 2) * T:(k - 1) * T],
                                                       modG[:, k, bass.ds(b, 1)], modS[:, k, bass.ds(b, 1)],
                                                       ALU.mult, ALU.add)
                    last.then_inc(xn_dve, 1)
                    for h in range(TB):
                        dve.wait_ge(sq_ready, b * TB + h + 1)
                        nc.vector.tensor_reduce(ss[:, h, :], sq[:].rearrange("p (n d) -> p n d", d=DH),
                                                AX.X, ALU.add).then_inc(ss_ready, 1)
                        dve.wait_ge(rt_ready, b * TB + h + 1)
                        nc.vector.reciprocal(ri[:, h, :], rt[:, h, :]).then_inc(ri_ready, 1)
                        dve.wait_ge(ri_ready, b * TB + h + 1)
                        for s in range(2):
                            last = nc.vector.tensor_tensor(
                                qkn[:, h, s * D:(s + 1) * D].rearrange("p (n d) -> p n d", d=DH),
                                S[2 * h + s][:].rearrange("p (n d) -> p n d", d=DH),
                                ri[:, h, s * HEADS:(s + 1) * HEADS].unsqueeze(2).broadcast_to([P, HEADS, DH]), ALU.mult)
                        last.then_inc(qkn_ready, 1)
                    for g in range(2):
                        dve.wait_ge(kT_done, b * 2 + g + 1)
                        nc.vector.tensor_scalar(kT[:, 2 * g:2 * g + 2, :], A[g][:].rearrange("p (k q) -> p k q", k=2),
                                                gcol[:, 1:2], None, ALU.mult).then_inc(kT_ready, 1)
                    for n in range(HEADS):
                        dve.wait_ge(s_done, b * HEADS + n + 1)
                        nc.vector.tensor_reduce(nmax[:, n // HPC, :, n % HPC], S[n % HPC][:].rearrange("p (h k) -> p h k", h=TB),
                                                AX.X, ALU.max, negate=True).then_inc(max_ready, 1)
                    if f is not None:
                        quantise(f, 0, step)
                        quantise(f, 1, step)
                    keep_o(b, 0)
                    if f is not None:
                        feed_forward(f, 0, step)
                    keep_o(b, 1)
                    if f is not None:
                        feed_forward(f, 1, step)
                        self.ysteps = step.n
                    keep_o(b, 2)
                    keep_o(b, 3)

                turn(0, None)
                with dve.Fori(1, B) as b:
                    turn(b, b - 1)
                step = Chain(dve, yc, (B - 1) * YSTEPS)
                for stage in (quantise, feed_forward):
                    for h in range(TB):
                        stage(B - 1, h, step)

            @block.gpsimd
            def _(pool):
                pool.sem_inc(x1_kept, PRIME)

                def scale_x(b):
                    for h in range(TB):
                        nc.gpsimd.tensor_tensor(xr[:, h, :], x[:, b * TB + h, :],
                                                rin[:, bass.ds(b * TB + h, 1)].broadcast_to([P, D]), ALU.mult
                                                ).then_inc(xr_ready, 1)

                def keep_x1(f):
                    for h in range(TB):
                        pool.wait_ge(x1_ready, f * TB + h + 1)
                        nc.gpsimd.tensor_copy(x[:, f * TB + h, :], x1s[:, h, :]).then_inc(x1_kept, 1)

                def turn(b, f, last_one=False):
                    if not last_one:
                        pool.wait_ge(xT_done, b * 2 + 2)
                        scale_x(b + 1)
                    for m in range(KC):
                        pool.wait_ge(max_ready, b * HEADS + (m + 1) * HPC)
                        pool.sem_inc(pool_turn, 1)
                        nc.gpsimd.tensor_copy(nmb[:, :, m, 0::DH], nmax[:, m, :, :]).then_inc(hi_ready, 1)
                        pool.wait_ge(hi_ready, 1 + b * KC + m + 1)
                        nc.gpsimd.tensor_tensor(nmb[:, :, m, 1::DH], nmax[:, m, :, :], nmb[:, :, m, 0::DH],
                                                ALU.subtract).then_inc(nm_ready, 1)
                    if f is not None:
                        keep_x1(f)

                nc.gpsimd.memset(nmb[:], 0.0).then_inc(hi_ready, 1)
                scale_x(0)
                pool.wait_ge(hi_ready, 1)
                turn(0, None)
                with pool.Fori(1, B - 1) as b:
                    turn(b, b - 1)
                turn(B - 1, B - 2, last_one=True)
                keep_x1(B - 1)
        assert self.ysteps == YSTEPS, self.ysteps

    def gru(self, ctx):
        nc, io, ident, bank, xT = self.nc, self.io, self.ident, self.bank, self.xT

        def sb(name, shape, dt=F32):
            return ctx.enter_context(nc.sbuf_tensor(name, shape, dt))

        def sem(name):
            return ctx.enter_context(nc.semaphore("g_" + name))

        gi = sb("gi", [P, 2, TC, NG * GB])
        wih, whh = self.w_in, self.whh
        bic = sb("bic", [P, NG * KC])
        bhc = sb("bhc", [P, NG * KC])
        bhn = sb("bhn", [P, KC, B])
        hT = sb("hT", [P, KC, 32])
        fold = sb("fold", [P, GB])
        gh = sb("gh", [P, NG, P])
        rg = sb("rg", [P, GB])
        zg = sb("zg", [P, GB])
        ng = sb("ng", [P, GB])
        t1 = sb("t1", [P, GB])
        t2 = sb("t2", [P, GB])
        dh = sb("dh", [P, GB])
        zd = sb("zd", [P, GB])

        ld = sem("ld")
        bias_ready, gi_done, gi_kept = sem("bias_ready"), sem("gi_done"), sem("gi_kept")
        h_ready, rn_done, z_done, rn_kept, z_kept = (
            sem("h_ready"), sem("rn_done"), sem("z_done"), sem("rn_kept"), sem("z_kept"))
        r_folded, n_folded, z_folded = sem("r_folded"), sem("n_folded"), sem("z_folded")
        r_ready, n_ready, z_ready, t1_ready, t2_ready, dh_ready, zd_ready, h_kept = (
            sem("r_ready"), sem("n_ready"), sem("z_ready"), sem("t1_ready"), sem("t2_ready"), sem("dh_ready"),
            sem("zd_ready"), sem("h_kept"))
        R, Z, NN = 0, 1, 2
        RN, ZB, FR, FN = bank[0], bank[1], bank[2], bank[3]
        FZ = bank[4:6]
        GI = bank[6:8]
        hv = hT[:, :, 0:B]
        NCH = T // TC
        UNITS, SPREAD = NG * KC * KC, TC - 2

        def units(s):
            return range(s * UNITS // SPREAD, min((s + 1) * UNITS // SPREAD, UNITS))

        KEEP_AT = [1 + next(s for s in range(TC) if (g + 1) * KC * KC - 1 in units(s)) for g in range(NG)]

        def cols(t):
            return t[:].rearrange("p (j b) -> p j b", b=B)

        with nc.Block() as block:
            @block.sync
            def _(sp):
                sp.dma_start(bic[:], io["b_ih"]).then_inc(ld, 16)
                sp.dma_start(bhc[:], io["b_hh"]).then_inc(ld, 16)
                sp.dma_start(hT[:, :, 0:B], io["condT"].rearrange("(k p) b -> p k b", p=P)).then_inc(ld, 16)

            @block.tensor
            def _(pe):
                pe.wait_ge(ld, 48)
                pe.wait_ge(bias_ready, 2)
                steps_of = xT[:].rearrange("p k (b t) -> p k b t", t=T)
                w = whh[:].rearrange("p k (g n) -> p k g n", g=NG)

                def input_part(c, p, u):
                    g, j, k = u // (KC * KC), u // KC % KC, u % KC
                    if j == 0 and k == 0:
                        if not isinstance(c, int):
                            pe.wait_ge(gi_kept, c * NG + g - 1)
                        elif c * NG + g >= 2:
                            pe.wait_ge(gi_kept, c * NG + g - 1)
                    last = nc.tensor.matmul(GI[(p + g) % 2][:, j * TC * B:(j + 1) * TC * B],
                                            wih[:, k, (g * KC + j) * P:(g * KC + j + 1) * P],
                                            steps_of[:, k, :, bass.ds(c * TC, TC)],
                                            start=(k == 0), stop=(k == KC - 1))
                    if j == KC - 1 and k == KC - 1:
                        last.then_inc(gi_done, 1)

                def seed_rn(p, s):
                    nc.tensor.matmul(FR[:, 0:GB], ident[:], gi[:, p, s, 0:GB], start=True, stop=False)
                    nc.tensor.matmul(FN[:, 0:GB], ident[:], bhn[:].rearrange("p j b -> p (j b)"),
                                     start=True, stop=False)

                def seed_z(p, s):
                    nc.tensor.matmul(FZ[s % 2][:, 0:GB], ident[:], gi[:, p, s, GB:2 * GB], start=True, stop=False)

                def chunk(c, p, final):
                    for s in range(TC):
                        t = c * TC + s
                        pe.wait_ge(h_ready, t + 1)
                        for k in range(KC):
                            for j in range(KC):
                                last = nc.tensor.matmul(RN[32 * j:32 * j + 32, 0:2 * P], hT[:, k, :],
                                                        w[:, k, 0::2, j * P:(j + 1) * P],
                                                        start=(k == 0), stop=(k == KC - 1))
                        last.then_inc(rn_done, 1)
                        for k in range(KC):
                            if k == 2:
                                pe.wait_ge(rn_kept, t + 1)
                                nc.tensor.matmul(FR[:, 0:GB], gh[:, 0, :], fold[:], start=False, stop=True
                                                 ).then_inc(r_folded, 1)
                                nc.tensor.matmul(FN[:, 0:GB], gh[:, 1, :], fold[:], start=False, stop=True
                                                 ).then_inc(n_folded, 1)
                            for j in range(KC):
                                last = nc.tensor.matmul(ZB[32 * j:32 * j + 32, 0:P], hT[:, k, :],
                                                        w[:, k, Z, j * P:(j + 1) * P],
                                                        start=(k == 0), stop=(k == KC - 1))
                        last.then_inc(z_done, 1)
                        more = s + 1 < TC or not final
                        if more:
                            pe.wait_ge(t1_ready, t + 1)
                            if s + 1 == TC:
                                pe.wait_ge(gi_kept, (c + 2) * NG)
                            seed_rn(*((p, s + 1) if s + 1 < TC else (1 - p, 0)))
                        pe.wait_ge(z_kept, t + 1)
                        nc.tensor.matmul(FZ[s % 2][:, 0:GB], gh[:, 2, :], fold[:], start=False, stop=True
                                         ).then_inc(z_folded, 1)
                        if more:
                            seed_z(*((p, s + 1) if s + 1 < TC else (1 - p, 0)))
                        if not final:
                            for u in units(s):
                                input_part(c + 1, 1 - p, u)

                for u in range(NG * KC * KC):
                    input_part(0, 0, u)
                pe.wait_ge(gi_kept, NG)
                seed_rn(0, 0)
                seed_z(0, 0)
                with pe.Fori(0, NCH // 2 - 1) as cc:
                    chunk(cc * 2, 0, False)
                    chunk(cc * 2 + 1, 1, False)
                chunk(NCH - 2, 0, False)
                chunk(NCH - 1, 1, True)

            @block.scalar
            def _(act):
                with act.Fori(0, NCH) as c:
                    for s in range(TC):
                        t = c * TC + s
                        act.wait_ge(rn_done, t + 1)
                        nc.scalar.copy(gh[:, 0:2, :], RN[:, 0:2 * P].rearrange("p (g c) -> p g c", g=2)
                                       ).then_inc(rn_kept, 1)
                        act.wait_ge(r_folded, t + 1)
                        nc.scalar.activation(rg[:], FR[:, 0:GB], ACT.Tanh, scale=0.5).then_inc(r_ready, 1)
                        act.wait_ge(z_done, t + 1)
                        nc.scalar.copy(gh[:, 2, :], ZB[:, 0:P]).then_inc(z_kept, 1)
                        act.wait_ge(t2_ready, t + 1)
                        nc.scalar.activation(ng[:], t2[:], ACT.Tanh).then_inc(n_ready, 1)
                        act.wait_ge(z_folded, t + 1)
                        nc.scalar.activation(zg[:], FZ[s % 2][:, 0:GB], ACT.Tanh, scale=0.5).then_inc(z_ready, 1)

            @block.vector
            def _(dve):
                dve.wait_ge(ld, 48)
                nc.vector.memset(hT[:, :, B:32], 0.0).then_inc(h_ready, 1)
                nc.vector.tensor_copy(bhn[:], bhc[:, 2 * KC:3 * KC].unsqueeze(2).broadcast_to([P, KC, B]))
                nc.vector.tensor_tensor(bic[:, 0:2 * KC], bic[:, 0:2 * KC], bhc[:, 0:2 * KC], ALU.add
                                        ).then_inc(bias_ready, 1)
                for j in range(KC):
                    last = nc.vector.tensor_copy(fold[:, j * B:(j + 1) * B], ident[:, 32 * j:32 * j + B])
                last.then_inc(bias_ready, 1)
                dve.wait_ge(bias_ready, 2)

                def keep_input(n, p, g):
                    dve.wait_ge(gi_done, n + 1)
                    nc.vector.tensor_tensor(
                        gi[:, p, :, g * GB:(g + 1) * GB].rearrange("p t (j b) -> p j b t", b=B),
                        GI[(p + g) % 2][:].rearrange("p (j b t) -> p j b t", b=B, t=TC)[:, 0:KC],
                        bic[:, g * KC:(g + 1) * KC].unsqueeze(2).unsqueeze(3).broadcast_to([P, KC, B, TC]),
                        ALU.add).then_inc(gi_kept, 1)

                def chunk(c, p, final):
                    dve.wait_ge(gi_kept, (c + 1) * NG)
                    for s in range(TC):
                        t = c * TC + s
                        if not final and s in KEEP_AT:
                            g = KEEP_AT.index(s)
                            keep_input((c + 1) * NG + g, 1 - p, g)
                        dve.wait_ge(r_ready, t + 1)
                        dve.wait_ge(n_folded, t + 1)
                        nc.vector.scalar_tensor_tensor(out=t1[:], in0=rg[:], scalar=1.0, in1=FN[:, 0:GB],
                                                       op0=ALU.add, op1=ALU.mult).then_inc(t1_ready, 1)
                        dve.wait_ge(t1_ready, t + 1)
                        nc.vector.scalar_tensor_tensor(out=t2[:], in0=t1[:], scalar=0.5,
                                                       in1=gi[:, p, s, 2 * GB:3 * GB],
                                                       op0=ALU.mult, op1=ALU.add).then_inc(t2_ready, 1)
                        dve.wait_ge(n_ready, t + 1)
                        nc.vector.tensor_tensor(cols(dh), hv, cols(ng), ALU.subtract).then_inc(dh_ready, 1)
                        dve.wait_ge(dh_ready, t + 1)
                        dve.wait_ge(z_ready, t + 1)
                        nc.vector.scalar_tensor_tensor(out=zd[:], in0=zg[:], scalar=1.0, in1=dh[:],
                                                       op0=ALU.add, op1=ALU.mult).then_inc(zd_ready, 1)
                        dve.wait_ge(h_kept, PRIME + t)
                        dve.wait_ge(zd_ready, t + 1)
                        nc.vector.scalar_tensor_tensor(out=hv, in0=cols(zd), scalar=0.5, in1=cols(ng),
                                                       op0=ALU.mult, op1=ALU.add).then_inc(h_ready, 1)

                for g in range(NG):
                    keep_input(g, 0, g)
                with dve.Fori(0, NCH // 2 - 1) as cc:
                    chunk(cc * 2, 0, False)
                    chunk(cc * 2 + 1, 1, False)
                chunk(NCH - 2, 0, False)
                chunk(NCH - 1, 1, True)

            @block.gpsimd
            def _(pool):
                hseq = xT[:].rearrange("p k (b t) -> p k b t", t=T)
                pool.sem_inc(h_kept, PRIME)
                with pool.Fori(0, T) as t:
                    pool.wait_ge(h_ready, t + 2)
                    nc.gpsimd.tensor_copy(hseq[:, :, :, t], hv).then_inc(h_kept, 1)

    def router(self, ctx):
        nc, io, x, ident, ones, bank, hT = self.nc, self.io, self.x, self.ident, self.ones, self.bank, self.xT

        def sb(name, shape, dt=F32):
            return ctx.enter_context(nc.sbuf_tensor(name, shape, dt))

        def sem(name):
            return ctx.enter_context(nc.semaphore("r_" + name))

        wr = sb("wr", [P, KC, E])
        shgu = sb("shgu", [P, 2, KC, I])
        shd = sb("shd", [IH, 2, D])
        ebias = sb("ebias", [P, E])
        before = sb("before", [P, P], BF16)
        onesb = sb("onesb", [P, P], BF16)
        slot0 = sb("slot0", [P, E])
        tokid = sb("tokid", [P, NT], I32)
        spare = sb("spare", [P, TOPK])
        zero = sb("zero", [P, 2, D + E])
        blank = sb("blank", [E, CAP], I32)
        hs = sb("hs", [P, KC, P])
        rows = sb("rows", [P, D + E])
        sig = sb("sig", [P, I])
        gs = sb("gs", [P, I])
        act_h = sb("act_h", [P, I])
        hTs = sb("hTs", [IH, 2, P])
        sco = sb("sco", [P, E])
        sc = sb("sc", [P, E])
        top2 = sb("top2", [P, NGRP, 8])
        gsc = sb("gsc", [P, NGRP + 4])
        gtop = sb("gtop", [P, 8])
        grep = sb("grep", [P, 16])
        gpick = sb("gpick", [P, 8])
        gmask = sb("gmask", [P, NGRP])
        mk = sb("mk", [P, E])
        top8 = sb("top8", [P, 8])
        taken = sb("taken", [P, E])
        sel = sb("sel", [P, E], BF16)
        count = sb("count", [P, E], BF16)
        wsum = sb("wsum", [P, 2])
        w = sb("w", [P, E])
        fits = sb("fits", [P, E])
        slot = sb("slot", [P, E])
        key = sb("key", [P, E])
        key8 = sb("key8", [P, 8])
        dest = sb("dest", [P, 8])
        desti = sb("desti", [P, 8], I32)
        entry = sb("entry", [P, 1], I32)

        ld, c_ready, k_ready = sem("ld"), sem("c_ready"), sem("k_ready")
        blank_ready, blank_out = sem("blank_ready"), sem("blank_out")
        staged, gu_done, sig_ready, act_ready, hT_done, hT_ready, dn_done, sum_ready = (
            sem("staged"), sem("gu_done"), sem("sig_ready"), sem("act_ready"), sem("hT_done"), sem("hT_ready"),
            sem("dn_done"), sem("sum_ready"))
        lg_done, sco_ready, sel_ready, pos_done, chain, row_done, row_ready, row_out = (
            sem("lg_done"), sem("sco_ready"), sem("sel_ready"), sem("pos_done"), sem("chain"), sem("row_done"),
            sem("row_ready"), sem("row_out"))
        sco_used, w_ready = sem("sco_used"), sem("w_ready")
        entry_ready, scattered, dchain = sem("entry_ready"), sem("scattered"), sem("dchain")
        acc_out, pool_turn, dve_turn = sem("acc_out"), sem("pool_turn"), sem("dve_turn")
        LG, GU, RW, HT, DN, PS = bank[0], bank[1], bank[2], bank[3], bank[4], bank[5]
        CSTEPS = 20
        with nc.Block() as block:
            @block.sync
            def _(sp):
                sp.dma_start(wr[:], io["routerT"].rearrange("(k p) e -> p k e", p=P)).then_inc(ld, 16)
                for a, n in enumerate(("sh_gate", "sh_up")):
                    sp.dma_start(shgu[:, a], io[n].rearrange("(k p) i -> p k i", p=P)).then_inc(ld, 16)
                sp.dma_start(shd[:], io["sh_down"].rearrange("(p c) d -> p c d", c=2)).then_inc(ld, 16)
                sp.dma_start(ebias[:], io["e_bias"].partition_broadcast(P)).then_inc(ld, 16)
                sp.wait_ge(blank_ready, 1)
                sp.dma_start(self.hs_rows[N:N + CAP, :].rearrange("(c p) d -> p c d", p=P),
                             zero[:]).then_inc(blank_out, 16)
                sp.sem_inc(row_out, PRIME_DMA)
                with sp.Fori(0, NT) as i:
                    sp.wait_ge(row_ready, i + 1)
                    sp.wait_ge(w_ready, i + 1)
                    sp.dma_start(self.hs_rows[bass.ds(i * P, P), :], rows[:]).then_inc(row_out, 16)
                    sp.wait_ge(sum_ready, i + 1)
                    sp.dma_start(self.acc_rows[bass.ds(i * P, P), :], x[:, bass.ds(i, 1), :].rearrange("p t d -> p (t d)")
                                 ).then_inc(acc_out, 16)
                sp.wait_ge(acc_out, 16 * NT)
                sp.wait_ge(row_out, PRIME_DMA + 16 * NT)
                sp.wait_ge(blank_out, 16)

            @block.gpsimd
            def _(pool):
                nc.gpsimd.memset(zero[:], 0.0)
                nc.gpsimd.memset(onesb[:], 1.0).then_inc(c_ready, 1)
                nc.gpsimd.memset(before[:], 1.0).then_inc(c_ready, 1)
                nc.gpsimd.iota(tokid[:], pattern=[[P, NT]], base=0, channel_multiplier=1).then_inc(c_ready, 1)
                nc.gpsimd.iota(slot0[:], pattern=[[-CAP, E]], base=int(KEY0), channel_multiplier=0,
                               allow_small_or_imprecise_dtypes=True).then_inc(c_ready, 1)
                nc.gpsimd.iota(spare[:], pattern=[[P, TOPK]], base=SLOTS, channel_multiplier=1,
                               allow_small_or_imprecise_dtypes=True).then_inc(c_ready, 1)
                pool.wait_ge(c_ready, 5)
                nc.gpsimd.iota(blank[:], pattern=[[1, CAP]], base=N, channel_multiplier=0).then_inc(blank_ready, 1)
                nc.gpsimd.affine_select(out=before[:], in_=before[:], compare_op=ALU.is_gt, fill=0.0, base=0,
                                        pattern=[[1, P]], channel_multiplier=-1).then_inc(c_ready, 1)
                pool.wait_ge(blank_ready, 1)
                nc.gpsimd.dma_start(self.table[0:SLOTS, :].rearrange("(e s) w -> e (s w)", e=E), blank[:]
                                    ).then_inc(scattered, 16)
                pool.wait_ge(scattered, PRIME_DMA)
                with pool.Fori(0, NT) as i:
                    pool.wait_ge(entry_ready, i + 1)
                    pool.sem_inc(pool_turn, 1)
                    for c in range(TOPK):
                        nc.gpsimd.indirect_dma_start(
                            self.table, bass.IndirectOffsetOnAxis(desti[:, c:c + 1].bitcast(U32), 0),
                            entry[:], None).then_inc(scattered, 16)
                pool.wait_ge(scattered, PRIME_DMA + 16 * TOPK * NT)

            @block.tensor
            def _(pe):
                pe.wait_ge(ld, 80)
                pe.wait_ge(c_ready, 6)

                def logits(i):
                    pe.wait_ge(staged, i + 1)
                    for k in range(KC):
                        last = nc.tensor.matmul(LG[:, 0:E], hs[:, k, :], wr[:, k, :], start=(k == 0), stop=(k == KC - 1))
                    last.then_inc(lg_done, 1)

                def turn_rows(i):
                    for k in range(KC):
                        last = nc.tensor.transpose(RW[:, k * P:(k + 1) * P], hs[:, k, :], ident[:])
                    last.then_inc(row_done, 1)

                def shared(i):
                    for k in range(KC):
                        last = nc.tensor.matmul(GU[:, 0:2 * I], hs[:, k, :], shgu[:, :, k, :],
                                                start=(k == 0), stop=(k == KC - 1))
                    last.then_inc(gu_done, 1)

                def tile(i, last_one):
                    pe.wait_ge(sel_ready, i + 1)
                    nc.tensor.matmul(PS[:, 0:E], before[:], sel[:], start=True, stop=False)
                    nc.tensor.matmul(PS[:, 0:E], onesb[:], count[:], start=False, stop=True).then_inc(pos_done, 1)
                    pe.wait_ge(act_ready, i + 1)
                    for c in range(2):
                        last = nc.tensor.transpose(HT[0:IH, c * P:(c + 1) * P], act_h[:, c::2], ident[:])
                    last.then_inc(hT_done, 1)
                    if not last_one:
                        logits(i + 1)
                        pe.wait_ge(row_ready, i + 1)
                        turn_rows(i + 1)
                    pe.wait_ge(hT_ready, i + 1)
                    for c in range(2):
                        last = nc.tensor.matmul(DN[:], hTs[:, c, :], shd[:, c, :], start=(c == 0), stop=(c == 1))
                    last.then_inc(dn_done, 1)
                    if not last_one:
                        shared(i + 1)

                logits(0)
                turn_rows(0)
                shared(0)
                with pe.Fori(0, NT - 1) as i:
                    tile(i, False)
                tile(NT - 1, True)

            @block.scalar
            def _(act):
                def stage(i):
                    nc.scalar.copy(hs[:], hT[:, :, bass.ds(i * P, P)]).then_inc(staged, 1)

                def tile(i, last_one):
                    act.wait_ge(lg_done, i + 1)
                    act.wait_ge(sco_used, PRIME + i)
                    nc.scalar.activation(sco[:], LG[:, 0:E], ACT.Sigmoid).then_inc(sco_ready, 1)
                    act.wait_ge(row_done, i + 1)
                    act.wait_ge(row_out, PRIME_DMA + i * 16)
                    nc.scalar.copy(rows[:, 0:D], RW[:]).then_inc(row_ready, 1)
                    act.wait_ge(gu_done, i + 1)
                    nc.scalar.activation(sig[:], GU[:, 0:I], ACT.Sigmoid).then_inc(sig_ready, 1)
                    if not last_one:
                        stage(i + 1)
                    act.wait_ge(hT_done, i + 1)
                    nc.scalar.copy(hTs[:], HT[0:IH, 0:2 * P].rearrange("p (c q) -> p c q", c=2)).then_inc(hT_ready, 1)

                act.sem_inc(sco_used, PRIME)
                stage(0)
                with act.Fori(0, NT - 1) as i:
                    tile(i, False)
                tile(NT - 1, True)

            @block.vector
            def _(dve):
                first = Chain(dve, dchain)
                first(nc.vector.memset(count[:], 0.0))
                first(nc.vector.memset(gsc[:, NGRP:NGRP + 4], TAKEN))
                first(nc.vector.memset(gpick[:, TOPG:8], TAKEN))
                dve.wait_ge(ld, 80)
                dve.wait_ge(c_ready, 6)
                with dve.Fori(0, NT) as i:
                    step = Chain(dve, chain, i * CSTEPS)
                    dve.wait_ge(sco_ready, i + 1)
                    step(nc.vector.tensor_tensor(sc[:], sco[:], ebias[:], ALU.add))
                    dve.sem_inc(dve_turn, 1)
                    for g in range(NGRP):
                        last = nc.vector.max(top2[:, g, :], sc[:, g * GSZ:(g + 1) * GSZ])
                    step(last)
                    step(nc.vector.tensor_tensor(gsc[:, 0:NGRP], top2[:, :, 0], top2[:, :, 1], ALU.add))
                    dve.sem_inc(dve_turn, 1)
                    step(nc.vector.max(gtop[:], gsc[:, 0:NGRP]))
                    step(nc.vector.tensor_copy(gpick[:, 0:TOPG], gtop[:, 0:TOPG]))
                    dve.sem_inc(dve_turn, 1)
                    step(nc.vector.match_replace(grep[:, 0:NGRP + 4], gpick[:], gsc[:], -2.0 * TAKEN))
                    step(nc.vector.tensor_scalar(gmask[:], grep[:, 0:NGRP], -2.0 * TAKEN, None, ALU.is_equal))
                    step(nc.vector.tensor_tensor(mk[:].rearrange("p (g s) -> p g s", s=GSZ),
                                                 sc[:].rearrange("p (g s) -> p g s", s=GSZ),
                                                 gmask[:].unsqueeze(2).broadcast_to([P, NGRP, GSZ]), ALU.mult))
                    dve.sem_inc(dve_turn, 1)
                    step(nc.vector.max(top8[:], mk[:]))
                    dve.sem_inc(dve_turn, 1)
                    step(nc.vector.match_replace(taken[:], top8[:], mk[:], TAKEN))
                    nc.vector.tensor_scalar(sel[:], taken[:], TAKEN, None, ALU.is_equal).then_inc(sel_ready, 1)
                    step(nc.vector.scalar_tensor_tensor(out=w[:], in0=taken[:], scalar=TAKEN, in1=sco[:],
                                                        op0=ALU.is_equal, op1=ALU.mult, accum_out=wsum[:, 0:1]))
                    dve.sem_inc(sco_used, 1)
                    step(nc.vector.tensor_scalar(wsum[:, 0:1], wsum[:, 0:1], 1e-20, None, ALU.add))
                    step(nc.vector.reciprocal(wsum[:, 1:2], wsum[:, 0:1]))
                    step(nc.vector.tensor_scalar(w[:], w[:], wsum[:, 1:2], ROUTE_SCALE, ALU.mult, ALU.mult))
                    dve.wait_ge(sig_ready, i + 1)
                    step(nc.vector.tensor_tensor(gs[:], GU[:, 0:I], sig[:], ALU.mult))
                    nc.vector.tensor_tensor(act_h[:], GU[:, I:2 * I], gs[:], ALU.mult).then_inc(act_ready, 1)
                    dve.wait_ge(pos_done, i + 1)
                    nc.vector.scalar_tensor_tensor(out=fits[:], in0=PS[:, 0:E], scalar=float(CAP), in1=sel[:],
                                                   op0=ALU.is_lt, op1=ALU.mult)
                    step(nc.vector.tensor_tensor(slot[:], slot0[:], PS[:, 0:E], ALU.subtract))
                    nc.vector.tensor_tensor(count[:], count[:], sel[:], ALU.add)
                    step(nc.vector.tensor_tensor(key[:], slot[:], fits[:], ALU.mult))
                    dve.sem_inc(dve_turn, 1)
                    step(nc.vector.max(key8[:], key[:]))
                    step(nc.vector.tensor_scalar(dest[:], key8[:], -1.0, KEY0, ALU.mult, ALU.add))
                    step(nc.vector.tensor_tensor(dest[:], dest[:], spare[:], ALU.min))
                    dve.wait_ge(scattered, PRIME_DMA + i * 16 * TOPK)
                    nc.vector.tensor_copy(desti[:], dest[:])
                    nc.vector.tensor_copy(entry[:], tokid[:, bass.ds(i, 1)]).then_inc(entry_ready, 1)
                    dve.wait_ge(row_out, PRIME_DMA + i * 16)
                    nc.vector.tensor_tensor(rows[:, D:D + E], w[:], fits[:], ALU.mult).then_inc(w_ready, 1)
                    dve.wait_ge(dn_done, i + 1)
                    nc.vector.tensor_tensor(x[:, i, :], x[:, i, :], DN[:], ALU.add).then_inc(sum_ready, 1)
                    self.csteps = step.n
        assert self.csteps == CSTEPS, self.csteps

    def experts(self, ctx):
        nc, io, ident, bank = self.nc, self.io, self.ident, self.bank

        def sb(name, shape, dt=F32):
            return ctx.enter_context(nc.sbuf_tensor(name, shape, dt))

        def sem(name):
            return ctx.enter_context(nc.semaphore("e_" + name))

        wgu = [sb(f"wgu{s}", [P, 2, KC, I]) for s in range(2)]
        wdn = [sb(f"wdn{s}", [IH, 2, D]) for s in range(2)]
        tab = sb("tab", [P, P], I32)
        tabf = sb("tabf", [P, P])
        slot_tok = sb("slot_tok", [P, NU], I32)
        slot_w = sb("slot_w", [P, NU])
        idx = [sb(f"idx{h}", [P, 1], I32) for h in range(2)]
        idy = [sb(f"idy{h}", [P, 1], I32) for h in range(2)]
        xg = [sb(f"xg{h}", [P, D + E]) for h in range(2)]
        xgT = sb("xgT", [P, 2, KC, P])
        sig = sb("sig_e", [P, 2, I])
        gs = sb("gs_e", [P, 2, I])
        ah = sb("ah", [P, 2, I])
        ahT = sb("ahT", [IH, 2, 2, P])
        y = [sb(f"y{h}", [P, D]) for h in range(2)]

        tab_ld, tab_f, tab_T, tab_ready = sem("tab_ld"), sem("tab_f"), sem("tab_T"), sem("tab_ready")
        w_ld = [sem("w_ld0"), sem("w_ld1")]
        idx_ready, gathered, idy_ready, added = (sem("idx_ready"), [sem("gathered0"), sem("gathered1")],
                                                 sem("idy_ready"), [sem("added0"), sem("added1")])
        xT_done, xT_ready, gu_done, sig_ready, gs_ready, ah_ready, ahT_done, ahT_ready, y_done, y_ready = (
            sem("xT_done"), sem("xT_ready"), sem("gu_done"), sem("sig_ready"), sem("gs_ready"), sem("ah_ready"),
            sem("ahT_done"), sem("ahT_ready"), sem("y_done"), sem("y_ready"))
        out_done, pool_turn, cleared, w_kept = sem("out_done"), sem("pool_turn"), sem("cleared"), sem("w_kept")
        XT, GU, HT, DN = bank[0:2], bank[2:4], bank[4:6], bank[6:8]

        def load(eng, e, s):
            for a, n in enumerate(("w_gate", "w_up")):
                eng.dma_start(wgu[s][:, a], io[n][e].rearrange("(p k) i -> p k i", k=KC)).then_inc(w_ld[s], 16)
            eng.dma_start(wdn[s][:], io["w_down"][e].rearrange("(p c) d -> p c d", c=2)).then_inc(w_ld[s], 16)

        with nc.Block() as block:
            @block.sync
            def _(sp):
                sp.dma_start(tab[:], self.table[0:SLOTS, :].rearrange("(c p) w -> c (p w)", p=P)).then_inc(tab_ld, 16)
                load(sp, 0, 0)
                load(sp, 1, 1)
                with sp.Fori(0, E // 2 - 1) as ee:
                    for s in range(2):
                        sp.wait_ge(y_done, (ee * 2 + s) * 2 + 2)
                        for a, n in enumerate(("w_gate", "w_up")):
                            sp.dma_start(wgu[s][:, a], io[n][bass.ds(ee * 2 + 2 + s, 1)].rearrange("e (p k) i -> p (e k) i", k=KC)
                                         ).then_inc(w_ld[s], 16)
                        sp.dma_start(wdn[s][:], io["w_down"][bass.ds(ee * 2 + 2 + s, 1)].rearrange("e (p c) d -> p (e c) d", c=2)
                                     ).then_inc(w_ld[s], 16)
                for h in range(2):
                    sp.wait_ge(added[h], PRIME_DMA + 16 * E)
                sp.dma_start(self.out, self.acc_rows[0:N, :]).then_inc(out_done, 16)
                sp.wait_ge(out_done, 16)

            @block.gpsimd
            def _(pool):
                pool.wait_ge(tab_ready, 1)

                def gather(u, h):
                    nc.gpsimd.tensor_copy(idx[h][:], slot_tok[:, bass.ds(u, 1)]).then_inc(idx_ready, 1)
                    pool.wait_ge(idx_ready, u + 1)
                    pool.sem_inc(pool_turn, 1)
                    nc.gpsimd.indirect_dma_start(xg[h][:], None, self.hs_rows,
                                                 bass.IndirectOffsetOnAxis(idx[h][:].bitcast(U32), 0)
                                                 ).then_inc(gathered[h], 16)

                def add_rows(u, e, h):
                    pool.wait_ge(added[h], PRIME_DMA + e * 16)
                    nc.gpsimd.tensor_copy(idy[h][:], slot_tok[:, bass.ds(u, 1)]).then_inc(idy_ready, 1)
                    pool.wait_ge(idy_ready, u + 1)
                    pool.wait_ge(y_ready, u + 1)
                    if h == 0:
                        pool.wait_ge(added[1], PRIME_DMA + e * 16)
                    pool.sem_inc(pool_turn, 1)
                    nc.gpsimd.indirect_dma_start(self.acc_rows, bass.IndirectOffsetOnAxis(idy[h][:].bitcast(U32), 0),
                                                 y[h][:], None, compute_op=ALU.add).then_inc(added[h], 16)

                for h in range(2):
                    nc.gpsimd.memset(y[h][:], 0.0).then_inc(cleared, 1)
                    pool.wait_ge(cleared, h + 1)
                    nc.gpsimd.dma_start(self.acc_rows[N + h * P:N + (h + 1) * P, :], y[h][:]).then_inc(added[h], 16)
                    gather(h, h)
                for h in range(2):
                    pool.wait_ge(w_kept, h + 1)
                    gather(2 + h, h)
                with pool.Fori(0, E - 2) as e:
                    for h in range(2):
                        pool.wait_ge(w_kept, e * 2 + 2 + h + 1)
                        gather(e * 2 + 4 + h, h)
                        add_rows(e * 2 + h, e, h)
                for e in (E - 2, E - 1):
                    for h in range(2):
                        add_rows(e * 2 + h, e, h)

            @block.tensor
            def _(pe):
                pe.wait_ge(tab_f, 1)
                nc.tensor.transpose(bank[0][:, 0:P], tabf[:], ident[:]).then_inc(tab_T, 1)
                pe.wait_ge(tab_ready, 1)

                def turn_x(e, h):
                    pe.wait_ge(gathered[h], e * 16 + 16)
                    for k in range(KC):
                        last = nc.tensor.transpose(XT[h][:, k * P:(k + 1) * P], xg[h][:, k:D:KC], ident[:])
                    last.then_inc(xT_done, 1)

                def expert(e, s, wl, last_one):
                    pe.wait_ge(w_ld[s], wl)
                    for h in range(2):
                        pe.wait_ge(xT_ready, e * 2 + h + 1)
                        for k in range(KC):
                            last = nc.tensor.matmul(GU[h][:, 0:2 * I], xgT[:, h, k, :], wgu[s][:, :, k, :],
                                                    start=(k == 0), stop=(k == KC - 1))
                        last.then_inc(gu_done, 1)
                    def turn_inner(h):
                        pe.wait_ge(ah_ready, e * 2 + h + 1)
                        for c in range(2):
                            last = nc.tensor.transpose(HT[h][0:IH, c * P:(c + 1) * P], ah[:, h, c::2], ident[:])
                        last.then_inc(ahT_done, 1)

                    def down(h):
                        pe.wait_ge(ahT_ready, e * 2 + h + 1)
                        for c in range(2):
                            last = nc.tensor.matmul(DN[h][:], ahT[:, h, c, :], wdn[s][:, c, :],
                                                    start=(c == 0), stop=(c == 1))
                        last.then_inc(y_done, 1)

                    turn_inner(0)
                    if not last_one:
                        turn_x(e + 1, 0)
                    turn_inner(1)
                    down(0)
                    if not last_one:
                        turn_x(e + 1, 1)
                    down(1)

                for h in range(2):
                    turn_x(0, h)
                with pe.Fori(0, E // 2 - 1) as ee:
                    for s in range(2):
                        expert(ee * 2 + s, s, ee * 48 + 48, False)
                expert(E - 2, 0, 24 * E, False)
                expert(E - 1, 1, 24 * E, True)

            @block.scalar
            def _(act):
                def keep_x(e, h):
                    act.wait_ge(xT_done, e * 2 + h + 1)
                    nc.scalar.copy(xgT[:, h, :, :], XT[h][:].rearrange("p (k q) -> p k q", k=KC)).then_inc(xT_ready, 1)
                    nc.scalar.copy(slot_w[:, bass.ds(e * 2 + h, 1)], xg[h][:, bass.ds(e + D, 1)]).then_inc(w_kept, 1)

                def expert(e, last_one):
                    for h in range(2):
                        act.wait_ge(gu_done, e * 2 + h + 1)
                        nc.scalar.activation(sig[:, h, :], GU[h][:, 0:I], ACT.Sigmoid).then_inc(sig_ready, 1)
                    def keep_inner(h):
                        act.wait_ge(ahT_done, e * 2 + h + 1)
                        nc.scalar.copy(ahT[:, h, :, :], HT[h][0:IH, 0:2 * P].rearrange("p (c q) -> p c q", c=2)
                                       ).then_inc(ahT_ready, 1)

                    keep_inner(0)
                    keep_inner(1)
                    if not last_one:
                        keep_x(e + 1, 0)
                        keep_x(e + 1, 1)

                for h in range(2):
                    keep_x(0, h)
                with act.Fori(0, E - 1) as e:
                    expert(e, False)
                expert(E - 1, True)

            @block.vector
            def _(dve):
                dve.wait_ge(tab_ld, 16)
                nc.vector.tensor_copy(tabf[:], tab[:]).then_inc(tab_f, 1)
                dve.wait_ge(tab_T, 1)
                nc.vector.tensor_copy(slot_tok[:], bank[0][:, 0:P]).then_inc(tab_ready, 1)

                with dve.Fori(0, E) as e:
                    for h in range(2):
                        u = e * 2 + h
                        dve.wait_ge(sig_ready, u + 1)
                        nc.vector.tensor_tensor(gs[:, h, :], GU[h][:, 0:I], sig[:, h, :], ALU.mult).then_inc(gs_ready, 1)
                        dve.wait_ge(gs_ready, u + 1)
                        nc.vector.tensor_tensor(ah[:, h, :], GU[h][:, I:2 * I], gs[:, h, :], ALU.mult
                                                ).then_inc(ah_ready, 1)
                    for h in range(2):
                        u = e * 2 + h
                        dve.wait_ge(w_kept, u + 1)
                        dve.wait_ge(y_done, u + 1)
                        dve.wait_ge(added[h], PRIME_DMA + e * 16)
                        nc.vector.tensor_scalar(y[h][:], DN[h][:], slot_w[:, bass.ds(u, 1)], None, ALU.mult
                                                ).then_inc(y_ready, 1)


_DIRECT = {"W_emb": "L0_cond_W_emb", "W_qkv": "L0_cond_W_qkv", "W_out": "L0_cond_W_out", "kernel": "L0_ffn_kernel",
           "ffn_bias": "L0_ffn_bias", "W_ih": "L1_cond_W_ih", "W_hh": "L1_cond_W_hh", "e_bias": "L1_ffn_e_bias",
           "w_gate": "L1_ffn_w_gate", "w_up": "L1_ffn_w_up", "w_down": "L1_ffn_w_down",
           "sh_gate": "L1_ffn_sh_gate", "sh_up": "L1_ffn_sh_up", "sh_down": "L1_ffn_sh_down"}


def lay_out(inputs):
    import numpy as np

    def chunks(v):
        return np.ascontiguousarray(np.asarray(v).reshape(-1, P).T)

    a = {k: np.ascontiguousarray(inputs[n]) for k, n in _DIRECT.items()}
    a["x"] = np.ascontiguousarray(inputs["x"]).reshape(N, D)
    a["condT"] = np.ascontiguousarray(np.asarray(inputs["cond_2048"]).T)
    a["b_emb"] = chunks(inputs["L0_cond_b_emb"])
    a["g_norm"] = chunks(inputs["L0_cond_g_norm"])
    a["g_q"] = np.ascontiguousarray(inputs["L0_cond_g_q"]).reshape(DH, 1)
    a["g_k"] = np.ascontiguousarray(inputs["L0_cond_g_k"]).reshape(DH, 1)
    a["kernelT"] = np.ascontiguousarray(np.asarray(inputs["L0_ffn_kernel"]).T)
    a["b_ih"] = chunks(inputs["L1_cond_b_ih"])
    a["b_hh"] = chunks(inputs["L1_cond_b_hh"])
    a["routerT"] = np.ascontiguousarray(np.asarray(inputs["L1_ffn_router_weight"]).T)
    return a


def program(nc, shapes):
    io = {n: nc.dram_tensor("in_" + n, s, dt, kind="ExternalInput").ap() for n, (s, dt) in shapes.items()}
    out = nc.dram_tensor("out_rows", [N, D], F32, kind="ExternalOutput").ap()
    Kernel(nc, io, out).build()


def kernel(**inputs):
    import numpy as np
    import concourse.bacc as bacc
    from concourse.bass_utils import run_bass_kernel_spmd

    arrays = lay_out(inputs)
    nc = bacc.Bacc("TRN2", target_bir_lowering=False, num_devices=1)
    program(nc, {n: (a.shape, mybir.dt.from_np(a.dtype)) for n, a in arrays.items()})
    r = run_bass_kernel_spmd(nc, [{"in_" + n: a for n, a in arrays.items()}], core_ids=[0])
    return np.asarray(r.results[0]["out_rows"]).reshape(B, T, D)
```

```python
from contextlib import ExitStack

import concourse.bass as bass
from concourse import mybir

P = 128
F32 = mybir.dt.float32
BF16 = mybir.dt.bfloat16
I32 = mybir.dt.int32
U32 = mybir.dt.uint32
ALU = mybir.AluOpType
ACT = mybir.ActivationFunctionType
AX = mybir.AxisListType

B, T, D = 8, 256, 512
N = B * T
KC = D // P
NT = N // P
TB = T // P
HEADS = 16
DH = D // HEADS
HPC = P // DH
NG = 3
TC = 16
GB = KC * B
E, I = 64, 176
IH = I // 2
NGRP, GSZ, TOPG, TOPK = 8, 8, 4, 8
CAP = 256
SLOTS = E * CAP
NU = SLOTS // P
ROUTE_SCALE = 2.5
QMAX = 127.0
MAGIC = 12582912.0
RMS_EPS = 1e-6
TAKEN = -1e30
KEY0 = 32768.0


class Chain:

    def __init__(self, eng, sem, base=0):
        self.eng, self.sem, self.base, self.n = eng, sem, base, 0

    def __call__(self, ins):
        self.n += 1
        ins.then_inc(self.sem, 1)
        self.eng.wait_ge(self.sem, self.base + self.n)


PRIME = 1
PRIME_DMA = 16


class Kernel:
    def __init__(self, nc, io, out):
        self.nc, self.io, self.out = nc, io, out
        self.hs_rows = nc.dram_tensor("hs_rows", [N + CAP, D + E], F32, kind="Internal").ap()
        self.acc_rows = nc.dram_tensor("acc_rows", [N + CAP, D], F32, kind="Internal").ap()
        self.table = nc.dram_tensor("slot_table", [SLOTS + 2 * TOPK * P, 1], I32, kind="Internal").ap()

    def build(self):
        with ExitStack() as ctx:
            nc = self.nc
            self.x = ctx.enter_context(nc.sbuf_tensor("x", [P, NT, D], F32))
            self.ident = ctx.enter_context(nc.sbuf_tensor("ident", [P, P], F32))
            self.ones = ctx.enter_context(nc.sbuf_tensor("ones", [P, P], F32))
            self.bank = [ctx.enter_context(nc.psum_tensor(f"bank{i}", [P, 512], F32)) for i in range(8)]
            self.xT = ctx.enter_context(nc.sbuf_tensor("xT", [P, KC, N], F32))
            with ExitStack() as c01:
                self.w_in = c01.enter_context(nc.sbuf_tensor("w_in", [P, KC, 3 * D], F32))
                self.whh = c01.enter_context(nc.sbuf_tensor("whh", [P, KC, NG * D], F32))
                with ExitStack() as c0:
                    self.layer0(c0)
                with ExitStack() as c1:
                    self.gru(c1)
            with ExitStack() as c2:
                self.router(c2)
            with ExitStack() as c3:
                self.experts(c3)

    def layer0(self, ctx):
        nc, io, x, ident, ones, bank, xT = self.nc, self.io, self.x, self.ident, self.ones, self.bank, self.xT

        def sb(name, shape, dt=F32):
            return ctx.enter_context(nc.sbuf_tensor(name, shape, dt))

        def sem(name):
            return ctx.enter_context(nc.semaphore("a_" + name))

        identb = sb("identb", [P, P], BF16)
        onesb = sb("ones_bf16", [P, P], BF16)
        gcol = sb("gcol", [P, 2])
        wqkv = self.w_in
        wout = sb("wout", [P, KC, D])
        biasrow = sb("biasrow", [P, D])
        modG = sb("modG", [P, KC, B])
        modS = sb("modS", [P, KC, B])
        kq = sb("kq", [P, KC, D], BF16)
        krow = sb("krow", [P, D])
        rin = sb("rin", [P, NT])
        epsc = sb("epsc", [P, 1])

        setup = ExitStack()

        def tmp_sb(name, shape, dt=F32):
            return setup.enter_context(nc.sbuf_tensor(name, shape, dt))

        wemb = tmp_sb("wemb", [P, KC, 2 * D])
        condT = tmp_sb("condT", [P, KC, B])
        bembc = tmp_sb("bembc", [P, 2 * KC])
        gnc = tmp_sb("gnc", [P, KC])
        kern = tmp_sb("kern", [P, KC, D])
        kernT = tmp_sb("kernT", [P, KC, D])
        krinv = tmp_sb("krinv", [P, D])
        kcol = tmp_sb("kcol", [P, 2, KC])
        kz = tmp_sb("kz", [P, KC])
        diag = tmp_sb("diag", [P, 2, KC, P])
        bqs = tmp_sb("bqs", [P, 3])
        ssq = tmp_sb("ssq", [P, NT])
        rms = tmp_sb("rms", [P, NT])
        sqd = tmp_sb("sqd", [P, D])
        sqa = tmp_sb("sqa", [P, D])

        ld_x, ld_e, ld_w, ld_b, ld_k = (
            [sem(f"ld_x{i}") for i in range(NT // 4)], sem("ld_e"), sem("ld_w"), sem("ld_b"), sem("ld_k"))
        c_id, c_ready = sem("c_id"), sem("c_ready")
        emb_done, mod_chain, ss_act, ss_done, rms_done = (
            sem("emb_done"), sem("mod_chain"), sem("ss_act"), sem("ss_done"), sem("rms_done"))
        krow_done, diag_ready = sem("krow_done"), sem("diag_ready")
        with nc.Block() as block:
            @block.sync
            def _(sp):
                sp.dma_start(condT[:], io["condT"].rearrange("(k p) b -> p k b", p=P)).then_inc(ld_e, 16)
                sp.dma_start(wemb[:], io["W_emb"].rearrange("(k p) n -> p k n", p=P)).then_inc(ld_e, 16)
                for t in range(0, NT, 4):
                    sp.dma_start(x[:, t:t + 4, :], io["x"][t * P:(t + 4) * P, :].rearrange("(t p) d -> p t d", p=P)
                                 ).then_inc(ld_x[t // 4], 16)
                sp.dma_start(wqkv[:], io["W_qkv"].rearrange("(k p) n -> p k n", p=P)).then_inc(ld_k, 16)

            @block.scalar
            def _(act):
                act.dma_start(bembc[:], io["b_emb"]).then_inc(ld_w, 16)
                act.dma_start(gnc[:], io["g_norm"]).then_inc(ld_w, 16)
                for r in range(HPC):
                    act.dma_start(gcol[DH * r:DH * r + DH, 0:1], io["g_q"]).then_inc(ld_w, 16)
                    act.dma_start(gcol[DH * r:DH * r + DH, 1:2], io["g_k"]).then_inc(ld_w, 16)
                act.dma_start(biasrow[:], io["ffn_bias"].partition_broadcast(P)).then_inc(ld_b, 16)
                act.dma_start(kern[:], io["kernel"].rearrange("(k p) n -> p k n", p=P)).then_inc(ld_k, 16)
                act.dma_start(kernT[:], io["kernelT"].rearrange("(k p) n -> p k n", p=P)).then_inc(ld_k, 16)
                act.dma_start(wout[:], io["W_out"].rearrange("(k p) n -> p k n", p=P)).then_inc(ld_k, 16)
                for t in range(1, NT, 2):
                    act.wait_ge(ld_x[t // 4], 16)
                    if t > 1:
                        act.wait_ge(ss_act, t // 2)
                    nc.scalar.activation(sqa[:], x[:, t, :], ACT.Square, accum_out=ssq[:, t:t + 1]
                                         ).then_inc(ss_act, 1)
                act.wait_ge(ss_act, NT // 2)
                act.wait_ge(ss_done, NT // 2)
                act.wait_ge(c_ready, 1)
                nc.scalar.activation(rms[:], ssq[:], ACT.Sqrt, bias=epsc[:], scale=1.0 / D).then_inc(rms_done, 1)

            @block.gpsimd
            def _(pool):
                nc.gpsimd.memset(ident[:], 0.0).then_inc(c_id, 1)
                nc.gpsimd.memset(identb[:], 0.0).then_inc(c_id, 1)
                pool.wait_ge(c_id, 2)
                for m in (ident, identb):
                    nc.gpsimd.affine_select(out=m[:], in_=m[:], compare_op=ALU.not_equal, fill=1.0, base=0,
                                            pattern=[[-1, P]], channel_multiplier=1)
                nc.gpsimd.memset(ones[:], 1.0)
                nc.gpsimd.memset(onesb[:], 1.0)
                nc.gpsimd.memset(epsc[:], RMS_EPS).then_inc(c_ready, 1)

            @block.vector
            def _(dve):
                step = Chain(dve, mod_chain)
                for t in range(0, NT, 2):
                    dve.wait_ge(ld_x[t // 4], 16)
                    if t:
                        dve.wait_ge(ss_done, t // 2)
                    nc.vector.tensor_tensor_reduce(sqd[:], x[:, t, :], x[:, t, :], 1.0, 0.0, ALU.mult, ALU.add,
                                                   ssq[:, t:t + 1]).then_inc(ss_done, 1)
                dve.wait_ge(ld_w, 16 * (2 + 2 * HPC))
                dve.wait_ge(emb_done, 1)
                emb = bank[0][:, 0:2 * KC * B].rearrange("p (m b) -> p m b", b=B)
                for k in range(KC):
                    nc.vector.tensor_scalar(modG[:, k, :], emb[:, k, :], bembc[:, k:k + 1], 1.0, ALU.add, ALU.add)
                    last = nc.vector.tensor_scalar(modS[:, k, :], emb[:, KC + k, :], bembc[:, KC + k:KC + k + 1],
                                                   None, ALU.add)
                step(last)
                for k in range(KC):
                    nc.vector.tensor_scalar(modG[:, k, :], modG[:, k, :], gnc[:, k:k + 1], None, ALU.mult)
                nc.vector.tensor_scalar(gcol[:, 0:1], gcol[:, 0:1], float(DH) ** -0.5, None, ALU.mult)
                dve.wait_ge(ld_b, 16)
                am, z, inv = bqs[:, 0:1], bqs[:, 1:2], bqs[:, 2:3]
                step(nc.vector.tensor_reduce(am, biasrow[:], AX.X, ALU.max, apply_absolute_value=True))
                step(nc.vector.tensor_scalar(z, am, 0.0, None, ALU.is_equal))
                step(nc.vector.scalar_tensor_tensor(out=am, in0=am, scalar=1.0 / QMAX, in1=z,
                                                    op0=ALU.mult, op1=ALU.add))
                step(nc.vector.reciprocal(inv, am))
                step(nc.vector.tensor_scalar(biasrow[:], biasrow[:], inv, None, ALU.mult))
                step(nc.vector.tensor_scalar(biasrow[:], biasrow[:], MAGIC, None, ALU.add))
                step(nc.vector.tensor_scalar(biasrow[:], biasrow[:], MAGIC, am, ALU.subtract, ALU.mult))
                dve.wait_ge(ld_k, 16 * 4)
                step(nc.vector.tensor_reduce(kcol[:, 0, :], kernT[:], AX.X, ALU.max, apply_absolute_value=True))
                step(nc.vector.tensor_scalar(kz[:], kcol[:, 0, :], 0.0, None, ALU.is_equal))
                step(nc.vector.scalar_tensor_tensor(out=kcol[:, 0, :], in0=kcol[:, 0, :], scalar=1.0 / QMAX, in1=kz[:],
                                                    op0=ALU.mult, op1=ALU.add))
                step(nc.vector.reciprocal(kcol[:, 1, :], kcol[:, 0, :]))
                dve.wait_ge(c_ready, 1)
                for i in range(2):
                    for k in range(KC):
                        last = nc.vector.tensor_scalar(diag[:, i, k, :], ident[:], kcol[:, i, k:k + 1], None, ALU.mult)
                    last.then_inc(diag_ready, 1)
                dve.wait_ge(krow_done, 2)
                nc.vector.tensor_copy(krow[:], bank[1][:])
                step(nc.vector.tensor_copy(krinv[:], bank[2][:]))
                for k in range(KC):
                    last = nc.vector.tensor_tensor(kern[:, k, :], kern[:, k, :], krinv[:], ALU.mult)
                step(last)
                for k in range(KC):
                    last = nc.vector.tensor_scalar(kern[:, k, :], kern[:, k, :], MAGIC, None, ALU.add)
                step(last)
                for k in range(KC):
                    nc.vector.tensor_scalar(kq[:, k, :], kern[:, k, :], MAGIC, None, ALU.subtract)
                for k in range(KC):
                    nc.vector.tensor_tensor(wout[:, k, k * P:(k + 1) * P], wout[:, k, k * P:(k + 1) * P], ident[:],
                                            ALU.add)
                dve.wait_ge(rms_done, 1)
                nc.vector.reciprocal(rin[:], rms[:])

            @block.tensor
            def _(pe):
                pe.wait_ge(ld_e, 32)
                for m in range(2 * KC):
                    for k in range(KC):
                        last = nc.tensor.matmul(bank[0][:, m * B:(m + 1) * B], wemb[:, k, m * P:(m + 1) * P],
                                                condT[:, k, :], start=(k == 0), stop=(k == KC - 1))
                last.then_inc(emb_done, 1)
                pe.wait_ge(c_ready, 1)
                for i in range(2):
                    pe.wait_ge(diag_ready, i + 1)
                    nc.tensor.matmul(bank[1 + i][:], ones[:], diag[:, i].rearrange("p k q -> p (k q)"),
                                     start=True, stop=True).then_inc(krow_done, 1)

        setup.close()

        xr = sb("xr", [P, TB, D])
        xnT = sb("xnT", [P, KC, T])
        sq = sb("sq", [P, 2 * D])
        ss = sb("ss", [P, TB, 2 * HEADS])
        rt = sb("rt", [P, TB, 2 * HEADS])
        ri = sb("ri", [P, TB, 2 * HEADS])
        qkn = sb("qkn", [P, TB, 2 * D])
        qT = sb("qT", [P, KC, T])
        kT = sb("kT", [P, KC, T])
        v = sb("v", [P, TB, D])
        nmax = sb("nmax", [P, KC, TB, HPC])
        nmb = sb("nmb", [P, TB, KC, P], BF16)
        nmT = sb("nmT", [P, KC, T], BF16)
        pT = sb("pT", [P, 2 * HPC, TB, T])
        orc = sb("orc", [P, 2, T])
        oT = sb("oT", [P, KC, T])
        yq = sb("yq", [P, TB, D])
        ys = sb("ys", [P, TB, 8])
        qn = sb("qn", [P, TB, D], BF16)
        qnT = sb("qnT", [P, TB, KC, P], BF16)
        zt = sb("zt", [P, TB, D])
        x1s = sb("x1s", [P, TB, D])

        G, S, A = bank[0:2], bank[2:6], bank[6:8]
        GB16 = [g[:].bitcast(BF16) for g in G]
        NMB = A[0][:].bitcast(BF16)
        xr_ready, xT_done, xn_act, xn_dve = sem("xr_ready"), sem("xT_done"), sem("xn_act"), sem("xn_dve")
        qk_done, sq_ready, ss_ready, rt_ready, ri_ready, qkn_ready = (
            sem("qk_done"), sem("sq_ready"), sem("ss_ready"), sem("rt_ready"), sem("ri_ready"), sem("qkn_ready"))
        v_done, v_ready = sem("v_done"), sem("v_ready")
        qT_done, qT_ready, kT_done, kT_ready = sem("qT_done"), sem("qT_ready"), sem("kT_done"), sem("kT_ready")
        s_done, max_ready, hi_ready, nm_ready, nmT_done, nmT_ready = (
            sem("s_done"), sem("max_ready"), sem("hi_ready"), sem("nm_ready"), sem("nmT_done"), sem("nmT_ready"))
        st_done, exp_ready, pv_done, orc_ready, oT_ready = (
            sem("st_done"), sem("exp_ready"), sem("pv_done"), sem("orc_ready"), sem("oT_ready"))
        y_done, yc, q_ready, qnT_done, qnT_ready, acc_done, x1_ready, x1T_done, x1T_ready, x1_kept = (
            sem("y_done"), sem("yc"), sem("q_ready"), sem("qnT_done"), sem("qnT_ready"), sem("acc_done"),
            sem("x1_ready"), sem("x1T_done"), sem("x1T_ready"), sem("x1_kept"))
        pool_turn = sem("pool_turn")
        w_next = sem("w_next")
        YSTEPS = 28

        with nc.Block() as block:
            @block.sync
            def _(sp):
                sp.dma_start(self.whh[:], io["W_hh"].rearrange("(k p) n -> p k n", p=P)).then_inc(w_next, 16)
                sp.wait_ge(v_done, B * TB)
                sp.dma_start(self.w_in[:], io["W_ih"].rearrange("(k p) n -> p k n", p=P)).then_inc(w_next, 16)
                sp.wait_ge(w_next, 32)

            @block.tensor
            def _(pe):
                def project(f, h, k):
                    if h == 0 and k == 0:
                        pe.wait_ge(oT_ready, f * KC + KC)
                    last = nc.tensor.matmul(G[h][:], oT[:, k, h * P:(h + 1) * P], wout[:, k, :],
                                            start=(k == 0), stop=(k == KC - 1))
                    if k == KC - 1:
                        last.then_inc(y_done, 1)

                def turn_quantised(f, h):
                    pe.wait_ge(q_ready, f * TB + h + 1)
                    for k in range(KC):
                        last = nc.tensor.transpose(GB16[h][:, k * P:(k + 1) * P], qn[:, h, k * P:(k + 1) * P], identb[:])
                    last.then_inc(qnT_done, 1)

                def feed(f, h):
                    pe.wait_ge(qnT_ready, f * TB + h + 1)
                    for k in range(KC):
                        last = nc.tensor.matmul(G[h][:], qnT[:, h, k, :], kq[:, k, :],
                                                start=(k == 0), stop=(k == KC - 1))
                    last.then_inc(acc_done, 1)

                def turn_x1(f, h):
                    pe.wait_ge(x1_ready, f * TB + h + 1)
                    for k in range(KC):
                        last = nc.tensor.transpose(G[h][:, k * P:(k + 1) * P], x1s[:, h, k * P:(k + 1) * P], ident[:])
                    last.then_inc(x1T_done, 1)

                def scores(b, m, f):
                    if m % 2 == 0:
                        pe.wait_ge(qT_ready, b * 2 + m // 2 + 1)
                        pe.wait_ge(kT_ready, b * 2 + m // 2 + 1)
                    for h in range(TB):
                        for r in range(HPC):
                            if m and h == 0:
                                pe.wait_ge(max_ready, b * HEADS + (m - 1) * HPC + r + 1)
                            rows = slice(DH * r, DH * r + DH)
                            last = nc.tensor.matmul(S[r][:, h * T:(h + 1) * T], qT[rows, m, h * P:(h + 1) * P],
                                                    kT[rows, m, :], start=True, stop=True)
                            if h == TB - 1:
                                last.then_inc(s_done, 1)
                        if f is not None:
                            project(f, m // 2, (m % 2) * 2 + h)

                def turn_max(b, m):
                    pe.wait_ge(nm_ready, b * KC + m + 1)
                    if m:
                        pe.wait_ge(nmT_ready, b * KC + m)
                    for h in range(TB):
                        last = nc.tensor.transpose(NMB[:, (m % 2) * T + h * P:(m % 2) * T + (h + 1) * P],
                                                   nmb[:, h, m, :], identb[:])
                    last.then_inc(nmT_done, 1)

                def scores_t(b, n):
                    m, r = n // HPC, n % HPC
                    if r == 0:
                        pe.wait_ge(nmT_ready, b * KC + m + 1)
                    if m == 0:
                        pe.wait_ge(max_ready, b * HEADS + (KC - 1) * HPC + r + 1)
                    else:
                        pe.wait_ge(exp_ready, b * HEADS + n - HPC + 1)
                    rows = slice(DH * r, DH * r + DH)
                    for kt in range(TB):
                        nc.tensor.matmul(S[r][:, kt * T:(kt + 1) * T], kT[rows, m, kt * P:(kt + 1) * P],
                                         qT[rows, m, :], start=True, stop=False)
                        last = nc.tensor.matmul(S[r][:, kt * T:(kt + 1) * T], onesb[rows, :], nmT[rows, m, :],
                                                start=False, stop=True)
                    last.then_inc(st_done, 1)

                def values(b, m):
                    pe.wait_ge(exp_ready, b * HEADS + (m + 1) * HPC)
                    if m == 1:
                        pe.wait_ge(nmT_ready, b * KC + KC)
                    if m >= 2:
                        pe.wait_ge(oT_ready, b * KC + m - 1)
                    for which in range(2):
                        for kt in range(TB):
                            for r in range(HPC):
                                n = m * HPC + r
                                last = nc.tensor.matmul(A[(m + 1) % 2][DH * r:DH * r + DH, which * T:(which + 1) * T],
                                                        ones[:, 0:DH] if which else v[:, kt, n * DH:(n + 1) * DH],
                                                        pT[:, n % (2 * HPC), kt, :],
                                                        start=(kt == 0), stop=(kt == TB - 1))
                    last.then_inc(pv_done, 1)

                def turn_xr(b, f, g):
                    if f is not None:
                        pe.wait_ge(x1T_ready, f * TB + g + 1)
                    pe.wait_ge(xr_ready, b * TB + TB)
                    for k in (2 * g, 2 * g + 1):
                        for h in range(TB):
                            last = nc.tensor.transpose(G[g][:, (k % 2) * T + h * P:(k % 2) * T + (h + 1) * P],
                                                       xr[:, h, k * P:(k + 1) * P], ident[:])
                    last.then_inc(xT_done, 1)

                def turn(b, f, last_one=False):
                    pe.wait_ge(xn_act, b + 1)
                    pe.wait_ge(xn_dve, b + 1)
                    for h in range(TB):
                        for s in range(2):
                            for k in range(KC):
                                last = nc.tensor.matmul(S[2 * h + s][:], xnT[:, k, h * P:(h + 1) * P],
                                                        wqkv[:, k, s * D:(s + 1) * D],
                                                        start=(k == 0), stop=(k == KC - 1))
                        last.then_inc(qk_done, 1)
                    if f is not None:
                        pe.wait_ge(oT_ready, f * KC + KC)
                    for h in range(TB):
                        for k in range(KC):
                            last = nc.tensor.matmul(A[h][:], xnT[:, k, h * P:(h + 1) * P], wqkv[:, k, 2 * D:3 * D],
                                                    start=(k == 0), stop=(k == KC - 1))
                        last.then_inc(v_done, 1)
                    pe.wait_ge(qkn_ready, b * TB + TB)
                    for g in range(2):
                        for s, (dst, done) in enumerate(((G[g], qT_done), (A[g], kT_done))):
                            if s:
                                pe.wait_ge(v_ready, b * TB + g + 1)
                            for m in (2 * g, 2 * g + 1):
                                for h in range(TB):
                                    c = (m % 2) * T + h * P
                                    last = nc.tensor.transpose(dst[:, c:c + P],
                                                               qkn[:, h, s * D + m * P:s * D + (m + 1) * P], ident[:])
                            last.then_inc(done, 1)
                    for m in range(KC):
                        scores(b, m, f)
                        if m:
                            turn_max(b, m - 1)
                    for n in range(HEADS + 2):
                        if n < HEADS:
                            scores_t(b, n)
                        if n == 2:
                            turn_max(b, 3)
                        if n >= HEADS and not last_one:
                            turn_xr(b + 1, f, n - HEADS)
                        if n % HPC == 1 and n > HPC:
                            values(b, n // HPC - 1)
                        if f is not None:
                            if n in (2, 4):
                                turn_quantised(f, n // 2 - 1)
                            if n in (5, 7):
                                feed(f, (n - 5) // 2)
                            if n in (11, 14):
                                turn_x1(f, (n - 11) // 3)

                for g in range(2):
                    turn_xr(0, None, g)
                turn(0, None)
                with pe.Fori(1, B - 1) as b:
                    turn(b, b - 1)
                turn(B - 1, B - 2, last_one=True)
                for h in range(TB):
                    if h == 0:
                        pe.wait_ge(x1T_ready, (B - 1) * TB)
                    for k in range(KC):
                        project(B - 1, h, k)
                for stage in (turn_quantised, feed, turn_x1):
                    for h in range(TB):
                        stage(B - 1, h)

            @block.scalar
            def _(act):
                def keep_quantised(f, h):
                    act.wait_ge(qnT_done, f * TB + h + 1)
                    nc.scalar.copy(qnT[:, h, :, :], GB16[h][:, 0:D].rearrange("p (k q) -> p k q", k=KC)
                                   ).then_inc(qnT_ready, 1)

                def keep_x1(f, h):
                    act.wait_ge(x1T_done, f * TB + h + 1)
                    nc.scalar.copy(xT[:, :, bass.ds(f * T + h * P, P)],
                                   G[h][:].rearrange("p (k q) -> p k q", k=KC)).then_inc(x1T_ready, 1)

                def keep_max(b, m):
                    act.wait_ge(nmT_done, b * KC + m + 1)
                    nc.scalar.copy(nmT[:, m, :], NMB[:, (m % 2) * T:(m % 2 + 1) * T]).then_inc(nmT_ready, 1)

                def modulate(b):
                    act.wait_ge(xT_done, b * 2 + 1)
                    for k in range(2):
                        last = nc.scalar.activation(xnT[:, k, :], G[0][:, k * T:(k + 1) * T], ACT.Identity,
                                                    bias=modS[:, k, bass.ds(b, 1)], scale=modG[:, k, bass.ds(b, 1)])
                    last.then_inc(xn_act, 1)

                def turn(b, f, last_one=False):
                    for h in range(TB):
                        act.wait_ge(qk_done, b * TB + h + 1)
                        for s in range(2):
                            last = nc.scalar.activation(sq[:, s * D:(s + 1) * D], S[2 * h + s][:], ACT.Square)
                        last.then_inc(sq_ready, 1)
                        act.wait_ge(ss_ready, b * TB + h + 1)
                        nc.scalar.activation(rt[:, h, :], ss[:, h, :], ACT.Sqrt, bias=epsc[:], scale=1.0 / DH
                                             ).then_inc(rt_ready, 1)
                    for h in range(TB):
                        act.wait_ge(v_done, b * TB + h + 1)
                        nc.scalar.copy(v[:, h, :], A[h][:]).then_inc(v_ready, 1)
                    for g in range(2):
                        act.wait_ge(qT_done, b * 2 + g + 1)
                        nc.scalar.activation(qT[:, 2 * g:2 * g + 2, :], G[g][:].rearrange("p (k q) -> p k q", k=2),
                                             ACT.Identity, scale=gcol[:, 0:1]).then_inc(qT_ready, 1)
                    for m in range(KC - 1):
                        keep_max(b, m)
                    for n in range(HEADS):
                        act.wait_ge(st_done, b * HEADS + n + 1)
                        if n >= 2 * HPC and n % HPC == 0:
                            act.wait_ge(pv_done, b * KC + n // HPC - 1)
                        nc.scalar.activation(pT[:, n % (2 * HPC), :, :], S[n % HPC][:].rearrange("p (k q) -> p k q", k=TB),
                                             ACT.Exp).then_inc(exp_ready, 1)
                        if n == 2:
                            keep_max(b, KC - 1)
                        if f is not None and n in (3, 5):
                            keep_quantised(f, (n - 3) // 2)
                        if f is not None and n in (11, 14):
                            keep_x1(f, (n - 11) // 3)
                    if not last_one:
                        modulate(b + 1)

                modulate(0)
                turn(0, None)
                with act.Fori(1, B - 1) as b:
                    turn(b, b - 1)
                turn(B - 1, B - 2, last_one=True)
                for stage in (keep_quantised, keep_x1):
                    for h in range(TB):
                        stage(B - 1, h)

            @block.vector
            def _(dve):
                def scale(step, h, c):
                    am, z, inv = ys[:, h, c:c + 1], ys[:, h, c + 1:c + 2], ys[:, h, c + 2:c + 3]
                    step(nc.vector.tensor_scalar(z, am, 0.0, None, ALU.is_equal))
                    step(nc.vector.scalar_tensor_tensor(out=am, in0=am, scalar=1.0 / QMAX, in1=z,
                                                        op0=ALU.mult, op1=ALU.add))
                    step(nc.vector.reciprocal(inv, am))
                    return am, inv

                def quantise(f, h, step):
                    dve.wait_ge(y_done, f * TB + h + 1)
                    step(nc.vector.tensor_reduce(ys[:, h, 0:1], G[h][:], AX.X, ALU.max, apply_absolute_value=True))
                    _, inv = scale(step, h, 0)
                    step(nc.vector.tensor_scalar(yq[:, h, :], G[h][:], inv, MAGIC, ALU.mult, ALU.add))
                    nc.vector.tensor_scalar(qn[:, h, :], yq[:, h, :], MAGIC, None, ALU.subtract).then_inc(q_ready, 1)

                def feed_forward(f, h, step):
                    dve.wait_ge(acc_done, f * TB + h + 1)
                    step(nc.vector.scalar_tensor_tensor(out=zt[:, h, :], in0=G[h][:], scalar=ys[:, h, 0:1],
                                                        in1=krow[:], op0=ALU.mult, op1=ALU.mult))
                    step(nc.vector.tensor_tensor(zt[:, h, :], zt[:, h, :], biasrow[:], ALU.add))
                    step(nc.vector.tensor_reduce(ys[:, h, 4:5], zt[:, h, :], AX.X, ALU.max))
                    step(nc.vector.tensor_scalar(ys[:, h, 4:5], ys[:, h, 4:5], 0.0, None, ALU.max))
                    s2, inv2 = scale(step, h, 4)
                    if h == 0:
                        dve.wait_ge(x1_kept, PRIME + f * TB)
                    step(nc.vector.tensor_scalar(zt[:, h, :], zt[:, h, :], 0.0, inv2, ALU.max, ALU.mult))
                    step(nc.vector.tensor_scalar(zt[:, h, :], zt[:, h, :], MAGIC, MAGIC, ALU.add, ALU.subtract))
                    nc.vector.scalar_tensor_tensor(out=x1s[:, h, :], in0=zt[:, h, :], scalar=s2,
                                                   in1=x[:, f * TB + h, :], op0=ALU.mult, op1=ALU.add
                                                   ).then_inc(x1_ready, 1)

                def keep_o(b, m):
                    dve.wait_ge(pv_done, b * KC + m + 1)
                    nc.vector.reciprocal(orc[:, m % 2, :], A[(m + 1) % 2][:, T:2 * T]).then_inc(orc_ready, 1)
                    dve.wait_ge(orc_ready, b * KC + m + 1)
                    nc.vector.tensor_tensor(oT[:, m, :], A[(m + 1) % 2][:, 0:T], orc[:, m % 2, :],
                                            ALU.mult).then_inc(oT_ready, 1)

                def modulate(b):
                    dve.wait_ge(xT_done, b * 2 + 2)
                    for k in (2, 3):
                        last = nc.vector.tensor_scalar(xnT[:, k, :], G[1][:, (k - 2) * T:(k - 1) * T],
                                                       modG[:, k, bass.ds(b, 1)], modS[:, k, bass.ds(b, 1)],
                                                       ALU.mult, ALU.add)
                    last.then_inc(xn_dve, 1)

                def turn(b, f, last_one=False):
                    step = f is not None and Chain(dve, yc, f * YSTEPS)
                    for h in range(TB):
                        dve.wait_ge(sq_ready, b * TB + h + 1)
                        nc.vector.tensor_reduce(ss[:, h, :], sq[:].rearrange("p (n d) -> p n d", d=DH),
                                                AX.X, ALU.add).then_inc(ss_ready, 1)
                        dve.wait_ge(rt_ready, b * TB + h + 1)
                        nc.vector.reciprocal(ri[:, h, :], rt[:, h, :]).then_inc(ri_ready, 1)
                        dve.wait_ge(ri_ready, b * TB + h + 1)
                        for s in range(2):
                            last = nc.vector.tensor_tensor(
                                qkn[:, h, s * D:(s + 1) * D].rearrange("p (n d) -> p n d", d=DH),
                                S[2 * h + s][:].rearrange("p (n d) -> p n d", d=DH),
                                ri[:, h, s * HEADS:(s + 1) * HEADS].unsqueeze(2).broadcast_to([P, HEADS, DH]), ALU.mult)
                        last.then_inc(qkn_ready, 1)
                    for g in range(2):
                        dve.wait_ge(kT_done, b * 2 + g + 1)
                        nc.vector.tensor_scalar(kT[:, 2 * g:2 * g + 2, :], A[g][:].rearrange("p (k q) -> p k q", k=2),
                                                gcol[:, 1:2], None, ALU.mult).then_inc(kT_ready, 1)
                    for n in range(HEADS):
                        dve.wait_ge(s_done, b * HEADS + n + 1)
                        nc.vector.tensor_reduce(nmax[:, n // HPC, :, n % HPC],
                                                S[n % HPC][:].rearrange("p (h k) -> p h k", h=TB),
                                                AX.X, ALU.max, negate=True).then_inc(max_ready, 1)
                    if f is not None:
                        quantise(f, 0, step)
                        quantise(f, 1, step)
                    keep_o(b, 0)
                    if f is not None:
                        feed_forward(f, 0, step)
                    keep_o(b, 1)
                    if f is not None:
                        feed_forward(f, 1, step)
                        self.ysteps = step.n
                    keep_o(b, 2)
                    if not last_one:
                        modulate(b + 1)
                    keep_o(b, 3)

                modulate(0)
                turn(0, None)
                with dve.Fori(1, B - 1) as b:
                    turn(b, b - 1)
                turn(B - 1, B - 2, last_one=True)
                step = Chain(dve, yc, (B - 1) * YSTEPS)
                for stage in (quantise, feed_forward):
                    for h in range(TB):
                        stage(B - 1, h, step)

            @block.gpsimd
            def _(pool):
                pool.sem_inc(x1_kept, PRIME)

                def scale_x(b):
                    for h in range(TB):
                        nc.gpsimd.tensor_tensor(xr[:, h, :], x[:, b * TB + h, :],
                                                rin[:, bass.ds(b * TB + h, 1)].broadcast_to([P, D]), ALU.mult
                                                ).then_inc(xr_ready, 1)

                def keep_x1(f):
                    for h in range(TB):
                        pool.wait_ge(x1_ready, f * TB + h + 1)
                        nc.gpsimd.tensor_copy(x[:, f * TB + h, :], x1s[:, h, :]).then_inc(x1_kept, 1)

                def turn(b, f, last_one=False):
                    if not last_one:
                        pool.wait_ge(xT_done, b * 2 + 2)
                        scale_x(b + 1)
                    for m in range(KC):
                        pool.wait_ge(max_ready, b * HEADS + (m + 1) * HPC)
                        pool.sem_inc(pool_turn, 1)
                        nc.gpsimd.tensor_copy(nmb[:, :, m, 0::DH], nmax[:, m, :, :]).then_inc(hi_ready, 1)
                        pool.wait_ge(hi_ready, 1 + b * KC + m + 1)
                        nc.gpsimd.tensor_tensor(nmb[:, :, m, 1::DH], nmax[:, m, :, :], nmb[:, :, m, 0::DH],
                                                ALU.subtract).then_inc(nm_ready, 1)
                    if f is not None:
                        keep_x1(f)

                nc.gpsimd.memset(nmb[:], 0.0).then_inc(hi_ready, 1)
                scale_x(0)
                pool.wait_ge(hi_ready, 1)
                turn(0, None)
                with pool.Fori(1, B - 1) as b:
                    turn(b, b - 1)
                turn(B - 1, B - 2, last_one=True)
                keep_x1(B - 1)
        assert self.ysteps == YSTEPS, self.ysteps

    def gru(self, ctx):
        nc, io, ident, bank, xT = self.nc, self.io, self.ident, self.bank, self.xT

        def sb(name, shape, dt=F32):
            return ctx.enter_context(nc.sbuf_tensor(name, shape, dt))

        def sem(name):
            return ctx.enter_context(nc.semaphore("g_" + name))

        gi = sb("gi", [P, 2, TC, NG * GB])
        wih, whh = self.w_in, self.whh
        bic = sb("bic", [P, NG * KC])
        bhc = sb("bhc", [P, NG * KC])
        bhn = sb("bhn", [P, KC, B])
        hT = sb("hT", [P, KC, 32])
        fold = sb("fold", [P, GB])
        gh = sb("gh", [P, NG, P])
        rg = sb("rg", [P, GB])
        zg = sb("zg", [P, GB])
        ng = sb("ng", [P, GB])
        t1 = sb("t1", [P, GB])
        t2 = sb("t2", [P, GB])
        dh = sb("dh", [P, GB])
        zd = sb("zd", [P, GB])

        ld = sem("ld")
        bias_ready, gi_done, gi_kept = sem("bias_ready"), sem("gi_done"), sem("gi_kept")
        h_ready, rn_done, z_done, rn_kept, z_kept = (
            sem("h_ready"), sem("rn_done"), sem("z_done"), sem("rn_kept"), sem("z_kept"))
        r_folded, n_folded, z_folded = sem("r_folded"), sem("n_folded"), sem("z_folded")
        r_ready, n_ready, z_ready, t1_ready, t2_ready, dh_ready, zd_ready, h_kept = (
            sem("r_ready"), sem("n_ready"), sem("z_ready"), sem("t1_ready"), sem("t2_ready"), sem("dh_ready"),
            sem("zd_ready"), sem("h_kept"))
        dve_turn = sem("dve_turn")
        R, Z, NN = 0, 1, 2
        RN, ZB, FR, FN = bank[0], bank[1], bank[2], bank[3]
        FZ = bank[4:6]
        GI = bank[6:8]
        hv = hT[:, :, 0:B]
        NCH = T // TC
        UNITS, SPREAD = NG * KC * KC, TC - 1

        def units(s):
            return range(s * UNITS // SPREAD, min((s + 1) * UNITS // SPREAD, UNITS))

        KEEP_AT = [1 + next(s for s in range(TC) if (g + 1) * KC * KC - 1 in units(s)) for g in range(NG)]

        def cols(t):
            return t[:].rearrange("p (j b) -> p j b", b=B)

        with nc.Block() as block:
            @block.sync
            def _(sp):
                sp.dma_start(bic[:], io["b_ih"]).then_inc(ld, 16)
                sp.dma_start(bhc[:], io["b_hh"]).then_inc(ld, 16)
                sp.dma_start(hT[:, :, 0:B], io["condT"].rearrange("(k p) b -> p k b", p=P)).then_inc(ld, 16)

            @block.tensor
            def _(pe):
                pe.wait_ge(ld, 48)
                pe.wait_ge(bias_ready, 2)
                steps_of = xT[:].rearrange("p k (b t) -> p k b t", t=T)
                w = whh[:].rearrange("p k (g n) -> p k g n", g=NG)

                def input_part(c, p, u):
                    g, j, k = u // (KC * KC), u // KC % KC, u % KC
                    if j == 0 and k == 0:
                        if not isinstance(c, int):
                            pe.wait_ge(gi_kept, c * NG + g - 1)
                        elif c * NG + g >= 2:
                            pe.wait_ge(gi_kept, c * NG + g - 1)
                    last = nc.tensor.matmul(GI[(p + g) % 2][:, j * TC * B:(j + 1) * TC * B],
                                            wih[:, k, (g * KC + j) * P:(g * KC + j + 1) * P],
                                            steps_of[:, k, :, bass.ds(c * TC, TC)],
                                            start=(k == 0), stop=(k == KC - 1))
                    if j == KC - 1 and k == KC - 1:
                        last.then_inc(gi_done, 1)

                def seed_rn(p, s):
                    nc.tensor.matmul(FR[:, 0:GB], ident[:], gi[:, p, s, 0:GB], start=True, stop=False)
                    nc.tensor.matmul(FN[:, 0:GB], ident[:], bhn[:].rearrange("p j b -> p (j b)"),
                                     start=True, stop=False)

                def seed_z(p, s):
                    nc.tensor.matmul(FZ[s % 2][:, 0:GB], ident[:], gi[:, p, s, GB:2 * GB], start=True, stop=False)

                def chunk(c, p, final):
                    for s in range(TC):
                        t = c * TC + s
                        pe.wait_ge(h_ready, t + 1)
                        for k in range(KC):
                            for j in range(KC):
                                last = nc.tensor.matmul(RN[32 * j:32 * j + 32, 0:2 * P], hT[:, k, :],
                                                        w[:, k, 0::2, j * P:(j + 1) * P],
                                                        start=(k == 0), stop=(k == KC - 1))
                        last.then_inc(rn_done, 1)
                        for k in range(KC):
                            if k == 2:
                                pe.wait_ge(rn_kept, t + 1)
                                nc.tensor.matmul(FR[:, 0:GB], gh[:, 0, :], fold[:], start=False, stop=True
                                                 ).then_inc(r_folded, 1)
                                nc.tensor.matmul(FN[:, 0:GB], gh[:, 1, :], fold[:], start=False, stop=True
                                                 ).then_inc(n_folded, 1)
                            for j in range(KC):
                                last = nc.tensor.matmul(ZB[32 * j:32 * j + 32, 0:P], hT[:, k, :],
                                                        w[:, k, Z, j * P:(j + 1) * P],
                                                        start=(k == 0), stop=(k == KC - 1))
                        last.then_inc(z_done, 1)
                        more = s + 1 < TC or not final
                        if more:
                            pe.wait_ge(t1_ready, t + 1)
                            if s + 1 == TC:
                                pe.wait_ge(gi_kept, (c + 2) * NG)
                            seed_rn(*((p, s + 1) if s + 1 < TC else (1 - p, 0)))
                        pe.wait_ge(z_kept, t + 1)
                        nc.tensor.matmul(FZ[s % 2][:, 0:GB], gh[:, 2, :], fold[:], start=False, stop=True
                                         ).then_inc(z_folded, 1)
                        if more:
                            seed_z(*((p, s + 1) if s + 1 < TC else (1 - p, 0)))
                        if not final:
                            for u in units(s):
                                input_part(c + 1, 1 - p, u)

                for u in range(NG * KC * KC):
                    input_part(0, 0, u)
                pe.wait_ge(gi_kept, NG)
                seed_rn(0, 0)
                seed_z(0, 0)
                with pe.Fori(0, NCH // 2 - 1) as cc:
                    chunk(cc * 2, 0, False)
                    chunk(cc * 2 + 1, 1, False)
                chunk(NCH - 2, 0, False)
                chunk(NCH - 1, 1, True)

            @block.scalar
            def _(act):
                with act.Fori(0, NCH) as c:
                    for s in range(TC):
                        t = c * TC + s
                        act.wait_ge(rn_done, t + 1)
                        nc.scalar.copy(gh[:, 0:2, :], RN[:, 0:2 * P].rearrange("p (g c) -> p g c", g=2)
                                       ).then_inc(rn_kept, 1)
                        act.wait_ge(r_folded, t + 1)
                        nc.scalar.activation(rg[:], FR[:, 0:GB], ACT.Tanh, scale=0.5).then_inc(r_ready, 1)
                        act.wait_ge(z_done, t + 1)
                        nc.scalar.copy(gh[:, 2, :], ZB[:, 0:P]).then_inc(z_kept, 1)
                        act.wait_ge(t2_ready, t + 1)
                        nc.scalar.activation(ng[:], t2[:], ACT.Tanh).then_inc(n_ready, 1)
                        act.wait_ge(z_folded, t + 1)
                        nc.scalar.activation(zg[:], FZ[s % 2][:, 0:GB], ACT.Tanh, scale=0.5).then_inc(z_ready, 1)

            @block.vector
            def _(dve):
                dve.wait_ge(ld, 48)
                nc.vector.memset(hT[:, :, B:32], 0.0).then_inc(h_ready, 1)
                nc.vector.tensor_copy(bhn[:], bhc[:, 2 * KC:3 * KC].unsqueeze(2).broadcast_to([P, KC, B]))
                nc.vector.tensor_tensor(bic[:, 0:2 * KC], bic[:, 0:2 * KC], bhc[:, 0:2 * KC], ALU.add
                                        ).then_inc(bias_ready, 1)
                for j in range(KC):
                    last = nc.vector.tensor_copy(fold[:, j * B:(j + 1) * B], ident[:, 32 * j:32 * j + B])
                last.then_inc(bias_ready, 1)
                dve.wait_ge(bias_ready, 2)

                def keep_input(n, p, g):
                    dve.wait_ge(gi_done, n + 1)
                    nc.vector.tensor_tensor(
                        gi[:, p, :, g * GB:(g + 1) * GB].rearrange("p t (j b) -> p j b t", b=B),
                        GI[(p + g) % 2][:].rearrange("p (j b t) -> p j b t", b=B, t=TC)[:, 0:KC],
                        bic[:, g * KC:(g + 1) * KC].unsqueeze(2).unsqueeze(3).broadcast_to([P, KC, B, TC]),
                        ALU.add).then_inc(gi_kept, 1)

                def chunk(c, p, final):
                    dve.wait_ge(gi_kept, (c + 1) * NG)
                    for s in range(TC):
                        t = c * TC + s
                        if not final and s in KEEP_AT:
                            g = KEEP_AT.index(s)
                            keep_input((c + 1) * NG + g, 1 - p, g)
                        dve.wait_ge(r_ready, t + 1)
                        dve.wait_ge(n_folded, t + 1)
                        nc.vector.scalar_tensor_tensor(out=t1[:], in0=rg[:], scalar=1.0, in1=FN[:, 0:GB],
                                                       op0=ALU.add, op1=ALU.mult).then_inc(t1_ready, 1)
                        dve.wait_ge(t1_ready, t + 1)
                        nc.vector.scalar_tensor_tensor(out=t2[:], in0=t1[:], scalar=0.5,
                                                       in1=gi[:, p, s, 2 * GB:3 * GB],
                                                       op0=ALU.mult, op1=ALU.add).then_inc(t2_ready, 1)
                        dve.wait_ge(h_kept, PRIME + t)
                        dve.wait_ge(n_ready, t + 1)
                        nc.vector.tensor_tensor(cols(dh), hv, cols(ng), ALU.subtract).then_inc(dh_ready, 1)
                        dve.wait_ge(dh_ready, t + 1)
                        dve.sem_inc(dve_turn, 1)
                        dve.wait_ge(z_ready, t + 1)
                        nc.vector.scalar_tensor_tensor(out=zd[:], in0=zg[:], scalar=1.0, in1=dh[:],
                                                       op0=ALU.add, op1=ALU.mult).then_inc(zd_ready, 1)
                        dve.wait_ge(zd_ready, t + 1)
                        nc.vector.scalar_tensor_tensor(out=hv, in0=cols(zd), scalar=0.5, in1=cols(ng),
                                                       op0=ALU.mult, op1=ALU.add).then_inc(h_ready, 1)

                for g in range(NG):
                    keep_input(g, 0, g)
                with dve.Fori(0, NCH // 2 - 1) as cc:
                    chunk(cc * 2, 0, False)
                    chunk(cc * 2 + 1, 1, False)
                chunk(NCH - 2, 0, False)
                chunk(NCH - 1, 1, True)

            @block.gpsimd
            def _(pool):
                hseq = xT[:].rearrange("p k (b t) -> p k b t", t=T)
                pool.sem_inc(h_kept, PRIME)
                with pool.Fori(0, T) as t:
                    pool.wait_ge(h_ready, t + 2)
                    nc.gpsimd.tensor_copy(hseq[:, :, :, t], hv).then_inc(h_kept, 1)

    def router(self, ctx):
        nc, io, x, ident, ones, bank, hT = self.nc, self.io, self.x, self.ident, self.ones, self.bank, self.xT

        def sb(name, shape, dt=F32):
            return ctx.enter_context(nc.sbuf_tensor(name, shape, dt))

        def sem(name):
            return ctx.enter_context(nc.semaphore("r_" + name))

        wr = sb("wr", [P, KC, E])
        shgu = sb("shgu", [P, 2, KC, I])
        shd = sb("shd", [IH, 2, D])
        ebias = sb("ebias", [P, E])
        before = sb("before", [P, P], BF16)
        onesb = sb("onesb", [P, P], BF16)
        slot0 = sb("slot0", [P, E])
        tokid = sb("tokid", [P, NT], I32)
        spare = sb("spare", [P, 2, TOPK])
        zero = sb("zero", [P, 2, D + E])
        blank = sb("blank", [E, CAP], I32)
        hs = sb("hs", [P, KC, P])
        rows = sb("rows", [P, D + E])
        sig = sb("sig", [P, I])
        gs = sb("gs", [P, I])
        act_h = sb("act_h", [P, I])
        hTs = sb("hTs", [IH, 2, P])
        sco = sb("sco", [P, E])
        sc = sb("sc", [P, E])
        top2 = sb("top2", [P, NGRP, 8])
        gsc = sb("gsc", [P, NGRP + 4])
        gtop = sb("gtop", [P, 8])
        grep = sb("grep", [P, 16])
        gpick = sb("gpick", [P, 8])
        gmask = sb("gmask", [P, NGRP])
        mk = sb("mk", [P, E])
        top8 = sb("top8", [P, 8])
        taken = sb("taken", [P, E])
        sel = sb("sel", [P, E], BF16)
        count = sb("count", [P, E], BF16)
        wsum = sb("wsum", [P, 2])
        w = sb("w", [P, E])
        fits = sb("fits", [P, E])
        slot = sb("slot", [P, E])
        key = sb("key", [P, E])
        key8 = sb("key8", [P, 8])
        dest = sb("dest", [P, 8])
        desti = [sb(f"desti{p}", [P, 8], I32) for p in range(2)]
        entry = [sb(f"entry{p}", [P, 1], I32) for p in range(2)]

        ld, c_ready = sem("ld"), sem("c_ready")
        blank_ready, blank_out = sem("blank_ready"), sem("blank_out")
        staged, gu_done, sig_ready, act_ready, hT_done, hT_ready, dn_done, sum_ready = (
            sem("staged"), sem("gu_done"), sem("sig_ready"), sem("act_ready"), sem("hT_done"), sem("hT_ready"),
            sem("dn_done"), sem("sum_ready"))
        lg_done, sco_ready, sel_ready, pos_done, chain, row_done, row_ready, row_out = (
            sem("lg_done"), sem("sco_ready"), sem("sel_ready"), sem("pos_done"), sem("chain"), sem("row_done"),
            sem("row_ready"), sem("row_out"))
        sco_used, w_ready = sem("sco_used"), sem("w_ready")
        entry_ready, scattered, dchain = sem("entry_ready"), [sem("scattered0"), sem("scattered1")], sem("dchain")
        acc_out, pool_turn, dve_turn, table_blank = sem("acc_out"), sem("pool_turn"), sem("dve_turn"), sem("table_blank")
        LG, GU, RW, HT, DN, PS = bank[0], bank[1], bank[2], bank[3], bank[4], bank[5]
        CSTEPS = 20
        with nc.Block() as block:
            @block.sync
            def _(sp):
                sp.dma_start(wr[:], io["routerT"].rearrange("(k p) e -> p k e", p=P)).then_inc(ld, 16)
                for a, n in enumerate(("sh_gate", "sh_up")):
                    sp.dma_start(shgu[:, a], io[n].rearrange("(k p) i -> p k i", p=P)).then_inc(ld, 16)
                sp.dma_start(shd[:], io["sh_down"].rearrange("(p c) d -> p c d", c=2)).then_inc(ld, 16)
                sp.dma_start(ebias[:], io["e_bias"].partition_broadcast(P)).then_inc(ld, 16)
                sp.wait_ge(blank_ready, 1)
                sp.dma_start(self.hs_rows[N:N + CAP, :].rearrange("(c p) d -> p c d", p=P),
                             zero[:]).then_inc(blank_out, 16)
                sp.sem_inc(row_out, PRIME_DMA)
                with sp.Fori(0, NT) as i:
                    sp.wait_ge(row_ready, i + 1)
                    sp.wait_ge(w_ready, i + 1)
                    sp.dma_start(self.hs_rows[bass.ds(i * P, P), :], rows[:]).then_inc(row_out, 16)
                    sp.wait_ge(sum_ready, PRIME + i + 1)
                    sp.dma_start(self.acc_rows[bass.ds(i * P, P), :], x[:, bass.ds(i, 1), :].rearrange("p t d -> p (t d)")
                                 ).then_inc(acc_out, 16)
                sp.wait_ge(acc_out, 16 * NT)
                sp.wait_ge(row_out, PRIME_DMA + 16 * NT)
                sp.wait_ge(blank_out, 16)

            @block.gpsimd
            def _(pool):
                nc.gpsimd.memset(zero[:], 0.0)
                nc.gpsimd.memset(onesb[:], 1.0).then_inc(c_ready, 1)
                nc.gpsimd.memset(before[:], 1.0).then_inc(c_ready, 1)
                nc.gpsimd.iota(tokid[:], pattern=[[P, NT]], base=0, channel_multiplier=1).then_inc(c_ready, 1)
                nc.gpsimd.iota(slot0[:], pattern=[[-CAP, E]], base=int(KEY0), channel_multiplier=0,
                               allow_small_or_imprecise_dtypes=True).then_inc(c_ready, 1)
                nc.gpsimd.iota(spare[:], pattern=[[TOPK * P, 2], [P, TOPK]], base=SLOTS, channel_multiplier=1,
                               allow_small_or_imprecise_dtypes=True).then_inc(c_ready, 1)
                pool.wait_ge(c_ready, 5)
                nc.gpsimd.iota(blank[:], pattern=[[1, CAP]], base=N, channel_multiplier=0).then_inc(blank_ready, 1)
                nc.gpsimd.affine_select(out=before[:], in_=before[:], compare_op=ALU.is_gt, fill=0.0, base=0,
                                        pattern=[[1, P]], channel_multiplier=-1).then_inc(c_ready, 1)
                pool.wait_ge(blank_ready, 1)
                nc.gpsimd.dma_start(self.table[0:SLOTS, :].rearrange("(e s) w -> e (s w)", e=E), blank[:]
                                    ).then_inc(table_blank, 16)
                pool.wait_ge(table_blank, 16)
                with pool.Fori(0, NT // 2) as i2:
                    for p in range(2):
                        pool.wait_ge(entry_ready, i2 * 2 + p + 1)
                        pool.sem_inc(pool_turn, 1)
                        for c in range(TOPK):
                            nc.gpsimd.indirect_dma_start(
                                self.table, bass.IndirectOffsetOnAxis(desti[p][:, c:c + 1].bitcast(U32), 0),
                                entry[p][:], None).then_inc(scattered[p], 16)
                for p in range(2):
                    pool.wait_ge(scattered[p], 16 * TOPK * (NT // 2))

            @block.tensor
            def _(pe):
                pe.wait_ge(ld, 80)
                pe.wait_ge(c_ready, 6)

                def logits(i):
                    pe.wait_ge(staged, i + 1)
                    for k in range(KC):
                        last = nc.tensor.matmul(LG[:, 0:E], hs[:, k, :], wr[:, k, :], start=(k == 0), stop=(k == KC - 1))
                    last.then_inc(lg_done, 1)

                def turn_rows(i):
                    for k in range(KC):
                        last = nc.tensor.transpose(RW[:, k * P:(k + 1) * P], hs[:, k, :], ident[:])
                    last.then_inc(row_done, 1)

                def shared(i):
                    for k in range(KC):
                        last = nc.tensor.matmul(GU[:, 0:2 * I], hs[:, k, :], shgu[:, :, k, :],
                                                start=(k == 0), stop=(k == KC - 1))
                    last.then_inc(gu_done, 1)

                def tile(i, last_one):
                    pe.wait_ge(sel_ready, i + 1)
                    nc.tensor.matmul(PS[:, 0:E], before[:], sel[:], start=True, stop=False)
                    nc.tensor.matmul(PS[:, 0:E], onesb[:], count[:], start=False, stop=True).then_inc(pos_done, 1)
                    pe.wait_ge(act_ready, i + 1)
                    for c in range(2):
                        last = nc.tensor.transpose(HT[0:IH, c * P:(c + 1) * P], act_h[:, c::2], ident[:])
                    last.then_inc(hT_done, 1)
                    if not last_one:
                        logits(i + 1)
                        pe.wait_ge(row_ready, i + 1)
                        turn_rows(i + 1)
                    pe.wait_ge(sum_ready, PRIME + i)
                    pe.wait_ge(hT_ready, i + 1)
                    for c in range(2):
                        last = nc.tensor.matmul(DN[:], hTs[:, c, :], shd[:, c, :], start=(c == 0), stop=(c == 1))
                    last.then_inc(dn_done, 1)
                    if not last_one:
                        shared(i + 1)

                logits(0)
                turn_rows(0)
                shared(0)
                with pe.Fori(0, NT - 1) as i:
                    tile(i, False)
                tile(NT - 1, True)

            @block.scalar
            def _(act):
                def stage(i):
                    nc.scalar.copy(hs[:], hT[:, :, bass.ds(i * P, P)]).then_inc(staged, 1)

                def tile(i, last_one):
                    act.wait_ge(lg_done, i + 1)
                    act.wait_ge(sco_used, PRIME + i)
                    nc.scalar.activation(sco[:], LG[:, 0:E], ACT.Sigmoid).then_inc(sco_ready, 1)
                    act.wait_ge(row_done, i + 1)
                    act.wait_ge(row_out, PRIME_DMA + i * 16)
                    nc.scalar.copy(rows[:, 0:D], RW[:]).then_inc(row_ready, 1)
                    act.wait_ge(gu_done, i + 1)
                    nc.scalar.activation(sig[:], GU[:, 0:I], ACT.Sigmoid).then_inc(sig_ready, 1)
                    if not last_one:
                        stage(i + 1)
                    act.wait_ge(hT_done, i + 1)
                    nc.scalar.copy(hTs[:], HT[0:IH, 0:2 * P].rearrange("p (c q) -> p c q", c=2)).then_inc(hT_ready, 1)

                act.sem_inc(sco_used, PRIME)
                stage(0)
                with act.Fori(0, NT // 4 - 1) as i4:
                    for u in range(4):
                        tile(i4 * 4 + u, False)
                for i in range(NT - 4, NT):
                    tile(i, i == NT - 1)

            @block.vector
            def _(dve):
                first = Chain(dve, dchain)
                first(nc.vector.memset(count[:], 0.0))
                first(nc.vector.memset(gsc[:, NGRP:NGRP + 4], TAKEN))
                first(nc.vector.memset(gpick[:, TOPG:8], TAKEN))
                dve.wait_ge(ld, 80)
                dve.wait_ge(c_ready, 6)
                dve.sem_inc(sum_ready, PRIME)

                def add_shared(i):
                    dve.wait_ge(dn_done, i + 1)
                    nc.vector.tensor_tensor(x[:, i, :], x[:, i, :], DN[:], ALU.add).then_inc(sum_ready, 1)

                def tile(i, p, scatters):
                    step = Chain(dve, chain, i * CSTEPS)
                    dve.wait_ge(sco_ready, i + 1)
                    step(nc.vector.tensor_tensor(sc[:], sco[:], ebias[:], ALU.add))
                    dve.sem_inc(dve_turn, 1)
                    for g in range(NGRP):
                        last = nc.vector.max(top2[:, g, :], sc[:, g * GSZ:(g + 1) * GSZ])
                    step(last)
                    step(nc.vector.tensor_tensor(gsc[:, 0:NGRP], top2[:, :, 0], top2[:, :, 1], ALU.add))
                    dve.sem_inc(dve_turn, 1)
                    step(nc.vector.max(gtop[:], gsc[:, 0:NGRP]))
                    step(nc.vector.tensor_copy(gpick[:, 0:TOPG], gtop[:, 0:TOPG]))
                    dve.sem_inc(dve_turn, 1)
                    step(nc.vector.match_replace(grep[:, 0:NGRP + 4], gpick[:], gsc[:], -2.0 * TAKEN))
                    step(nc.vector.tensor_scalar(gmask[:], grep[:, 0:NGRP], -2.0 * TAKEN, None, ALU.is_equal))
                    step(nc.vector.tensor_tensor(mk[:].rearrange("p (g s) -> p g s", s=GSZ),
                                                 sc[:].rearrange("p (g s) -> p g s", s=GSZ),
                                                 gmask[:].unsqueeze(2).broadcast_to([P, NGRP, GSZ]), ALU.mult))
                    dve.sem_inc(dve_turn, 1)
                    step(nc.vector.max(top8[:], mk[:]))
                    dve.sem_inc(dve_turn, 1)
                    step(nc.vector.match_replace(taken[:], top8[:], mk[:], TAKEN))
                    nc.vector.tensor_scalar(sel[:], taken[:], TAKEN, None, ALU.is_equal).then_inc(sel_ready, 1)
                    step(nc.vector.scalar_tensor_tensor(out=w[:], in0=taken[:], scalar=TAKEN, in1=sco[:],
                                                        op0=ALU.is_equal, op1=ALU.mult, accum_out=wsum[:, 0:1]))
                    dve.sem_inc(sco_used, 1)
                    step(nc.vector.tensor_scalar(wsum[:, 0:1], wsum[:, 0:1], 1e-20, None, ALU.add))
                    step(nc.vector.reciprocal(wsum[:, 1:2], wsum[:, 0:1]))
                    step(nc.vector.tensor_scalar(w[:], w[:], wsum[:, 1:2], ROUTE_SCALE, ALU.mult, ALU.mult))
                    if not isinstance(i, int) or i:
                        add_shared(i - 1)
                    dve.wait_ge(sig_ready, i + 1)
                    step(nc.vector.tensor_tensor(gs[:], GU[:, 0:I], sig[:], ALU.mult))
                    nc.vector.tensor_tensor(act_h[:], GU[:, I:2 * I], gs[:], ALU.mult).then_inc(act_ready, 1)
                    dve.wait_ge(pos_done, i + 1)
                    nc.vector.scalar_tensor_tensor(out=fits[:], in0=PS[:, 0:E], scalar=float(CAP), in1=sel[:],
                                                   op0=ALU.is_lt, op1=ALU.mult)
                    step(nc.vector.tensor_tensor(slot[:], slot0[:], PS[:, 0:E], ALU.subtract))
                    nc.vector.tensor_tensor(count[:], count[:], sel[:], ALU.add)
                    step(nc.vector.tensor_tensor(key[:], slot[:], fits[:], ALU.mult))
                    dve.sem_inc(dve_turn, 1)
                    step(nc.vector.max(key8[:], key[:]))
                    step(nc.vector.tensor_scalar(dest[:], key8[:], -1.0, KEY0, ALU.mult, ALU.add))
                    step(nc.vector.tensor_tensor(dest[:], dest[:], spare[:, p, :], ALU.min))
                    if scatters is not None:
                        dve.wait_ge(scattered[p], scatters)
                    nc.vector.tensor_copy(desti[p][:], dest[:])
                    nc.vector.tensor_copy(entry[p][:], tokid[:, bass.ds(i, 1)]).then_inc(entry_ready, 1)
                    dve.wait_ge(row_out, PRIME_DMA + i * 16)
                    nc.vector.tensor_tensor(rows[:, D:D + E], w[:], fits[:], ALU.mult).then_inc(w_ready, 1)
                    self.csteps = step.n

                for p in range(2):
                    tile(p, p, None)
                with dve.Fori(1, NT // 2) as i2:
                    for p in range(2):
                        tile(i2 * 2 + p, p, i2 * (16 * TOPK))
                add_shared(NT - 1)
        assert self.csteps == CSTEPS, self.csteps

    def experts(self, ctx):
        nc, io, ident, bank = self.nc, self.io, self.ident, self.bank

        def sb(name, shape, dt=F32):
            return ctx.enter_context(nc.sbuf_tensor(name, shape, dt))

        def sem(name):
            return ctx.enter_context(nc.semaphore("e_" + name))

        wgu = [sb(f"wgu{s}", [P, 2, KC, I]) for s in range(2)]
        wdn = [sb(f"wdn{s}", [IH, 2, D]) for s in range(2)]
        tab = sb("tab", [P, P], I32)
        tabf = sb("tabf", [P, P])
        slot_tok = sb("slot_tok", [P, NU], I32)
        slot_w = sb("slot_w", [P, NU])
        idx = [sb(f"idx{h}", [P, 1], I32) for h in range(2)]
        idy = [sb(f"idy{h}", [P, 1], I32) for h in range(2)]
        xg = [sb(f"xg{h}", [P, D + E]) for h in range(2)]
        wgu_part = [[sb(f"wgu_{n}{s}", [P, 2, KC, I], BF16) for n in ("hi", "lo")] for s in range(2)]
        wdn_part = [[sb(f"wdn_{n}{s}", [IH, 2, D], BF16) for n in ("hi", "lo")] for s in range(2)]
        xgT = [sb(f"xgT_{n}", [P, 2, KC, P], BF16) for n in ("hi", "lo")]
        sig = sb("sig_e", [P, 2, I])
        gs = sb("gs_e", [P, 2, I])
        ah = sb("ah", [P, 2, I])
        ahT = [sb(f"ahT_{n}", [IH, 2, 2, P], BF16) for n in ("hi", "lo")]
        y = [sb(f"y{h}", [P, D]) for h in range(2)]

        tab_ld, tab_f, tab_T, tab_ready = sem("tab_ld"), sem("tab_f"), sem("tab_T"), sem("tab_ready")
        w_ld = [sem("w_ld0"), sem("w_ld1")]
        idx_ready, gathered, idy_ready, added = (sem("idx_ready"), [sem("gathered0"), sem("gathered1")],
                                                 sem("idy_ready"), [sem("added0"), sem("added1")])
        x_hi, a_hi, act_turn = sem("x_hi"), sem("a_hi"), sem("act_turn")
        gu_hi, gu_split, dn_hi, dn_split = sem("gu_hi"), sem("gu_split"), sem("dn_hi"), sem("dn_split")
        xT_done, xT_ready, gu_done, sig_ready, gs_ready, ah_ready, ahT_done, ahT_ready, y_done, y_ready = (
            sem("xT_done"), sem("xT_ready"), sem("gu_done"), sem("sig_ready"), sem("gs_ready"), sem("ah_ready"),
            sem("ahT_done"), sem("ahT_ready"), sem("y_done"), sem("y_ready"))
        out_done, pool_turn, cleared, w_kept = sem("out_done"), sem("pool_turn"), sem("cleared"), sem("w_kept")
        XT, GU, HT, DN = bank[0:2], bank[2:4], bank[4:6], bank[6:8]

        def load(eng, e, s):
            for a, n in enumerate(("w_gate", "w_up")):
                eng.dma_start(wgu[s][:, a], io[n][e].rearrange("(p k) i -> p k i", k=KC)).then_inc(w_ld[s], 16)
            eng.dma_start(wdn[s][:], io["w_down"][e].rearrange("(p c) d -> p c d", c=2)).then_inc(w_ld[s], 16)

        with nc.Block() as block:
            @block.sync
            def _(sp):
                sp.dma_start(tab[:], self.table[0:SLOTS, :].rearrange("(c p) w -> c (p w)", p=P)).then_inc(tab_ld, 16)
                load(sp, 0, 0)
                load(sp, 1, 1)
                with sp.Fori(0, E // 2 - 1) as ee:
                    for s in range(2):
                        sp.wait_ge(gu_split, ee * 2 + s + 1)
                        sp.wait_ge(dn_split, ee * 2 + s + 1)
                        for a, n in enumerate(("w_gate", "w_up")):
                            sp.dma_start(wgu[s][:, a], io[n][bass.ds(ee * 2 + 2 + s, 1)].rearrange(
                                "e (p k) i -> p (e k) i", k=KC)).then_inc(w_ld[s], 16)
                        sp.dma_start(wdn[s][:], io["w_down"][bass.ds(ee * 2 + 2 + s, 1)].rearrange(
                            "e (p c) d -> p (e c) d", c=2)).then_inc(w_ld[s], 16)
                for h in range(2):
                    sp.wait_ge(added[h], PRIME_DMA + 16 * E)
                sp.dma_start(self.out, self.acc_rows[0:N, :]).then_inc(out_done, 16)
                sp.wait_ge(out_done, 16)

            @block.gpsimd
            def _(pool):
                pool.wait_ge(tab_ready, 1)

                def gather(u, h):
                    nc.gpsimd.tensor_copy(idx[h][:], slot_tok[:, bass.ds(u, 1)]).then_inc(idx_ready, 1)
                    pool.wait_ge(idx_ready, u + 1)
                    pool.sem_inc(pool_turn, 1)
                    nc.gpsimd.indirect_dma_start(xg[h][:], None, self.hs_rows,
                                                 bass.IndirectOffsetOnAxis(idx[h][:].bitcast(U32), 0)
                                                 ).then_inc(gathered[h], 16)

                def add_rows(u, e, h):
                    pool.wait_ge(added[h], PRIME_DMA + e * 16)
                    nc.gpsimd.tensor_copy(idy[h][:], slot_tok[:, bass.ds(u, 1)]).then_inc(idy_ready, 1)
                    pool.wait_ge(idy_ready, u + 1)
                    pool.wait_ge(y_ready, u + 1)
                    if h == 0:
                        pool.wait_ge(added[1], PRIME_DMA + e * 16)
                    pool.sem_inc(pool_turn, 1)
                    nc.gpsimd.indirect_dma_start(self.acc_rows, bass.IndirectOffsetOnAxis(idy[h][:].bitcast(U32), 0),
                                                 y[h][:], None, compute_op=ALU.add).then_inc(added[h], 16)

                for h in range(2):
                    nc.gpsimd.memset(y[h][:], 0.0).then_inc(cleared, 1)
                    pool.wait_ge(cleared, h + 1)
                    nc.gpsimd.dma_start(self.acc_rows[N + h * P:N + (h + 1) * P, :], y[h][:]).then_inc(added[h], 16)
                    gather(h, h)
                for h in range(2):
                    pool.wait_ge(w_kept, h + 1)
                    pool.wait_ge(xT_done, h + 1)
                    gather(2 + h, h)
                with pool.Fori(0, E - 2) as e:
                    for h in range(2):
                        pool.wait_ge(w_kept, e * 2 + 2 + h + 1)
                        pool.wait_ge(xT_done, e * 2 + 2 + h + 1)
                        gather(e * 2 + 4 + h, h)
                    for h in range(2):
                        add_rows(e * 2 + h, e, h)
                for e in (E - 2, E - 1):
                    for h in range(2):
                        add_rows(e * 2 + h, e, h)

            @block.tensor
            def _(pe):
                pe.wait_ge(tab_f, 1)
                nc.tensor.transpose(bank[0][:, 0:P], tabf[:], ident[:]).then_inc(tab_T, 1)
                pe.wait_ge(tab_ready, 1)

                def turn_x(e, h):
                    pe.wait_ge(gathered[h], e * 16 + 16)
                    for k in range(KC):
                        last = nc.tensor.transpose(XT[h][:, k * P:(k + 1) * P], xg[h][:, k:D:KC], ident[:])
                    last.then_inc(xT_done, 1)

                PARTS = ((0, 0), (0, 1), (1, 0))

                def expert(e, s, last_one):
                    def turn_inner(h):
                        pe.wait_ge(ah_ready, e * 2 + h + 1)
                        for c in range(2):
                            last = nc.tensor.transpose(HT[h][0:IH, c * P:(c + 1) * P], ah[:, h, c::2], ident[:])
                        last.then_inc(ahT_done, 1)

                    pe.wait_ge(gu_split, e + 1)
                    for h in range(2):
                        pe.wait_ge(xT_ready, e * 2 + h + 1)
                        for k in range(KC):
                            for a, b in PARTS:
                                last = nc.tensor.matmul(GU[h][:, 0:2 * I], xgT[a][:, h, k, :],
                                                        wgu_part[s][b][:, :, k, :],
                                                        start=(k == 0 and (a, b) == PARTS[0]),
                                                        stop=(k == KC - 1 and (a, b) == PARTS[-1]))
                        last.then_inc(gu_done, 1)

                    def down(h, c):
                        if c == 0:
                            pe.wait_ge(ahT_ready, e * 2 + h + 1)
                        for a, b in PARTS:
                            last = nc.tensor.matmul(DN[h][:], ahT[a][:, h, c, :], wdn_part[s][b][:, c, :],
                                                    start=(c == 0 and (a, b) == PARTS[0]),
                                                    stop=(c == 1 and (a, b) == PARTS[-1]))
                        if c == 1:
                            last.then_inc(y_done, 1)

                    turn_inner(0)
                    if not last_one:
                        turn_x(e + 1, 0)
                    pe.wait_ge(dn_split, e + 1)
                    down(0, 0)
                    turn_inner(1)
                    if not last_one:
                        turn_x(e + 1, 1)
                    down(0, 1)
                    down(1, 0)
                    down(1, 1)

                for h in range(2):
                    turn_x(0, h)
                with pe.Fori(0, E // 2 - 1) as ee:
                    for s in range(2):
                        expert(ee * 2 + s, s, False)
                expert(E - 2, 0, False)
                expert(E - 1, 1, True)

            @block.scalar
            def _(act):
                def split_gu(s, ld):
                    act.wait_ge(w_ld[s], ld)
                    nc.scalar.copy(wgu_part[s][0][:], wgu[s][:]).then_inc(gu_hi, 1)

                def split_dn(s):
                    nc.scalar.copy(wdn_part[s][0][:], wdn[s][:]).then_inc(dn_hi, 1)

                def keep_x(e, h):
                    act.wait_ge(xT_done, e * 2 + h + 1)
                    nc.scalar.copy(xgT[0][:, h, :, :], XT[h][:].rearrange("p (k q) -> p k q", k=KC)).then_inc(x_hi, 1)

                def keep_weight(e, h):
                    act.wait_ge(gathered[h], e * 16 + 16)
                    nc.scalar.copy(slot_w[:, bass.ds(e * 2 + h, 1)], xg[h][:, bass.ds(e + D, 1)]).then_inc(w_kept, 1)

                def expert(e, s, ld, more):
                    def keep_inner(h):
                        act.wait_ge(ahT_done, e * 2 + h + 1)
                        nc.scalar.copy(ahT[0][:, h, :, :], HT[h][0:IH, 0:2 * P].rearrange("p (c q) -> p c q", c=2)
                                       ).then_inc(a_hi, 1)

                    def gate(h):
                        act.wait_ge(gu_done, e * 2 + h + 1)
                        nc.scalar.activation(sig[:, h, :], GU[h][:, 0:I], ACT.Sigmoid).then_inc(sig_ready, 1)

                    def weigh(h):
                        act.wait_ge(w_kept, e * 2 + h + 1)
                        act.wait_ge(added[h], PRIME_DMA + e * 16)
                        act.wait_ge(y_done, e * 2 + h + 1)
                        act.sem_inc(act_turn, 1)
                        nc.scalar.activation(y[h][:], DN[h][:], ACT.Copy, scale=slot_w[:, bass.ds(e * 2 + h, 1)]
                                             ).then_inc(y_ready, 1)

                    if more:
                        split_dn(1 - s)
                    gate(0)
                    keep_inner(0)
                    gate(1)
                    if more:
                        keep_x(e + 1, 0)
                        keep_weight(e + 1, 0)
                    keep_inner(1)
                    if more > 1:
                        split_gu(s, ld)
                    if more:
                        keep_weight(e + 1, 1)
                    weigh(0)
                    if more:
                        keep_x(e + 1, 1)
                    weigh(1)

                split_gu(0, 48)
                split_dn(0)
                split_gu(1, 48)
                for h in range(2):
                    keep_x(0, h)
                    keep_weight(0, h)
                with act.Fori(0, E // 2 - 1) as ee:
                    for s in range(2):
                        expert(ee * 2 + s, s, ee * 48 + 96, 2)
                expert(E - 2, 0, 0, 1)
                expert(E - 1, 1, 0, 0)

            @block.vector
            def _(dve):
                dve.wait_ge(tab_ld, 16)
                nc.vector.tensor_copy(tabf[:], tab[:]).then_inc(tab_f, 1)
                dve.wait_ge(tab_T, 1)
                nc.vector.tensor_copy(slot_tok[:], bank[0][:, 0:P]).then_inc(tab_ready, 1)

                def split_gu(e, s):
                    dve.wait_ge(gu_hi, e + 1)
                    nc.vector.tensor_tensor(wgu_part[s][1][:], wgu[s][:], wgu_part[s][0][:], ALU.subtract
                                            ).then_inc(gu_split, 1)

                def split_dn(e, s):
                    dve.wait_ge(dn_hi, e + 1)
                    nc.vector.tensor_tensor(wdn_part[s][1][:], wdn[s][:], wdn_part[s][0][:], ALU.subtract
                                            ).then_inc(dn_split, 1)

                def rest_x(e, h):
                    dve.wait_ge(x_hi, e * 2 + h + 1)
                    nc.vector.tensor_tensor(xgT[1][:, h, :, :], XT[h][:].rearrange("p (k q) -> p k q", k=KC),
                                            xgT[0][:, h, :, :], ALU.subtract).then_inc(xT_ready, 1)

                def expert(e, s, more):
                    def silu_up(h):
                        u = e * 2 + h
                        dve.wait_ge(sig_ready, u + 1)
                        nc.vector.tensor_tensor(gs[:, h, :], GU[h][:, 0:I], sig[:, h, :], ALU.mult).then_inc(gs_ready, 1)
                        dve.wait_ge(gs_ready, u + 1)
                        nc.vector.tensor_tensor(ah[:, h, :], GU[h][:, I:2 * I], gs[:, h, :], ALU.mult
                                                ).then_inc(ah_ready, 1)

                    def rest_inner(h):
                        dve.wait_ge(a_hi, e * 2 + h + 1)
                        nc.vector.tensor_tensor(ahT[1][:, h, :, :], HT[h][0:IH, 0:2 * P].rearrange("p (c q) -> p c q", c=2),
                                                ahT[0][:, h, :, :], ALU.subtract).then_inc(ahT_ready, 1)

                    if more:
                        split_gu(e + 1, 1 - s)
                    silu_up(0)
                    rest_inner(0)
                    silu_up(1)
                    if more:
                        rest_x(e + 1, 0)
                    rest_inner(1)
                    if more:
                        split_dn(e + 1, 1 - s)
                        rest_x(e + 1, 1)

                split_gu(0, 0)
                split_dn(0, 0)
                for h in range(2):
                    rest_x(0, h)
                with dve.Fori(0, E // 2 - 1) as ee:
                    for s in range(2):
                        expert(ee * 2 + s, s, True)
                expert(E - 2, 0, True)
                expert(E - 1, 1, False)


_DIRECT = {"W_emb": "L0_cond_W_emb", "W_qkv": "L0_cond_W_qkv", "W_out": "L0_cond_W_out", "kernel": "L0_ffn_kernel",
           "ffn_bias": "L0_ffn_bias", "W_ih": "L1_cond_W_ih", "W_hh": "L1_cond_W_hh", "e_bias": "L1_ffn_e_bias",
           "w_gate": "L1_ffn_w_gate", "w_up": "L1_ffn_w_up", "w_down": "L1_ffn_w_down",
           "sh_gate": "L1_ffn_sh_gate", "sh_up": "L1_ffn_sh_up", "sh_down": "L1_ffn_sh_down"}


def lay_out(inputs):
    import numpy as np

    def chunks(v):
        return np.ascontiguousarray(np.asarray(v).reshape(-1, P).T)

    a = {k: np.ascontiguousarray(inputs[n]) for k, n in _DIRECT.items()}
    a["x"] = np.ascontiguousarray(inputs["x"]).reshape(N, D)
    a["condT"] = np.ascontiguousarray(np.asarray(inputs["cond_2048"]).T)
    a["b_emb"] = chunks(inputs["L0_cond_b_emb"])
    a["g_norm"] = chunks(inputs["L0_cond_g_norm"])
    a["g_q"] = np.ascontiguousarray(inputs["L0_cond_g_q"]).reshape(DH, 1)
    a["g_k"] = np.ascontiguousarray(inputs["L0_cond_g_k"]).reshape(DH, 1)
    a["kernelT"] = np.ascontiguousarray(np.asarray(inputs["L0_ffn_kernel"]).T)
    a["b_ih"] = chunks(inputs["L1_cond_b_ih"])
    a["b_hh"] = chunks(inputs["L1_cond_b_hh"])
    a["routerT"] = np.ascontiguousarray(np.asarray(inputs["L1_ffn_router_weight"]).T)
    return a


def program(nc, shapes):
    io = {n: nc.dram_tensor("in_" + n, s, dt, kind="ExternalInput").ap() for n, (s, dt) in shapes.items()}
    out = nc.dram_tensor("out_rows", [N, D], F32, kind="ExternalOutput").ap()
    Kernel(nc, io, out).build()


def kernel(**inputs):
    import numpy as np
    import concourse.bacc as bacc
    from concourse.bass_utils import run_bass_kernel_spmd

    arrays = lay_out(inputs)
    nc = bacc.Bacc("TRN2", target_bir_lowering=False, num_devices=1)
    program(nc, {n: (a.shape, mybir.dt.from_np(a.dtype)) for n, a in arrays.items()})
    r = run_bass_kernel_spmd(nc, [{"in_" + n: a for n, a in arrays.items()}], core_ids=[0])
    return np.asarray(r.results[0]["out_rows"]).reshape(B, T, D)
```
